# Optimizing a Trainium2 kernel written in Bass

```python
import numpy as np
import jax
import jax.numpy as jnp

def _softmax(x, axis=-1):
    return jax.nn.softmax(x, axis=axis)

def _gelu(x):
    return jax.nn.gelu(x, approximate=True)

def _silu(x):
    return jax.nn.silu(x)

def _sigmoid(x):
    return jax.nn.sigmoid(x)

def _layernorm(x, axis=-1, eps=1e-05):
    m = jnp.mean(x, axis=axis, keepdims=True)
    v = jnp.var(x, axis=axis, keepdims=True)
    return (x - m) / jnp.sqrt(v + eps)

def _scatter_add(tgt, idx, src, axis=0):
    return tgt.at[idx].add(src)

def _segment_sum(src, seg, n):
    return jax.ops.segment_sum(src, seg, n)
kernel_name = 'mk_xattn_seq_d2_seqx_r8_ae09c7'

def setup_inputs(seed: int=0):
    np.random.seed(seed)
    _w = jnp.asarray

    def _rec_inputs():
        import jax
        import jax.numpy as jnp
        _rk = jax.random.key(seed)
        x = -0.0001951 + 1 * jax.random.normal(jax.random.fold_in(_rk, 1), (32, 56, 128), jnp.float32)
        _lenS = 56 - jax.random.randint(jax.random.fold_in(_rk, 7), (32,), 0, max(1, 56 // 4) + 1, jnp.int32)
        _lenS2 = 1500 - jax.random.randint(jax.random.fold_in(_rk, 8), (32,), 0, max(1, 1500 // 4) + 1, jnp.int32)
        _ctx_1024P = jax.random.normal(jax.random.fold_in(_rk, 11), (32, 16, 128), jnp.float32)
        _ctx_1024c = jax.random.dirichlet(jax.random.fold_in(_rk, 511), 0.3 * jnp.ones((16,), jnp.float32), (32, 1500))
        _ctx_1024t = jnp.einsum('bsk,bkd->bsd', _ctx_1024c, _ctx_1024P)
        _ctx_1024t = _ctx_1024t * jax.lax.rsqrt(jnp.mean(jnp.square(_ctx_1024t)) + 1e-12) * 0.953939
        ctx_1024 = -4.82715e-05 + 0.999928 * (_ctx_1024t + 0.3 * jax.random.normal(jax.random.fold_in(_rk, 611), (32, 1500, 128), jnp.float32))
        _validS = jnp.arange(56)[None, :] < _lenS[:, None]
        _validS2 = jnp.arange(1500)[None, :] < _lenS2[:, None]
        _causal = jnp.tril(jnp.ones((56, 56), dtype=bool))
        mask_BxS_bf0 = jnp.logical_not(jnp.ones((32, 56), dtype=bool))
        return (x, ctx_1024, mask_BxS_bf0)
    x, ctx_1024, mask_BxS_bf0 = _rec_inputs()

    def _L0_xattn_setup():
        import jax, jax.numpy as jnp
        import numpy as np
        B, T, J, C, H = (16, 56, 56, 128, 16)
        HD = C // H
        NEG_INF = float('-inf')

        def _layernorm(x, g, b, eps=1e-05):
            mu = jnp.mean(x, axis=-1, keepdims=True)
            var = jnp.var(x, axis=-1, keepdims=True)
            return (x - mu) * jax.lax.rsqrt(var + eps) * g + b

        def _heads(x):
            Bv, S, _ = x.shape
            return x.reshape(Bv, S, H, HD).transpose(0, 2, 1, 3)

        def _merge(x):
            Bv, _, S, _ = x.shape
            return x.transpose(0, 2, 1, 3).reshape(Bv, S, C)

        def _forward(tgt, src, sa_wqkv, sa_wproj, sa_bproj, ed_wkv, ed_wq, ed_wproj, ed_bproj, ff_w1, ff_b1, ff_w2, ff_b2, ln1_g, ln1_b, ln2_g, ln2_b, ln3_g, ln3_b, tgt_padding_mask):
            scale = C ** (-0.5)
            x = _layernorm(tgt, ln1_g, ln1_b)
            qkv = x @ sa_wqkv
            q, k, v = (_heads(t) for t in jnp.split(qkv, 3, axis=-1))
            wei = jnp.einsum('bhtd,bhsd->bhts', q, k) * scale
            causal = jnp.tril(jnp.ones((T, T), bool))
            wei = jnp.where(causal[None, None], wei, NEG_INF)
            wei = jnp.where(tgt_padding_mask[:, None, None, :], NEG_INF, wei)
            wei = jax.nn.softmax(wei, axis=-1)
            sa_out = _merge(jnp.einsum('bhts,bhsd->bhtd', wei, v)) @ sa_wproj + sa_bproj
            result = tgt + sa_out
            xq = _layernorm(result, ln2_g, ln2_b)
            xs = _layernorm(src, ln2_g, ln2_b)
            kv = xs @ ed_wkv
            k2, v2 = (_heads(t) for t in jnp.split(kv, 2, axis=-1))
            q2 = _heads(xq @ ed_wq)
            wei2 = jnp.einsum('bhtd,bhjd->bhtj', q2, k2) * scale
            wei2 = jax.nn.softmax(wei2, axis=-1)
            ed_out = _merge(jnp.einsum('bhtj,bhjd->bhtd', wei2, v2)) @ ed_wproj + ed_bproj
            result = result + ed_out
            h = jax.nn.relu(_layernorm(tgt, ln3_g, ln3_b) @ ff_w1 + ff_b1)
            result = result + (h @ ff_w2 + ff_b2)
            return result
        key = jax.random.key(seed)
        ks = jax.random.split(key, 16)
        s = 0.02
        return {'tgt': jax.random.normal(ks[0], (B, T, C), jnp.float32), 'src': jax.random.normal(ks[1], (B, J, C), jnp.float32), 'sa_wqkv': jax.random.normal(ks[2], (C, 3 * C), jnp.float32) * s, 'sa_wproj': jax.random.normal(ks[3], (C, C), jnp.float32) * s, 'sa_bproj': jnp.zeros((C,), jnp.float32), 'ed_wkv': jax.random.normal(ks[4], (C, 2 * C), jnp.float32) * s, 'ed_wq': jax.random.normal(ks[5], (C, C), jnp.float32) * s, 'ed_wproj': jax.random.normal(ks[6], (C, C), jnp.float32) * s, 'ed_bproj': jnp.zeros((C,), jnp.float32), 'ff_w1': jax.random.normal(ks[7], (C, 4 * C), jnp.float32) * s, 'ff_b1': jnp.zeros((4 * C,), jnp.float32), 'ff_w2': jax.random.normal(ks[8], (4 * C, C), jnp.float32) * s, 'ff_b2': jnp.zeros((C,), jnp.float32), 'ln1_g': jnp.ones((C,), jnp.float32), 'ln1_b': jnp.zeros((C,), jnp.float32), 'ln2_g': jnp.ones((C,), jnp.float32), 'ln2_b': jnp.zeros((C,), jnp.float32), 'ln3_g': jnp.ones((C,), jnp.float32), 'ln3_b': jnp.zeros((C,), jnp.float32), 'tgt_padding_mask': jnp.zeros((B, T), bool)}
    _L0_xattn_all = _L0_xattn_setup()
    _L0_xattn_in = {k: v for k, v in _L0_xattn_all.items() if k in ('sa_wqkv', 'sa_wproj', 'sa_bproj', 'ed_wkv', 'ed_wq', 'ed_wproj', 'ed_bproj', 'ff_w1', 'ff_b1', 'ff_w2', 'ff_b2', 'ln1_g', 'ln1_b', 'ln2_g', 'ln2_b', 'ln3_g', 'ln3_b')}
    del _L0_xattn_all

    def _L1_xattn_setup():
        import jax, jax.numpy as jnp
        import numpy as np
        N_HEAD = 16
        Q_DIM = 128
        V_DIM = 128
        LN_EPS = 1e-05
        key = jax.random.key(seed)
        ks = jax.random.split(key, 13)
        b, lq, lv = (4, 128, 256)
        s_q = 1.0 / np.sqrt(Q_DIM)
        s_v = 1.0 / np.sqrt(V_DIM)
        return {'q': jax.random.normal(ks[0], (b, lq, Q_DIM), jnp.float32), 'k': jax.random.normal(ks[1], (b, lv, Q_DIM), jnp.float32), 'v': jax.random.normal(ks[2], (b, lv, V_DIM), jnp.float32), 'Wq': jax.random.normal(ks[3], (Q_DIM, Q_DIM), jnp.float32) * s_q, 'bq': jnp.zeros((Q_DIM,), jnp.float32), 'Wk': jax.random.normal(ks[4], (Q_DIM, Q_DIM), jnp.float32) * s_q, 'bk': jnp.zeros((Q_DIM,), jnp.float32), 'Wv': jax.random.normal(ks[5], (V_DIM, V_DIM), jnp.float32) * s_v, 'bv': jnp.zeros((V_DIM,), jnp.float32), 'Wo': jax.random.normal(ks[6], (V_DIM, V_DIM), jnp.float32) * s_v, 'bo': jnp.zeros((V_DIM,), jnp.float32), 'ln_g': jnp.ones((V_DIM,), jnp.float32), 'ln_b': jnp.zeros((V_DIM,), jnp.float32)}
    _L1_xattn_all = _L1_xattn_setup()
    _L1_xattn_in = {k: v for k, v in _L1_xattn_all.items() if k in ('Wq', 'bq', 'Wk', 'bk', 'Wv', 'bv', 'Wo', 'bo', 'ln_g', 'ln_b')}
    del _L1_xattn_all
    return {'x': x, 'ctx_1024': ctx_1024, 'mask_BxS_bf0': mask_BxS_bf0, 'L0_xattn_sa_wqkv': _L0_xattn_in['sa_wqkv'], 'L0_xattn_sa_wproj': _L0_xattn_in['sa_wproj'], 'L0_xattn_sa_bproj': _L0_xattn_in['sa_bproj'], 'L0_xattn_ed_wkv': _L0_xattn_in['ed_wkv'], 'L0_xattn_ed_wq': _L0_xattn_in['ed_wq'], 'L0_xattn_ed_wproj': _L0_xattn_in['ed_wproj'], 'L0_xattn_ed_bproj': _L0_xattn_in['ed_bproj'], 'L0_xattn_ff_w1': _L0_xattn_in['ff_w1'], 'L0_xattn_ff_b1': _L0_xattn_in['ff_b1'], 'L0_xattn_ff_w2': _L0_xattn_in['ff_w2'], 'L0_xattn_ff_b2': _L0_xattn_in['ff_b2'], 'L0_xattn_ln1_g': _L0_xattn_in['ln1_g'], 'L0_xattn_ln1_b': _L0_xattn_in['ln1_b'], 'L0_xattn_ln2_g': _L0_xattn_in['ln2_g'], 'L0_xattn_ln2_b': _L0_xattn_in['ln2_b'], 'L0_xattn_ln3_g': _L0_xattn_in['ln3_g'], 'L0_xattn_ln3_b': _L0_xattn_in['ln3_b'], 'L1_xattn_Wq': _L1_xattn_in['Wq'], 'L1_xattn_bq': _L1_xattn_in['bq'], 'L1_xattn_Wk': _L1_xattn_in['Wk'], 'L1_xattn_bk': _L1_xattn_in['bk'], 'L1_xattn_Wv': _L1_xattn_in['Wv'], 'L1_xattn_bv': _L1_xattn_in['bv'], 'L1_xattn_Wo': _L1_xattn_in['Wo'], 'L1_xattn_bo': _L1_xattn_in['bo'], 'L1_xattn_ln_g': _L1_xattn_in['ln_g'], 'L1_xattn_ln_b': _L1_xattn_in['ln_b']}

def reference(x, ctx_1024, mask_BxS_bf0, L0_xattn_sa_wqkv, L0_xattn_sa_wproj, L0_xattn_sa_bproj, L0_xattn_ed_wkv, L0_xattn_ed_wq, L0_xattn_ed_wproj, L0_xattn_ed_bproj, L0_xattn_ff_w1, L0_xattn_ff_b1, L0_xattn_ff_w2, L0_xattn_ff_b2, L0_xattn_ln1_g, L0_xattn_ln1_b, L0_xattn_ln2_g, L0_xattn_ln2_b, L0_xattn_ln3_g, L0_xattn_ln3_b, L1_xattn_Wq, L1_xattn_bq, L1_xattn_Wk, L1_xattn_bk, L1_xattn_Wv, L1_xattn_bv, L1_xattn_Wo, L1_xattn_bo, L1_xattn_ln_g, L1_xattn_ln_b):
    import jax
    import jax.numpy as jnp

    def _L0_xattn_ref(tgt, src, sa_wqkv, sa_wproj, sa_bproj, ed_wkv, ed_wq, ed_wproj, ed_bproj, ff_w1, ff_b1, ff_w2, ff_b2, ln1_g, ln1_b, ln2_g, ln2_b, ln3_g, ln3_b, tgt_padding_mask):
        import jax, jax.numpy as jnp
        import numpy as np
        B, T, J, C, H = (16, 56, 56, 128, 16)
        HD = C // H
        NEG_INF = float('-inf')

        def _layernorm(x, g, b, eps=1e-05):
            mu = jnp.mean(x, axis=-1, keepdims=True)
            var = jnp.var(x, axis=-1, keepdims=True)
            return (x - mu) * jax.lax.rsqrt(var + eps) * g + b

        def _heads(x):
            Bv, S, _ = x.shape
            return x.reshape(Bv, S, H, HD).transpose(0, 2, 1, 3)

        def _merge(x):
            Bv, _, S, _ = x.shape
            return x.transpose(0, 2, 1, 3).reshape(Bv, S, C)

        def _forward(tgt, src, sa_wqkv, sa_wproj, sa_bproj, ed_wkv, ed_wq, ed_wproj, ed_bproj, ff_w1, ff_b1, ff_w2, ff_b2, ln1_g, ln1_b, ln2_g, ln2_b, ln3_g, ln3_b, tgt_padding_mask):
            scale = C ** (-0.5)
            x = _layernorm(tgt, ln1_g, ln1_b)
            qkv = x @ sa_wqkv
            q, k, v = (_heads(t) for t in jnp.split(qkv, 3, axis=-1))
            wei = jnp.einsum('bhtd,bhsd->bhts', q, k) * scale
            causal = jnp.tril(jnp.ones((T, T), bool))
            wei = jnp.where(causal[None, None], wei, NEG_INF)
            wei = jnp.where(tgt_padding_mask[:, None, None, :], NEG_INF, wei)
            wei = jax.nn.softmax(wei, axis=-1)
            sa_out = _merge(jnp.einsum('bhts,bhsd->bhtd', wei, v)) @ sa_wproj + sa_bproj
            result = tgt + sa_out
            xq = _layernorm(result, ln2_g, ln2_b)
            xs = _layernorm(src, ln2_g, ln2_b)
            kv = xs @ ed_wkv
            k2, v2 = (_heads(t) for t in jnp.split(kv, 2, axis=-1))
            q2 = _heads(xq @ ed_wq)
            wei2 = jnp.einsum('bhtd,bhjd->bhtj', q2, k2) * scale
            wei2 = jax.nn.softmax(wei2, axis=-1)
            ed_out = _merge(jnp.einsum('bhtj,bhjd->bhtd', wei2, v2)) @ ed_wproj + ed_bproj
            result = result + ed_out
            h = jax.nn.relu(_layernorm(tgt, ln3_g, ln3_b) @ ff_w1 + ff_b1)
            result = result + (h @ ff_w2 + ff_b2)
            return result
        return _forward(tgt, src, sa_wqkv, sa_wproj, sa_bproj, ed_wkv, ed_wq, ed_wproj, ed_bproj, ff_w1, ff_b1, ff_w2, ff_b2, ln1_g, ln1_b, ln2_g, ln2_b, ln3_g, ln3_b, tgt_padding_mask)

    def _L1_xattn_ref(q, k, v, Wq, bq, Wk, bk, Wv, bv, Wo, bo, ln_g, ln_b):
        import jax, jax.numpy as jnp
        import numpy as np
        N_HEAD = 16
        Q_DIM = 128
        V_DIM = 128
        LN_EPS = 1e-05
        b, lq, _ = q.shape
        lv = k.shape[1]
        qh = Q_DIM // N_HEAD
        vh = V_DIM // N_HEAD
        q_ = (q @ Wq + bq).reshape(b, lq, N_HEAD, qh)
        k_ = (k @ Wk + bk).reshape(b, lv, N_HEAD, qh)
        v_ = (v @ Wv + bv).reshape(b, lv, N_HEAD, vh)
        scores = jnp.einsum('bqhd,bkhd->bhqk', q_, k_) / np.sqrt(qh).astype(jnp.float32)
        attn = jax.nn.softmax(scores, axis=-1)
        out = jnp.einsum('bhqk,bkhd->bqhd', attn, v_).reshape(b, lq, V_DIM)
        out = out @ Wo + bo
        resid = q[..., :V_DIM] if V_DIM < Q_DIM else q
        x = resid + out
        mu = jnp.mean(x, axis=-1, keepdims=True)
        var = jnp.mean(jnp.square(x - mu), axis=-1, keepdims=True)
        return (x - mu) / jnp.sqrt(var + LN_EPS) * ln_g + ln_b
    x = _L0_xattn_ref(x, ctx_1024, L0_xattn_sa_wqkv, L0_xattn_sa_wproj, L0_xattn_sa_bproj, L0_xattn_ed_wkv, L0_xattn_ed_wq, L0_xattn_ed_wproj, L0_xattn_ed_bproj, L0_xattn_ff_w1, L0_xattn_ff_b1, L0_xattn_ff_w2, L0_xattn_ff_b2, L0_xattn_ln1_g, L0_xattn_ln1_b, L0_xattn_ln2_g, L0_xattn_ln2_b, L0_xattn_ln3_g, L0_xattn_ln3_b, mask_BxS_bf0)
    x = _L1_xattn_ref(x, ctx_1024, ctx_1024, L1_xattn_Wq, L1_xattn_bq, L1_xattn_Wk, L1_xattn_bk, L1_xattn_Wv, L1_xattn_bv, L1_xattn_Wo, L1_xattn_bo, L1_xattn_ln_g, L1_xattn_ln_b)
    return x

_drawn_inputs = setup_inputs


def setup_inputs(seed=0):
    import zlib

    import numpy as np

    out = dict(_drawn_inputs(seed))
    spreads = {'L0_xattn_sa_bproj': (0.0, 0.1),
     'L0_xattn_ed_bproj': (0.0, 0.1),
     'L0_xattn_ff_b1': (0.0, 0.287),
     'L0_xattn_ff_b2': (0.0, 0.1),
     'L0_xattn_ln1_g': (1.0, 0.6),
     'L0_xattn_ln1_b': (0.0, 0.8),
     'L0_xattn_ln2_g': (1.0, 0.6),
     'L0_xattn_ln2_b': (0.0, 0.8),
     'L0_xattn_ln3_g': (1.0, 0.6),
     'L0_xattn_ln3_b': (0.0, 0.8),
     'L1_xattn_bq': (0.0, 0.414),
     'L1_xattn_bk': (0.0, 2.0),
     'L1_xattn_bv': (0.0, 0.1),
     'L1_xattn_bo': (0.0, 0.1),
     'L1_xattn_ln_g': (1.0, 0.2),
     'L1_xattn_ln_b': (0.0, 0.1)}
    factors = {'L0_xattn_sa_wqkv': 3.939, 'L0_xattn_sa_wproj': 3.897, 'L0_xattn_ed_wq': 200.0}
    for name, (base, spread) in spreads.items():
        noise = np.random.default_rng([zlib.crc32(name.encode()), seed]).standard_normal(out[name].shape)
        drawn = base * np.exp(spread * noise) if base else spread * noise
        out[name] = jnp.asarray(drawn.astype(out[name].dtype))
    for name, factor in factors.items():
        out[name] = (out[name] * factor).astype(out[name].dtype)
    return out
```

```python
from contextlib import ExitStack, contextmanager

import concourse.bass as bass
from concourse import mybir
from concourse.alu_op_type import AluOpType as ALU

F32 = mybir.dt.float32
F32R = mybir.dt.float32r
U8 = mybir.dt.uint8
ACT = mybir.ActivationFunctionType
AX = mybir.AxisListType

B, T, J, C, H = 32, 56, 1500, 128, 16
D = C // H
FF = 4 * C
GH = 4
G = H // GH
HT = H * T
GT = GH * T
NT = 12
JP = J // NT
JB = J // 3
SM = HT // 128
KROWS = 96 + SM
VH = D + 1
VW = 168
TOK = B * T
NC = 4
CT = TOK // NC
CB = B // NC
PT = 2 * T
NP = CT // PT
EPS = 1e-5
MASKED = -1e30


def build(nc, x, ctx, mask, w, out):
    with ExitStack() as stack:
        def sb(name, shape, dt=F32):
            return stack.enter_context(nc.sbuf_tensor(name, shape, dt))

        s = {
            "ident": sb("ident", [128, 128]),
            "head_mask": sb("head_mask", [128, H]),
            "quad_mask": sb("quad_mask", [128, GH]),
            "minus_half": sb("minus_half", [128, NT]),
            "zero_cols": sb("zero_cols", [128, G]),
            "rows": sb("rows", [PT, 6, C]),
            "cols": sb("cols", [C, 9]),
            "bq_rep": sb("bq_rep", [96, G]),
            "bq_rep_scaled": sb("bq_rep_scaled", [96, G]),
            "bq_scaled": sb("bq_scaled", [C, 1]),
            "kv_bias": sb("kv_bias", [C, 2]),
            "resid": sb("resid", [PT, B // 2, C]),
            "qT_all": sb("qT_all", [C, TOK]),
            "q_parts": sb("q_parts", [96, G, TOK]),
            "oT_all": sb("oT_all", [128, GH, TOK]),
        }
        s["wq1"] = sb("wq1", [C, C])
        s["wq_rep1"] = sb("wq_rep1", [C, G, 3, 32])
        for layer in (0, 1):
            s[f"wk{layer}"] = sb(f"wk{layer}", [C, C])
            s[f"wv{layer}"] = sb(f"wv{layer}", [C, C])
            s[f"wo{layer}"] = sb(f"wo{layer}", [C, C])
        ps = stack.enter_context(nc.psum_tensor("ps", [128, 8, 512], F32))

        with ExitStack() as own:
            for name, shape in (("wqkv", [C, 3 * C]), ("wproj", [C, C]), ("w1", [C, FF]), ("w2", [C, 4, C]),
                                ("ed_wkv", [C, 2 * C]), ("b1_cols", [C, 4]), ("causal", [128, T]),
                                ("causal_low", [128, T]), ("wq0", [C, C]), ("wq_rep0", [C, G, 3, 32])):
                s[name] = own.enter_context(nc.sbuf_tensor(name, shape, F32))
            setup(nc, s, own, ps, w)
            self_attention_and_ff(nc, s, own, ps, x, mask)
        for layer in (0, 1):
            with ExitStack() as own:
                cross_attention(nc, s, own, ps, ctx, layer)
            with ExitStack() as own:
                after_cross(nc, s, own, ps, layer, out)


@contextmanager
def semaphores(nc, prefix, names):
    m = {n: nc.alloc_semaphore(prefix + n) for n in names}
    yield m
    nc.clear_and_free_semaphores(list(m.values()))
    nc.all_engine_barrier()


def wait_alone(eng, gates, sem, value):
    eng.wait_ge(sem, value)
    eng.sem_inc(gates, 1)


COLS = ["L0_xattn_ln1_g", "L0_xattn_ln1_b", "L0_xattn_ln2_g", "L0_xattn_ln2_b", "L0_xattn_ln3_g",
        "L0_xattn_ln3_b", "L1_xattn_bq", "L1_xattn_bk", "L1_xattn_bv"]
LN1_G, LN1_B, LN2_G, LN2_B, LN3_G, LN3_B, BQ, BK, BV = range(9)
ROWS = ["L0_xattn_sa_bproj", "L0_xattn_ed_bproj", "L0_xattn_ff_b2", "L1_xattn_bo", "L1_xattn_ln_g",
        "L1_xattn_ln_b"]
SA_B, ED_B, FF_B2, BO, LN_G, LN_B = range(6)
SCALE = [C ** -0.5, D ** -0.5]


def setup(nc, s, own, ps, w):
    m = own.enter_context(semaphores(nc, "su_", ["loaded", "consts", "consts_dve", "bias_ready", "folded"]))
    loaded, consts, consts_dve = m["loaded"], m["consts"], m["consts_dve"]
    bias_ready, folded = m["bias_ready"], m["folded"]
    loads = [
        (s["wqkv"][:, :], w["L0_xattn_sa_wqkv"]),
        (s["wproj"][:, :], w["L0_xattn_sa_wproj"]),
        (s["w1"][:, :], w["L0_xattn_ff_w1"]),
        (s["w2"][:, :, :], w["L0_xattn_ff_w2"].rearrange("(k p) n -> p k n", p=C)),
        (s["ed_wkv"][:, :], w["L0_xattn_ed_wkv"]),
        (s["wq0"][:, :], w["L0_xattn_ed_wq"]),
        (s["wo0"][:, :], w["L0_xattn_ed_wproj"]),
        (s["wq1"][:, :], w["L1_xattn_Wq"]),
        (s["wk1"][:, :], w["L1_xattn_Wk"]),
        (s["wv1"][:, :], w["L1_xattn_Wv"]),
        (s["wo1"][:, :], w["L1_xattn_Wo"]),
        (s["b1_cols"][:, :], w["L0_xattn_ff_b1"].rearrange("(k p) -> p k", p=C)),
    ]
    loads += [(s["cols"][:, i:i + 1], w[n].unsqueeze(1)) for i, n in enumerate(COLS)]
    loads += [(s["rows"][:, i, :], w[n].unsqueeze(0).to_broadcast([PT, C])) for i, n in enumerate(ROWS)]
    loads += [(s["bq_rep"][32 * i:32 * i + 32, :], w["L1_xattn_bq"].rearrange("(g r) -> r g", r=32))
              for i in range(3)]

    with nc.Block() as block:
        @block.sync
        def _(sp):
            with nc.allow_non_contiguous_dma("parameters as columns, once"):
                for dst, src in loads[::2]:
                    sp.dma_start(dst, src).then_inc(loaded, 16)

        @block.scalar
        def _(act):
            with nc.allow_non_contiguous_dma("parameters as columns, once"):
                for dst, src in loads[1::2]:
                    act.dma_start(dst, src).then_inc(loaded, 16)

        @block.gpsimd
        def _(pool):
            nc.gpsimd.memset(s["ident"][:, :], 1.0).then_inc(consts, 1)
            nc.gpsimd.memset(s["head_mask"][:, :], 1.0).then_inc(consts, 1)
            nc.gpsimd.memset(s["causal"][:, :], 0.0).then_inc(consts, 1)
            nc.gpsimd.memset(s["causal_low"][:, :], 0.0).then_inc(consts, 1)
            nc.gpsimd.memset(s["minus_half"][:, :], -0.5).then_inc(consts, 1)
            nc.gpsimd.memset(s["zero_cols"][:, :], 0.0).then_inc(consts, 1)
            pool.wait_ge(consts, 6)
            nc.gpsimd.affine_select(out=s["ident"][:, :], in_=s["ident"][:, :], compare_op=ALU.is_equal,
                                    fill=0.0, base=0, pattern=[[-1, 128]], channel_multiplier=1
                                    ).then_inc(consts, 1)
            nc.gpsimd.affine_select(out=s["head_mask"][:, :], in_=s["head_mask"][:, :],
                                    compare_op=ALU.is_ge, fill=0.0, base=0, pattern=[[-D, H]],
                                    channel_multiplier=1).then_inc(consts, 1)
            pool.wait_ge(consts, 8)
            nc.gpsimd.affine_select(out=s["head_mask"][:, :], in_=s["head_mask"][:, :],
                                    compare_op=ALU.is_ge, fill=0.0, base=D - 1, pattern=[[D, H]],
                                    channel_multiplier=-1).then_inc(consts, 1)
            nc.gpsimd.affine_select(out=s["causal"][:, :], in_=s["causal"][:, :], compare_op=ALU.is_ge,
                                    fill=MASKED, base=0, pattern=[[-1, T]], channel_multiplier=1
                                    ).then_inc(consts, 1)
            nc.gpsimd.affine_select(out=s["causal_low"][:, :], in_=s["causal_low"][:, :],
                                    compare_op=ALU.is_ge, fill=MASKED, base=-64, pattern=[[-1, T]],
                                    channel_multiplier=1).then_inc(consts, 1)

        @block.tensor
        def _(pe):
            pe.wait_ge(loaded, 16 * len(loads))
            nc.tensor.matmul(ps[:, 0, 0:1], s["ed_wkv"][:, 0:C], s["cols"][:, LN2_B:LN2_B + 1],
                             start=True, stop=True)
            nc.tensor.matmul(ps[:, 0, 1:2], s["ed_wkv"][:, C:2 * C], s["cols"][:, LN2_B:LN2_B + 1],
                             start=True, stop=True).then_inc(bias_ready, 1)

        @block.vector
        def _(dve):
            dve.wait_ge(consts, 11)
            nc.vector.tensor_reduce(s["quad_mask"][:, :],
                                    s["head_mask"][:, :].rearrange("p (g a) -> p a g", a=GH),
                                    AX.X, ALU.add).then_inc(consts_dve, 1)
            nc.vector.tensor_copy(s["causal"][64:128, :], s["causal_low"][64:128, :]).then_inc(consts_dve, 1)
            dve.wait_ge(loaded, 16 * len(loads))
            g2 = s["cols"][:, LN2_G:LN2_G + 1]
            nc.vector.tensor_scalar(s["wk0"][:, :], s["ed_wkv"][:, 0:C], g2, None, ALU.mult).then_inc(folded, 1)
            nc.vector.tensor_scalar(s["wv0"][:, :], s["ed_wkv"][:, C:2 * C], g2, None, ALU.mult).then_inc(folded, 1)
            for layer in (0, 1):
                for part in range(3):
                    nc.vector.tensor_copy(s[f"wq_rep{layer}"][:, :, part, :],
                                          s[f"wq{layer}"][:, :].rearrange("p (g r) -> p g r", r=32)
                                          ).then_inc(folded, 1)
            nc.vector.tensor_scalar(s["bq_rep_scaled"][:, :], s["bq_rep"][:, :], SCALE[1], None,
                                    ALU.mult).then_inc(folded, 1)
            nc.vector.tensor_scalar(s["bq_scaled"][:, :], s["cols"][:, BQ:BQ + 1], SCALE[1], None,
                                    ALU.mult).then_inc(folded, 1)
            dve.wait_ge(bias_ready, 1)
            nc.vector.tensor_copy(s["kv_bias"][:, :], ps[:, 0, 0:2]).then_inc(folded, 1)


def queries(layer, s):
    if layer == 0:
        return s["wq0"], s["wq_rep0"], SCALE[0], s["zero_cols"][:, 0:1], s["zero_cols"][0:96, :]
    return s["wq1"], s["wq_rep1"], SCALE[1], s["bq_scaled"][:, :], s["bq_rep_scaled"][:, :]


def q_project_pe(nc, s, layer, ps, hT, bank_q, banks_g, done):
    wq, wq_rep, _, _, _ = queries(layer, s)
    nc.tensor.matmul(ps[:, bank_q, 0:CT], wq[:, :], hT[:, :], start=True, stop=True).then_inc(done, 1)
    for g in range(G):
        nc.tensor.matmul(ps[0:96, banks_g[g], 0:CT], wq_rep[:, g, :, :].rearrange("p a r -> p (a r)"),
                         hT[:, :], start=True, stop=True).then_inc(done, 1)


def self_attention_and_ff(nc, s, own, ps, x, mask):
    def sb(name, shape, dt=F32):
        return own.enter_context(nc.sbuf_tensor(name, shape, dt))

    xc = sb("a_x", [PT, NP, C])
    pad = sb("a_pad", [128, NP, T], U8)
    bias = sb("a_bias", [128, NP, T])
    stats = sb("a_stats", [PT, NP, 6])
    mv = sb("a_mv", [PT, NP, 2])
    ve = sb("a_ve", [PT, NP])
    rstd = sb("a_rstd", [PT, NP])
    xhat = sb("a_xhat", [PT, NP, C])
    x_b = sb("a_x_b", [PT, NP, C])
    h1T = sb("a_h1T", [C, CT])
    h3T = sb("a_h3T", [C, CT])
    qTp = sb("a_qTp", [C, CB, 64])
    kT = sb("a_kT", [C, CB, T])
    vS = sb("a_v", [T, CB, C])
    kblk = sb("a_kblk", [C, CB, H, T])
    scores = sb("a_scores", [128, NP, H, T])
    negmax = sb("a_negmax", [128, NP, H])
    probs = sb("a_probs", [128, NP, H, T])
    denom = sb("a_denom", [128, NP, H])
    rden = sb("a_rden", [128, NP, H])
    probsT = sb("a_probsT", [T, 2, H, 128])
    ao = sb("a_ao", [128, NP, H, D])
    aoT = sb("a_aoT", [C, NP, PT])
    r1 = sb("a_r1", [PT, NP, C])
    r1_b = sb("a_r1_b", [PT, NP, C])
    h2T = sb("a_h2T", [C, CT])
    hidT = sb("a_hidT", [C, 4, CT])
    ff = sb("a_ff", [PT, NP, C])
    q32 = sb("a_q32", [96, G, CT])

    names = ["x_loaded", "zeroed", "bias_done", "st1", "ag1", "ve1", "rs1", "xh1", "tr1", "h1", "h3",
             "qkv", "q_ev", "k_ev", "v_ev", "kblk_done", "ff1", "hid", "ff2", "ff_ev", "xb", "sc",
             "masked", "mx", "shifted", "exp", "den", "rden_done", "ptr", "pt_ev", "pv", "ao_done",
             "ao_tr", "aoT_ev", "proj", "r1_done", "r1b", "st2", "ag2", "ve2", "rs2", "xh2", "tr2", "h2",
             "qp", "q_store", "q32_done", "q_hi", "q_lo", "res_done", "gates", "pe_gates"]
    m = own.enter_context(semaphores(nc, "a_", names))
    x_pairs = x.rearrange("b t d -> (b t) d").rearrange("(n p) d -> p n d", p=PT)
    mask_pairs = mask.rearrange("(n u) s -> u n s", u=2)

    with nc.Block() as block:
        @block.vector
        def _(dve):
            nc.vector.memset(qTp[:, :, :], 0.0).then_inc(m["zeroed"], 1)
            nc.vector.memset(pad[:, :, :], 0).then_inc(m["zeroed"], 1)

    with nc.Fori(0, NC) as c:
        with nc.Block() as block:
            def step(name, per_chunk, k):
                return m[name], c * per_chunk + k

            @block.sync
            def _(sp):
                sp.dma_start(xc[:, :, :], x_pairs[:, bass.ds(c * NP, NP), :]).then_inc(m["x_loaded"], 16)
                for u in range(2):
                    sp.dma_start(pad[64 * u:64 * u + T, :, :],
                                 mask_pairs[u:u + 1, bass.ds(c * NP, NP), :].to_broadcast([T, NP, T])
                                 ).then_inc(m["x_loaded"], 16)

            @block.gpsimd
            def _(pool):
                pool.wait_ge(*step("x_loaded", 48, 48))
                nc.gpsimd.tensor_tensor(x_b[:, :, :], xc[:, :, :],
                                        s["rows"][:, SA_B, :].unsqueeze(1).to_broadcast([PT, NP, C]),
                                        ALU.add).then_inc(m["xb"], 1)
                pool.wait_ge(*step("ve1", 1, 1))
                nc.gpsimd.tensor_tensor(rstd[:, :], ve[:, :], s["minus_half"][0:PT, 0:NP], ALU.pow
                                        ).then_inc(m["rs1"], 1)
                for j in range(CB):
                    if j == 0:
                        pool.wait_ge(*step("k_ev", 1, 1))
                    nc.gpsimd.tensor_tensor(kblk[:, j, :, :],
                                            kT[:, j, :].unsqueeze(1).to_broadcast([C, H, T]),
                                            s["head_mask"][:, :].unsqueeze(2).to_broadcast([C, H, T]),
                                            ALU.mult).then_inc(m["kblk_done"], 1)
                pool.wait_ge(*step("r1_done", 1, 1))
                nc.gpsimd.tensor_tensor(r1_b[:, :, :], r1[:, :, :],
                                        s["rows"][:, ED_B, :].unsqueeze(1).to_broadcast([PT, NP, C]),
                                        ALU.add).then_inc(m["r1b"], 1)
                pool.wait_ge(*step("ve2", 1, 1))
                nc.gpsimd.tensor_tensor(rstd[:, :], ve[:, :], s["minus_half"][0:PT, 0:NP], ALU.pow
                                        ).then_inc(m["rs2"], 1)

            def layer_norm(dve, src, n, wait):
                dve.wait_ge(*wait)
                for p in range(NP):
                    nc.vector.bn_stats(stats[:, p, :], src[:, p, :]).then_inc(m[f"st{n}"], 1)
                wait_alone(dve, m["gates"], *step(f"st{n}", NP, NP))
                for p in range(NP):
                    nc.vector.bn_aggr(mv[:, p, :], stats[:, p, :]).then_inc(m[f"ag{n}"], 1)
                dve.wait_ge(*step(f"ag{n}", NP, NP))
                nc.vector.tensor_scalar(ve[:, :], mv[:, :, 1], EPS, None, ALU.add).then_inc(m[f"ve{n}"], 1)
                dve.wait_ge(*step(f"rs{n}", 1, 1))
                for p in range(NP):
                    nc.vector.tensor_scalar(xhat[:, p, :], src[:, p, :], mv[:, p, 0:1], rstd[:, p:p + 1],
                                            ALU.subtract, ALU.mult).then_inc(m[f"xh{n}"], 1)

            @block.vector
            def _(dve):
                layer_norm(dve, xc, 1, step("x_loaded", 48, 48))
                nc.vector.scalar_tensor_tensor(out=bias[:, :, :], in0=pad[:, :, :], scalar=MASKED,
                                               in1=s["causal"][:, :].unsqueeze(1).to_broadcast([128, NP, T]),
                                               op0=ALU.mult, op1=ALU.add).then_inc(m["bias_done"], 1)
                dve.wait_ge(*step("h1", 1, 1))
                nc.vector.tensor_scalar(h3T[:, :], ps[:, 0, 0:CT], s["cols"][:, LN3_G:LN3_G + 1],
                                        s["cols"][:, LN3_B:LN3_B + 1], ALU.mult, ALU.add
                                        ).then_inc(m["h3"], 1)
                dve.wait_ge(*step("qkv", 4, 1))
                nc.vector.tensor_copy(kT[:, :, :], ps[:, 1, 0:CT].rearrange("p (b t) -> p b t", t=T)
                                      ).then_inc(m["k_ev"], 1)
                dve.wait_ge(*step("qkv", 4, 4))
                nc.vector.tensor_copy(vS[:, :, :], ps[0:T, 2:4, :].rearrange("p a (b n) -> p (a b) n", n=C)
                                      ).then_inc(m["v_ev"], 1)
                dve.wait_ge(*step("ff2", 1, 1))
                nc.vector.tensor_tensor(ff[:, :, :], ps[0:PT, 5, :].rearrange("p (a n) -> p a n", n=C),
                                        s["rows"][:, FF_B2, :].unsqueeze(1).to_broadcast([PT, NP, C]),
                                        ALU.add).then_inc(m["ff_ev"], 1)

                def normalised(p):
                    dve.wait_ge(*step("pv", NP, p + 1))
                    dve.wait_ge(*step("rden_done", NP, p + 1))
                    nc.vector.tensor_tensor(ao[:, p, :, :],
                                            ps[:, 6 + p % 2, 0:C].rearrange("p (h d) -> p h d", d=D),
                                            rden[:, p, :].unsqueeze(2).to_broadcast([128, H, D]),
                                            ALU.mult).then_inc(m["ao_done"], 1)

                def denominators(p):
                    dve.wait_ge(*step("exp", NP, p + 1))
                    nc.vector.tensor_reduce(denom[:, p, :], probs[:, p, :, :], AX.X, ALU.add
                                            ).then_inc(m["den"], 1)
                    dve.wait_ge(*step("den", NP, p + 1))
                    nc.vector.reciprocal(rden[:, p, :], denom[:, p, :]).then_inc(m["rden_done"], 1)

                for p in range(NP):
                    dve.wait_ge(*step("sc", NP, p + 1))
                    if p == 0:
                        dve.wait_ge(*step("bias_done", 1, 1))
                    for half in range(2):
                        hs = slice(8 * half, 8 * half + 8)
                        nc.vector.tensor_tensor(scores[:, p, hs, :],
                                                ps[:, 4 + half, 0:CT].rearrange("p (h t) -> p h t", t=T),
                                                bias[:, p, :].unsqueeze(1).to_broadcast([128, 8, T]),
                                                ALU.add).then_inc(m["masked"], 1)
                    dve.wait_ge(*step("masked", 2 * NP, 2 * p + 2))
                    nc.vector.tensor_reduce(negmax[:, p, :], scores[:, p, :, :], AX.X, ALU.max,
                                            negate=True).then_inc(m["mx"], 1)
                    dve.wait_ge(*step("mx", NP, p + 1))
                    nc.vector.tensor_tensor(scores[:, p, :, :], scores[:, p, :, :],
                                            negmax[:, p, :].unsqueeze(2).to_broadcast([128, H, T]),
                                            ALU.add).then_inc(m["shifted"], 1)
                    if p >= 1:
                        denominators(p - 1)
                    if p >= 2:
                        normalised(p - 2)
                denominators(NP - 1)
                normalised(NP - 2)
                normalised(NP - 1)
                dve.wait_ge(*step("proj", 1, 1))
                dve.wait_ge(*step("xb", 1, 1))
                nc.vector.tensor_tensor(r1[:, :, :], ps[0:PT, 6, :].rearrange("p (a n) -> p a n", n=C),
                                        x_b[:, :, :], ALU.add).then_inc(m["r1_done"], 1)
                layer_norm(dve, r1, 2, step("r1_done", 1, 1))
                dve.wait_ge(*step("r1b", 1, 1))
                nc.vector.tensor_tensor(s["resid"][:, bass.ds(c * NP, NP), :], r1_b[:, :, :], ff[:, :, :],
                                        ALU.add).then_inc(m["res_done"], 1)
                q_low_dve(nc, dve, s, c, q32, m, step)

            @block.scalar
            def _(act):
                act.wait_ge(*step("tr1", 1, 1))
                nc.scalar.activation(h1T[:, :], ps[:, 0, 0:CT], ACT.Identity, bias=s["cols"][:, LN1_B:LN1_B + 1],
                                     scale=s["cols"][:, LN1_G:LN1_G + 1]).then_inc(m["h1"], 1)
                act.wait_ge(*step("qkv", 4, 2))
                nc.scalar.activation(qTp[:, :, 0:T], ps[:, 0, 0:CT].rearrange("p (b t) -> p b t", t=T),
                                     ACT.Copy, scale=SCALE[0]).then_inc(m["q_ev"], 1)
                for k in range(4):
                    act.wait_ge(*step("ff1", 4, k + 1))
                    nc.scalar.activation(hidT[:, k, :], ps[:, 6 + k % 2, 0:CT], ACT.Relu,
                                         bias=s["b1_cols"][:, k:k + 1]).then_inc(m["hid"], 1)

                def transposed(p):
                    act.wait_ge(*step("ptr", NP, p + 1))
                    nc.scalar.activation(probsT[:, p % 2, :, :].rearrange("p h n -> p (h n)"),
                                         ps[0:T, 0:4, :].rearrange("p a n -> p (a n)"), ACT.Copy
                                         ).then_inc(m["pt_ev"], 1)

                for p in range(NP):
                    act.wait_ge(*step("shifted", NP, p + 1))
                    nc.scalar.activation(probs[:, p, :, :], scores[:, p, :, :], ACT.Exp).then_inc(m["exp"], 1)
                    if p >= 1:
                        transposed(p - 1)
                transposed(NP - 1)
                act.wait_ge(*step("ao_tr", 1, 1))
                for p in range(NP):
                    nc.scalar.activation(aoT[:, p, :].rearrange("p (u t) -> p u t", t=T),
                                         ps[:, 7, 128 * p:128 * p + 128].rearrange("p (u t) -> p u t", t=64)[:, :, 0:T],
                                         ACT.Copy).then_inc(m["aoT_ev"], 1)
                act.wait_ge(*step("tr2", 1, 1))
                nc.scalar.activation(h2T[:, :], ps[:, 7, 0:CT], ACT.Identity, bias=s["cols"][:, LN2_B:LN2_B + 1],
                                     scale=s["cols"][:, LN2_G:LN2_G + 1]).then_inc(m["h2"], 1)
                q_store_act(nc, act, s, 0, c, ps, q32, 4, range(G), m, step)

            @block.tensor
            def _(pe):
                pe.wait_ge(*step("xh1", NP, NP))
                for p in range(NP):
                    mm = nc.tensor.transpose(ps[:, 0, PT * p:PT * p + PT], xhat[:, p, :], s["ident"][0:PT, 0:PT])
                mm.then_inc(m["tr1"], 1)
                pe.wait_ge(*step("h1", 1, 1))
                nc.tensor.matmul(ps[:, 1, 0:CT], s["wqkv"][:, C:2 * C], h1T[:, :], start=True, stop=True
                                 ).then_inc(m["qkv"], 1)
                pe.wait_ge(*step("h3", 1, 1))
                nc.tensor.matmul(ps[:, 0, 0:CT], s["wqkv"][:, 0:C], h1T[:, :], start=True, stop=True
                                 ).then_inc(m["qkv"], 1)
                for j in range(CB):
                    mm = nc.tensor.matmul(ps[0:T, 2 + j // 4, C * (j % 4):C * (j % 4) + C],
                                          h1T[:, T * j:T * j + T], s["wqkv"][:, 2 * C:3 * C],
                                          start=True, stop=True)
                    if j % 4 == 3:
                        mm.then_inc(m["qkv"], 1)
                for k in range(4):
                    if k >= 2:
                        pe.wait_ge(*step("hid", 4, k - 1))
                    nc.tensor.matmul(ps[:, 6 + k % 2, 0:CT], s["w1"][:, C * k:C * k + C], h3T[:, :],
                                     start=True, stop=True).then_inc(m["ff1"], 1)
                pe.wait_ge(*step("hid", 4, 4))
                for p in range(NP):
                    for k in range(4):
                        mm = nc.tensor.matmul(ps[0:PT, 5, C * p:C * p + C], hidT[:, k, PT * p:PT * p + PT],
                                              s["w2"][:, k, :], start=(k == 0), stop=(k == 3))
                mm.then_inc(m["ff2"], 1)
                pe.wait_ge(*step("ff_ev", 1, 1))
                pe.wait_ge(*step("q_ev", 1, 1))
                pe.wait_ge(m["zeroed"], 2)

                def score(p):
                    pe.wait_ge(*step("kblk_done", CB, 2 * p + 2))
                    if p >= 1:
                        pe.wait_ge(*step("masked", 2 * NP, 2 * p))
                    for half in range(2):
                        for u in range(2):
                            mm = nc.tensor.matmul(ps[64 * u:64 * u + 64, 4 + half, 0:CT], qTp[:, 2 * p + u, :],
                                                  kblk[:, 2 * p + u, 8 * half:8 * half + 8, :].rearrange(
                                                      "p h t -> p (h t)"), start=True, stop=True)
                    mm.then_inc(m["sc"], 1)

                def transpose_probs(p):
                    pe.wait_ge(*step("exp", NP, p + 1))
                    if p == 0:
                        wait_alone(pe, m["pe_gates"], *step("v_ev", 1, 1))
                    else:
                        wait_alone(pe, m["pe_gates"], *step("pt_ev", NP, p))
                    for h in range(H):
                        mm = nc.tensor.transpose(ps[0:T, h // 4, 128 * (h % 4):128 * (h % 4) + 128],
                                                 probs[:, p, h, :], s["ident"][:, :])
                    mm.then_inc(m["ptr"], 1)

                def values(p):
                    if p >= 2:
                        pe.wait_ge(*step("ao_done", NP, p - 1))
                    wait_alone(pe, m["pe_gates"], *step("pt_ev", NP, p + 1))
                    for u in range(2):
                        for h in range(H):
                            mm = nc.tensor.matmul(ps[64 * u:64 * u + 64, 6 + p % 2, D * h:D * h + D],
                                                  probsT[:, p % 2, h, 64 * u:64 * u + 64],
                                                  vS[:, 2 * p + u, D * h:D * h + D], start=True, stop=True)
                    mm.then_inc(m["pv"], 1)

                score(0)
                for p in range(NP):
                    if p + 1 < NP:
                        score(p + 1)
                    transpose_probs(p)
                    values(p)
                pe.wait_ge(*step("ao_done", NP, NP))
                for p in range(NP):
                    mm = nc.tensor.transpose(ps[:, 7, 128 * p:128 * p + 128],
                                             ao[:, p, :, :].rearrange("p h d -> p (h d)"), s["ident"][:, :])
                mm.then_inc(m["ao_tr"], 1)
                pe.wait_ge(*step("aoT_ev", NP, NP))
                for p in range(NP):
                    mm = nc.tensor.matmul(ps[0:PT, 6, C * p:C * p + C], aoT[:, p, :], s["wproj"][:, :],
                                          start=True, stop=True)
                mm.then_inc(m["proj"], 1)
                pe.wait_ge(*step("xh2", NP, NP))
                for p in range(NP):
                    mm = nc.tensor.transpose(ps[:, 7, PT * p:PT * p + PT], xhat[:, p, :], s["ident"][0:PT, 0:PT])
                mm.then_inc(m["tr2"], 1)
                pe.wait_ge(*step("h2", 1, 1))
                q_project_pe(nc, s, 0, ps, h2T, 4, range(G), m["qp"])


def q_store_act(nc, act, s, layer, c, ps, q32, bank_q, banks_g, m, step):
    _, _, scale, bias, bias_rep = queries(layer, s)
    tokens = bass.ds(c * CT, CT)
    act.wait_ge(*step("qp", 1 + G, 1))
    nc.scalar.activation(s["qT_all"][:, tokens], ps[:, bank_q, 0:CT], ACT.Identity, bias=bias,
                         scale=scale).then_inc(m["q_store"], 1)
    for g in range(G):
        act.wait_ge(*step("qp", 1 + G, 2 + g))
        nc.scalar.activation(q32[:, g, :], ps[0:96, banks_g[g], 0:CT], ACT.Identity,
                             bias=bias_rep[:, g:g + 1], scale=scale).then_inc(m["q32_done"], 1)
    act.wait_ge(*step("q32_done", G, G))
    nc.scalar.activation(s["q_parts"][:, :, tokens].bitcast(F32R), q32[:, :, :], ACT.Copy
                         ).then_inc(m["q_hi"], 1)


def q_low_dve(nc, dve, s, c, q32, m, step):
    low = s["q_parts"][64:96, :, bass.ds(c * CT, CT)]
    dve.wait_ge(*step("q_hi", 1, 1))
    nc.vector.tensor_tensor(low, q32[64:96, :, :], low, ALU.subtract).then_inc(m["q_lo"], 1)


def cross_attention(nc, s, own, ps, ctx, layer):
    def sb(name, shape, dt=F32):
        return own.enter_context(nc.sbuf_tensor(f"c{layer}_{name}", shape, dt))

    raw = [sb(f"raw{u}", [JP, NT, C]) for u in range(2)]
    xhat = [sb(f"xhat{u}", [JP, NT, C]) for u in range(2)] if layer == 0 else raw
    stats = sb("stats", [JP, NT, 6])
    mv = sb("mv", [JP, NT, 2])
    ve = sb("ve", [JP, NT])
    rstd = sb("rstd", [JP, NT])
    ctxT = sb("ctxT", [C, J])
    k_hi = sb("k_hi", [C, J], F32R)
    k_lo = sb("k_lo", [C, J], F32R)
    k_op = [sb(f"k_op{u}", [KROWS, G, J], F32R) for u in range(2)]
    v_op = [sb(f"v_op{u}", [JP, NT, VW]) for u in range(2)]
    q_blk = [sb(f"q_blk{u}", [C, H, T], F32R) for u in range(2)]
    q_op = [sb(f"q_op{u}", [KROWS, G, GH, T], F32R) for u in range(2)]
    negmax = [sb(f"negmax{u}", [128, SM]) for u in range(2)]
    probs = [sb(f"probs{u}", [JP, HT]) for u in range(2)]
    wk, wv = s[f"wk{layer}"], s[f"wv{layer}"]
    k_bias = s["kv_bias"][:, 0:1] if layer == 0 else s["cols"][:, BK:BK + 1]

    CREDIT = {"scored": 1, "exped": 2, "summed": 2, "sums_read": 1, "transposed": 2, "v_read": 1,
              "copied": 16, "max_scored": 1, "normed": 1, "stats_read": 0}
    names = ["loaded0", "loaded1", "stat", "aggr", "ve_done", "rstd_done", "centred", "normed", "transposed", "ctxT_done",
             "k_projected", "k_hi_done", "k_lo_done", "copied", "q_blk_done", "q_op_done", "max_scored",
             "max_done", "max_turned", "max_rows", "v_projected", "v_read", "scored", "exped", "summed",
             "sums_read", "ones_done", "gates"]
    m = own.enter_context(semaphores(nc, f"c{layer}_", names))
    CPY = 3 * G * 16

    def loaded(q, u):
        return m[f"loaded{u}"], 8 * (q - u) + 16

    source_ready = (lambda q, u: (m["normed"], q + 1 + CREDIT["normed"])) if layer == 0 else \
                   loaded
    ctx_rows = ctx.rearrange("b (p n) d -> p b (n d)", p=JP)
    AHEAD = 3 if layer == 0 else 2

    def load(sp, q, u):
        sp.dma_start(raw[u][:, :, :].rearrange("p n d -> p (n d)").unsqueeze(1),
                     ctx_rows[:, bass.ds(q, 1), :]).then_inc(m[f"loaded{u}"], 16)

    def load_ahead(sp, b, u):
        if layer == 0:
            sp.wait_ge(m["normed"], b + 2 + CREDIT["normed"])
        else:
            sp.wait_ge(m["transposed"], b + 1 + CREDIT["transposed"])
        load(sp, b + AHEAD, (u + AHEAD) % 2)

    def copy_keys(sp, q, u, first):
        sp.wait_ge(m["k_hi_done"], q + 1)
        sp.wait_ge(m["k_lo_done"], q + 1)
        if not first:
            sp.wait_ge(m["scored"], 12 * (q - 1) + CREDIT["scored"])
        for part, src in enumerate((k_hi, k_lo, k_hi)):
            for g in range(G):
                sp.dma_start(k_op[u][32 * part:32 * part + 32, g, :].bitcast(F32),
                             src[32 * g:32 * g + 32, :].bitcast(F32)).then_inc(m["copied"], 16)

    def build_queries(pool, q, u, first):
        if not first:
            pool.wait_ge(m["max_scored"], SM * (q - 1) + CREDIT["max_scored"])
        qT = s["qT_all"][:, bass.ds(q * T, T)]
        nc.gpsimd.tensor_tensor(q_blk[u][:, :, :], qT.unsqueeze(1).to_broadcast([C, H, T]),
                                s["head_mask"][:, :].unsqueeze(2).to_broadcast([C, H, T]), ALU.mult
                                ).then_inc(m["q_blk_done"], 1)
        if not first:
            pool.wait_ge(m["scored"], 12 * (q - 1) + CREDIT["scored"])
        for g in range(G):
            parts = s["q_parts"][:, g, bass.ds(q * T, T)]
            nc.gpsimd.tensor_tensor(q_op[u][0:96, g, :, :], parts.unsqueeze(1).to_broadcast([96, GH, T]),
                                    s["quad_mask"][0:96, :].unsqueeze(2).to_broadcast([96, GH, T]),
                                    ALU.mult).then_inc(m["q_op_done"], 1)

    def normalise(pool, q, u, first):
        pool.wait_ge(m["ve_done"], q + 1)
        nc.gpsimd.tensor_tensor(rstd[:, :], ve[:, :], s["minus_half"][0:JP, :], ALU.pow
                                ).then_inc(m["rstd_done"], 1)
        if not first:
            pool.wait_ge(m["transposed"], q - 1 + CREDIT["transposed"])
        nc.gpsimd.tensor_tensor(xhat[u][:, :, :], raw[u][:, :, :],
                                mv[:, :, 0:1].to_broadcast([JP, NT, C]), ALU.subtract
                                ).then_inc(m["centred"], 1)
        pool.wait_ge(m["centred"], q + 1)
        pool.wait_ge(m["rstd_done"], q + 1)
        nc.gpsimd.tensor_tensor(xhat[u][:, :, :], xhat[u][:, :, :],
                                rstd[:, :].unsqueeze(2).to_broadcast([JP, NT, C]), ALU.mult
                                ).then_inc(m["normed"], 1)

    def statistics(dve, q, u, first):
        dve.wait_ge(*loaded(q, u))
        if not first:
            dve.wait_ge(m["normed"], q + CREDIT["normed"])
        for n in range(NT):
            nc.vector.bn_stats(stats[:, n, :], raw[u][:, n, :]).then_inc(m["stat"], 1)
        wait_alone(dve, m["gates"], m["stat"], NT * (q + 1))
        for n in range(NT):
            nc.vector.bn_aggr(mv[:, n, :], stats[:, n, :]).then_inc(m["aggr"], 1)
        dve.wait_ge(m["aggr"], NT * (q + 1))
        nc.vector.tensor_scalar(ve[:, :], mv[:, :, 1], EPS, None, ALU.add).then_inc(m["ve_done"], 1)

    def low_keys(dve, q, first):
        dve.wait_ge(m["k_hi_done"], q + 1)
        if not first:
            dve.wait_ge(m["copied"], CPY * q + CREDIT["copied"])
        nc.vector.scalar_tensor_tensor(out=k_lo[:, :].rearrange("p (a n) -> p a n", a=3),
                                       in0=ps[:, 4:7, 0:JB], scalar=k_bias,
                                       in1=k_hi[:, :].bitcast(F32).rearrange("p (a n) -> p a n", a=3),
                                       op0=ALU.add, op1=ALU.subtract).then_inc(m["k_lo_done"], 1)

    def maximum(dve, q, u, t):
        dve.wait_ge(m["max_scored"], SM * q + t + 1 + CREDIT["max_scored"])
        nc.vector.tensor_reduce(negmax[u][:, t:t + 1], ps[:, 4:7, 0:JB], AX.XY, ALU.max, negate=True
                                ).then_inc(m["max_done"], 1)

    def maxima_rows(dve, q, u):
        dve.wait_ge(m["max_turned"], q + 1)
        nc.vector.tensor_tensor(q_op[u][96:KROWS, :, :, :].rearrange("p g h t -> p (g h t)").rearrange(
                                    "p (a n) -> p a n", n=128),
                                ps[0:SM, 4, 0:128].unsqueeze(1).to_broadcast([SM, SM, 128]),
                                s["ident"][0:SM, 0:SM].unsqueeze(2).to_broadcast([SM, SM, 128]),
                                ALU.mult).then_inc(m["max_rows"], 1)

    def read_sums(dve, b):
        dve.wait_ge(m["summed"], NT * (b + 1) + CREDIT["summed"])
        nc.vector.tensor_copy(s["oT_all"][:, :, bass.ds(b * T, T)],
                              ps[:, 7, 0:GT].rearrange("p (k t) -> p k t", t=T)).then_inc(m["sums_read"], 1)

    def exponential(act, b, u, n):
        act.wait_ge(m["scored"], NT * b + n + 1 + CREDIT["scored"])
        act.wait_ge(m["summed"], NT * b + n - 1 + CREDIT["summed"])
        k = n % 2
        nc.scalar.activation(probs[k][:, :].rearrange("p (a n) -> p a n", a=2),
                             ps[0:JP, 2 * k:2 * k + 2, 0:2 * GT], ACT.Exp).then_inc(m["exped"], 1)

    def read_ctxT(act, q):
        act.wait_ge(m["transposed"], q + 1 + CREDIT["transposed"])
        nc.scalar.activation(ctxT[:, :].rearrange("p (a n) -> p a n", a=3), ps[:, 4:7, 0:JB], ACT.Copy
                             ).then_inc(m["ctxT_done"], 1)

    def high_keys(act, q, first):
        act.wait_ge(m["k_projected"], q + 1)
        if not first:
            act.wait_ge(m["copied"], CPY * q + CREDIT["copied"])
        nc.scalar.activation(k_hi[:, :].rearrange("p (a n) -> p a n", a=3), ps[:, 4:7, 0:JB],
                             ACT.Identity, bias=k_bias).then_inc(m["k_hi_done"], 1)

    def read_values(act, q, u):
        act.wait_ge(m["v_projected"], q + 1)
        nc.scalar.activation(v_op[u][:, :, 0:H * VH].rearrange("p n (h e) -> p n h e", e=VH)[:, :, :, 0:D],
                             ps[0:JP, 4:7, :].rearrange("p a (b h d) -> p (a b) h d", b=4, d=D), ACT.Copy
                             ).then_inc(m["v_read"], 1)

    def transpose_ctx(pe, q, u, first):
        pe.wait_ge(*source_ready(q, u))
        if not first:
            pe.wait_ge(m["v_read"], q + CREDIT["v_read"])
        for n in range(NT):
            mm = nc.tensor.transpose(ps[:, 4 + n // 4, JP * (n % 4):JP * (n % 4) + JP], xhat[u][:, n, :],
                                     s["ident"][0:JP, 0:JP])
        mm.then_inc(m["transposed"], 1)

    def project_keys(pe, q):
        pe.wait_ge(m["ctxT_done"], q + 1)
        for a in range(3):
            mm = nc.tensor.matmul(ps[:, 4 + a, 0:JB], wk[:, :], ctxT[:, JB * a:JB * a + JB],
                                  start=True, stop=True)
        mm.then_inc(m["k_projected"], 1)

    def score_for_max(pe, q, u, t):
        if t == 0:
            pe.wait_ge(m["k_lo_done"], q + 1)
            pe.wait_ge(m["q_blk_done"], q + 1)
        else:
            pe.wait_ge(m["max_done"], SM * q + t)
        rows = q_blk[u][:, :, :].rearrange("p h t -> p (h t)")[:, 128 * t:128 * t + 128]
        for a in range(3):
            mm = nc.tensor.matmul(ps[:, 4 + a, 0:JB], rows, k_hi[:, JB * a:JB * a + JB], start=True, stop=True)
        mm.then_inc(m["max_scored"], 1)

    def turn_maxima(pe, q, u):
        pe.wait_ge(m["max_done"], SM * (q + 1))
        nc.tensor.transpose(ps[0:SM, 4, 0:128], negmax[u][:, :], s["ident"][:, :]).then_inc(m["max_turned"], 1)

    def project_values(pe, q):
        for bank in (1, 2, 0):
            if bank == 0:
                pe.wait_ge(m["max_rows"], q + 1)
            for n in range(4 * bank, 4 * bank + 4):
                mm = nc.tensor.matmul(ps[0:JP, 4 + bank, C * (n % 4):C * (n % 4) + C],
                                      ctxT[:, JP * n:JP * n + JP], wv[:, :], start=True, stop=True)
        mm.then_inc(m["v_projected"], 1)

    def score(pe, b, u, n):
        if n == 0:
            pe.wait_ge(m["copied"], CPY * (b + 1) + CREDIT["copied"])
            pe.wait_ge(m["q_op_done"], G * (b + 1))
            pe.wait_ge(m["max_rows"], b + 1)
        pe.wait_ge(m["exped"], NT * b + n - 1 + CREDIT["exped"])
        for g in range(G):
            mm = nc.tensor.matmul(ps[0:JP, 2 * (n % 2) + g // 2, GT * (g % 2):GT * (g % 2) + GT],
                                  k_op[u][:, g, JP * n:JP * n + JP],
                                  q_op[u][:, g, :, :].rearrange("p h t -> p (h t)"), start=True, stop=True)
        mm.then_inc(m["scored"], 1)

    def weighted_sum(pe, b, u, n):
        if n == 0:
            pe.wait_ge(m["v_read"], b + 1 + CREDIT["v_read"])
            pe.wait_ge(m["sums_read"], b + CREDIT["sums_read"])
        pe.wait_ge(m["exped"], NT * b + n + 1 + CREDIT["exped"])
        for c0, c1, v0 in ((0, 3 * T, 0), (3 * T, 4 * T, 3 * VH)):
            for g in range(G):
                mm = nc.tensor.matmul(ps[32 * g:32 * g + 32, 7, c0:c1],
                                      v_op[u][:, n, GH * VH * g + v0:GH * VH * g + v0 + 32],
                                      probs[n % 2][:, GT * g + c0:GT * g + c1],
                                      start=(n == 0 and c0 == 0), stop=(n == NT - 1), skip_group_check=True)
        mm.then_inc(m["summed"], 1)

    T_SLOT, K_SLOT, S_SLOT = 1, 3, 5

    def tensor_step(pe, b, u, prepare):
        for n in range(NT):
            score(pe, b, u, n)
            if prepare and n == T_SLOT:
                transpose_ctx(pe, b + 1, 1 - u, False)
            if prepare and n == K_SLOT:
                project_keys(pe, b + 1)
            if prepare and n >= S_SLOT:
                score_for_max(pe, b + 1, 1 - u, n - S_SLOT)
            if n >= 1:
                weighted_sum(pe, b, u, n - 1)
        weighted_sum(pe, b, u, NT - 1)
        if prepare:
            turn_maxima(pe, b + 1, 1 - u)
            project_values(pe, b + 1)

    def scalar_step(act, b, u, prepare):
        for n in range(NT):
            exponential(act, b, u, n)
            if prepare and n == T_SLOT:
                read_ctxT(act, b + 1)
            if prepare and n == K_SLOT:
                high_keys(act, b + 1, False)
        if prepare:
            read_values(act, b + 1, 1 - u)

    def vector_step(dve, b, u, prepare, ahead):
        if layer == 0 and ahead:
            statistics(dve, b + 2, u, False)
        if prepare:
            low_keys(dve, b + 1, False)
            for t in range(SM):
                maximum(dve, b + 1, 1 - u, t)
            maxima_rows(dve, b + 1, 1 - u)
        read_sums(dve, b)

    def gpsimd_step(pool, b, u, prepare, ahead):
        if prepare:
            build_queries(pool, b + 1, 1 - u, False)
        if layer == 0 and ahead:
            normalise(pool, b + 2, u, False)

    def sync_step(sp, b, u, prepare, load_next):
        if load_next:
            load_ahead(sp, b, u)
        if prepare:
            copy_keys(sp, b + 1, 1 - u, False)

    LOOPED = B - 4
    TAIL = range(LOOPED, B)

    with nc.Block() as block:
        @block.gpsimd
        def _(pool):
            for name, credit in CREDIT.items():
                if credit:
                    pool.sem_inc(m[name], credit)

        @block.vector
        def _(dve):
            for u in range(2):
                nc.vector.memset(k_op[u][96:KROWS, :, :].bitcast(F32), 1.0).then_inc(m["ones_done"], 1)
                nc.vector.memset(v_op[u][:, :, :], 1.0).then_inc(m["ones_done"], 1)

    with nc.Block() as block:
        @block.sync
        def _(sp):
            load(sp, 0, 0)
            load(sp, 1, 1)
            if layer == 0:
                sp.wait_ge(m["normed"], 1 + CREDIT["normed"])
                load(sp, 2, 0)
            copy_keys(sp, 0, 0, True)
            with sp.Fori(0, LOOPED, 2) as b:
                for u in range(2):
                    sync_step(sp, b + u, u, True, True)
            for b in TAIL:
                sync_step(sp, b, b % 2, b + 1 < B, b + AHEAD < B)

        @block.gpsimd
        def _(pool):
            build_queries(pool, 0, 0, True)
            if layer == 0:
                normalise(pool, 0, 0, True)
                normalise(pool, 1, 1, True)
            with pool.Fori(0, LOOPED, 2) as b:
                for u in range(2):
                    gpsimd_step(pool, b + u, u, True, True)
            for b in TAIL:
                gpsimd_step(pool, b, b % 2, b + 1 < B, b + 2 < B)

        @block.vector
        def _(dve):
            if layer == 0:
                statistics(dve, 0, 0, True)
                statistics(dve, 1, 1, False)
            low_keys(dve, 0, True)
            for t in range(SM):
                maximum(dve, 0, 0, t)
            maxima_rows(dve, 0, 0)
            with dve.Fori(0, LOOPED, 2) as b:
                for u in range(2):
                    vector_step(dve, b + u, u, True, True)
            for b in TAIL:
                vector_step(dve, b, b % 2, b + 1 < B, b + 2 < B)

        @block.scalar
        def _(act):
            read_ctxT(act, 0)
            high_keys(act, 0, True)
            read_values(act, 0, 0)
            with act.Fori(0, LOOPED, 2) as b:
                for u in range(2):
                    scalar_step(act, b + u, u, True)
            for b in TAIL:
                scalar_step(act, b, b % 2, b + 1 < B)

        @block.tensor
        def _(pe):
            transpose_ctx(pe, 0, 0, True)
            project_keys(pe, 0)
            for t in range(SM):
                score_for_max(pe, 0, 0, t)
            turn_maxima(pe, 0, 0)
            project_values(pe, 0)
            with pe.Fori(0, LOOPED, 2) as b:
                for u in range(2):
                    tensor_step(pe, b + u, u, True)
            for b in TAIL:
                tensor_step(pe, b, b % 2, b + 1 < B)


def after_cross(nc, s, own, ps, layer, out):
    def sb(name, shape, dt=F32):
        return own.enter_context(nc.sbuf_tensor(f"p{layer}_{name}", shape, dt))

    oT = sb("oT", [128, GH, CT])
    rden = sb("rden", [PT, NP, G, GH])
    ao = sb("ao", [PT, NP, G, GH, D])
    aoT = sb("aoT", [C, CT])
    y = sb("y", [PT, NP, C])
    yT = sb("yT", [C, CT])
    q32 = sb("q32", [96, G, CT])
    stats = sb("stats", [PT, NP, 6])
    mv = sb("mv", [PT, NP, 2])
    ve = sb("ve", [PT, NP])
    rstd = sb("rstd", [PT, NP])
    yhat = sb("yhat", [PT, NP, C])
    yg = sb("yg", [PT, NP, C])
    yb = sb("yb", [PT, NP, C])
    names = ["staged", "turned", "rden_done", "ao_done", "ao_tr", "aoT_done", "proj", "y_done", "y_kept",
             "y_tr", "yT_done", "qp", "q_store", "q32_done", "q_hi", "q_lo", "st", "ag", "ve_done", "rs",
             "xh", "gained", "offset", "stored", "gates", "sp_gates"]
    m = own.enter_context(semaphores(nc, f"p{layer}_", names))
    wo = s[f"wo{layer}"]
    v_bias = s["kv_bias"][:, 1:2] if layer == 0 else s["cols"][:, BV:BV + 1]
    out_pairs = out.rearrange("b t d -> (b t) d").rearrange("(n p) d -> p n d", p=PT)

    with nc.Fori(0, NC) as c:
        with nc.Block() as block:
            def step(name, per_chunk, k):
                return m[name], c * per_chunk + k

            @block.scalar
            def _(act):
                nc.scalar.activation(oT[:, :, :], s["oT_all"][:, :, bass.ds(c * CT, CT)], ACT.Copy
                                     ).then_inc(m["staged"], 1)
                act.wait_ge(*step("ao_tr", 1, 1))
                nc.scalar.activation(aoT[:, :], ps[:, 4, 0:CT], ACT.Identity, bias=v_bias
                                     ).then_inc(m["aoT_done"], 1)
                if layer == 0:
                    act.wait_ge(*step("y_tr", 1, 1))
                    nc.scalar.activation(yT[:, :], ps[:, 6, 0:CT], ACT.Copy).then_inc(m["yT_done"], 1)
                    q_store_act(nc, act, s, 1, c, ps, q32, 7, range(G), m, step)

            @block.tensor
            def _(pe):
                pe.wait_ge(*step("staged", 1, 1))
                for p in range(NP):
                    for k in range(GH):
                        mm = nc.tensor.transpose(ps[0:PT, p, 128 * k:128 * k + 128],
                                                 oT[:, k, PT * p:PT * p + PT], s["ident"][:, :])
                    mm.then_inc(m["turned"], 1)
                for p in range(NP):
                    pe.wait_ge(*step("ao_done", 2 * NP, 2 * p + 2))
                    mm = nc.tensor.transpose(ps[:, 4, PT * p:PT * p + PT],
                                             ao[:, p, :, :, :].rearrange("p g k d -> p (g k d)"),
                                             s["ident"][0:PT, 0:PT])
                mm.then_inc(m["ao_tr"], 1)
                pe.wait_ge(*step("aoT_done", 1, 1))
                for p in range(NP):
                    mm = nc.tensor.matmul(ps[0:PT, 5, C * p:C * p + C], aoT[:, PT * p:PT * p + PT], wo[:, :],
                                          start=True, stop=True)
                mm.then_inc(m["proj"], 1)
                if layer == 0:
                    pe.wait_ge(*step("y_done", 1, 1))
                    for p in range(NP):
                        mm = nc.tensor.transpose(ps[:, 6, PT * p:PT * p + PT], y[:, p, :], s["ident"][0:PT, 0:PT])
                    mm.then_inc(m["y_tr"], 1)
                    pe.wait_ge(*step("yT_done", 1, 1))
                    q_project_pe(nc, s, 1, ps, yT, 7, range(G), m["qp"])

            @block.vector
            def _(dve):
                for p in range(NP):
                    dve.wait_ge(*step("turned", NP, p + 1))
                    low = ps[0:PT, p, 0:3 * (128 + VH)].rearrange("p (k f) -> p k f", k=3)[:, :, 0:128].rearrange(
                        "p k (g r) -> p k g r", g=G)
                    top = ps[0:PT, p, 3 * 128:4 * 128].rearrange("p (g r) -> p g r", g=G)
                    nc.vector.reciprocal(rden[:, p, :, 0:3].rearrange("p g k -> p k g"), low[:, :, :, D]
                                         ).then_inc(m["rden_done"], 1)
                    nc.vector.reciprocal(rden[:, p, :, 3], top[:, :, D]).then_inc(m["rden_done"], 1)
                    dve.wait_ge(*step("rden_done", 2 * NP, 2 * p + 2))
                    nc.vector.tensor_tensor(ao[:, p, :, 0:3, :].rearrange("p g k d -> p k g d"),
                                            low[:, :, :, 0:D],
                                            rden[:, p, :, 0:3].rearrange("p g k -> p k g").unsqueeze(3).to_broadcast(
                                                [PT, 3, G, D]), ALU.mult).then_inc(m["ao_done"], 1)
                    nc.vector.tensor_tensor(ao[:, p, :, 3, :], top[:, :, 0:D],
                                            rden[:, p, :, 3].unsqueeze(2).to_broadcast([PT, G, D]), ALU.mult
                                            ).then_inc(m["ao_done"], 1)
                dve.wait_ge(*step("proj", 1, 1))
                nc.vector.tensor_tensor(y[:, :, :], ps[0:PT, 5, :].rearrange("p (a n) -> p a n", n=C),
                                        s["resid"][:, bass.ds(c * NP, NP), :], ALU.add).then_inc(m["y_done"], 1)
                if layer == 0:
                    q_low_dve(nc, dve, s, c, q32, m, step)
                    return
                dve.wait_ge(*step("y_done", 1, 1))
                for p in range(NP):
                    nc.vector.bn_stats(stats[:, p, :], y[:, p, :]).then_inc(m["st"], 1)
                wait_alone(dve, m["gates"], *step("st", NP, NP))
                for p in range(NP):
                    nc.vector.bn_aggr(mv[:, p, :], stats[:, p, :]).then_inc(m["ag"], 1)
                dve.wait_ge(*step("ag", NP, NP))
                nc.vector.tensor_scalar(ve[:, :], mv[:, :, 1], EPS, None, ALU.add).then_inc(m["ve_done"], 1)
                dve.wait_ge(*step("rs", 1, 1))
                for p in range(NP):
                    nc.vector.tensor_scalar(yhat[:, p, :], y[:, p, :], mv[:, p, 0:1], rstd[:, p:p + 1],
                                            ALU.subtract, ALU.mult).then_inc(m["xh"], 1)
                dve.wait_ge(*step("xh", NP, NP))
                nc.vector.tensor_tensor(yg[:, :, :], yhat[:, :, :],
                                        s["rows"][:, LN_G, :].unsqueeze(1).to_broadcast([PT, NP, C]), ALU.mult
                                        ).then_inc(m["gained"], 1)
                dve.wait_ge(*step("gained", 1, 1))
                nc.vector.tensor_tensor(yb[:, :, :], yg[:, :, :],
                                        s["rows"][:, LN_B, :].unsqueeze(1).to_broadcast([PT, NP, C]), ALU.add
                                        ).then_inc(m["offset"], 1)

            @block.gpsimd
            def _(pool):
                if layer == 0:
                    pool.wait_ge(*step("y_done", 1, 1))
                    nc.gpsimd.tensor_tensor(s["resid"][:, bass.ds(c * NP, NP), :], y[:, :, :],
                                            s["rows"][:, BO, :].unsqueeze(1).to_broadcast([PT, NP, C]), ALU.add
                                            ).then_inc(m["y_kept"], 1)
                else:
                    pool.wait_ge(*step("ve_done", 1, 1))
                    nc.gpsimd.tensor_tensor(rstd[:, :], ve[:, :], s["minus_half"][0:PT, 0:NP], ALU.pow
                                            ).then_inc(m["rs"], 1)

            @block.sync
            def _(sp):
                if layer == 1:
                    sp.wait_ge(*step("offset", 1, 1))
                    sp.dma_start(out_pairs[:, bass.ds(c * NP, NP), :], yb[:, :, :]).then_inc(m["stored"], 16)
                    wait_alone(sp, m["sp_gates"], *step("stored", 16, 16))


def kernel(**inputs):
    import numpy as _np
    import concourse.bacc as _bacc
    from concourse import mybir as _mybir
    from concourse.bass_utils import run_bass_kernel_spmd as _run

    nc = _bacc.Bacc("TRN2", target_bir_lowering=False, num_devices=1)
    arrays, args = {}, {}
    for name, value in inputs.items():
        a = _np.ascontiguousarray(value)
        arrays[f"in_{name}_dram"] = a
        args[name] = nc.dram_tensor(f"in_{name}_dram", a.shape, _mybir.dt.from_np(a.dtype),
                                    kind="ExternalInput").ap()
    y = nc.dram_tensor("out_0_dram", (B, T, C), F32, kind="ExternalOutput").ap()
    build(nc, args.pop("x"), args.pop("ctx_1024"), args.pop("mask_BxS_bf0"), args, y)
    r = _run(nc, [arrays], core_ids=[0])
    return r.results[0]["out_0_dram"]
```

```python
from contextlib import ExitStack, contextmanager

import concourse.bass as bass
from concourse import mybir
from concourse.alu_op_type import AluOpType as ALU

F32 = mybir.dt.float32
F32R = mybir.dt.float32r
U8 = mybir.dt.uint8
ACT = mybir.ActivationFunctionType
AX = mybir.AxisListType

B, T, J, C, H = 32, 56, 1500, 128, 16
D = C // H
FF = 4 * C
GH = 4
G = H // GH
HT = H * T
GT = GH * T
NT = 12
JP = J // NT
JB = J // 3
SM = HT // 128
KROWS = 96 + SM
VH = D + 1
VW = 168
TOK = B * T
NC = 4
CT = TOK // NC
CB = B // NC
PT = 2 * T
NP = CT // PT
EPS = 1e-5
MASKED = -1e30


def build(nc, x, ctx, mask, w, out):
    with ExitStack() as stack:
        def sb(name, shape, dt=F32):
            return stack.enter_context(nc.sbuf_tensor(name, shape, dt))

        s = {
            "ident": sb("ident", [128, 128]),
            "head_mask": sb("head_mask", [128, H]),
            "quad_mask": sb("quad_mask", [128, GH]),
            "minus_half": sb("minus_half", [128, NT]),
            "zero_cols": sb("zero_cols", [128, G]),
            "rows": sb("rows", [PT, 6, C]),
            "cols": sb("cols", [C, 9]),
            "bq_rep": sb("bq_rep", [96, G]),
            "bq_rep_scaled": sb("bq_rep_scaled", [96, G]),
            "bq_scaled": sb("bq_scaled", [C, 1]),
            "kv_bias": sb("kv_bias", [C, 2]),
            "resid": sb("resid", [PT, B // 2, C]),
            "qT_all": sb("qT_all", [C, TOK]),
            "q_parts": sb("q_parts", [96, G, TOK]),
            "oT_all": sb("oT_all", [128, GH, TOK]),
        }
        s["wq1"] = sb("wq1", [C, C])
        s["wq_rep1"] = sb("wq_rep1", [C, G, 3, 32])
        for layer in (0, 1):
            s[f"wk{layer}"] = sb(f"wk{layer}", [C, C])
            s[f"wv{layer}"] = sb(f"wv{layer}", [C, C])
            s[f"wo{layer}"] = sb(f"wo{layer}", [C, C])
        ps = stack.enter_context(nc.psum_tensor("ps", [128, 8, 512], F32))

        with ExitStack() as own:
            for name, shape in (("wqkv", [C, 3 * C]), ("wproj", [C, C]), ("w1", [C, FF]), ("w2", [C, 4, C]),
                                ("ed_wkv", [C, 2 * C]), ("b1_cols", [C, 4]), ("causal", [128, T]),
                                ("causal_low", [128, T]), ("wq0", [C, C]), ("wq_rep0", [C, G, 3, 32])):
                s[name] = own.enter_context(nc.sbuf_tensor(name, shape, F32))
            setup(nc, s, own, ps, w)
            self_attention_and_ff(nc, s, own, ps, x, mask)
        for layer in (0, 1):
            with ExitStack() as own:
                cross_attention(nc, s, own, ps, ctx, layer)
            with ExitStack() as own:
                after_cross(nc, s, own, ps, layer, out)


@contextmanager
def semaphores(nc, prefix, names):
    m = {n: nc.alloc_semaphore(prefix + n) for n in names}
    yield m
    nc.clear_and_free_semaphores(list(m.values()))
    nc.all_engine_barrier()


def wait_alone(eng, gates, sem, value):
    eng.wait_ge(sem, value)
    eng.sem_inc(gates, 1)


COLS = ["L0_xattn_ln1_g", "L0_xattn_ln1_b", "L0_xattn_ln2_g", "L0_xattn_ln2_b", "L0_xattn_ln3_g",
        "L0_xattn_ln3_b", "L1_xattn_bq", "L1_xattn_bk", "L1_xattn_bv"]
LN1_G, LN1_B, LN2_G, LN2_B, LN3_G, LN3_B, BQ, BK, BV = range(9)
ROWS = ["L0_xattn_sa_bproj", "L0_xattn_ed_bproj", "L0_xattn_ff_b2", "L1_xattn_bo", "L1_xattn_ln_g",
        "L1_xattn_ln_b"]
SA_B, ED_B, FF_B2, BO, LN_G, LN_B = range(6)
SCALE = [C ** -0.5, D ** -0.5]


def setup(nc, s, own, ps, w):
    m = own.enter_context(semaphores(nc, "su_", ["loaded", "consts", "consts_dve", "bias_ready", "folded"]))
    loaded, consts, consts_dve = m["loaded"], m["consts"], m["consts_dve"]
    bias_ready, folded = m["bias_ready"], m["folded"]
    loads = [
        (s["wqkv"][:, :], w["L0_xattn_sa_wqkv"]),
        (s["wproj"][:, :], w["L0_xattn_sa_wproj"]),
        (s["w1"][:, :], w["L0_xattn_ff_w1"]),
        (s["w2"][:, :, :], w["L0_xattn_ff_w2"].rearrange("(k p) n -> p k n", p=C)),
        (s["ed_wkv"][:, :], w["L0_xattn_ed_wkv"]),
        (s["wq0"][:, :], w["L0_xattn_ed_wq"]),
        (s["wo0"][:, :], w["L0_xattn_ed_wproj"]),
        (s["wq1"][:, :], w["L1_xattn_Wq"]),
        (s["wk1"][:, :], w["L1_xattn_Wk"]),
        (s["wv1"][:, :], w["L1_xattn_Wv"]),
        (s["wo1"][:, :], w["L1_xattn_Wo"]),
        (s["b1_cols"][:, :], w["L0_xattn_ff_b1"].rearrange("(k p) -> p k", p=C)),
    ]
    loads += [(s["cols"][:, i:i + 1], w[n].unsqueeze(1)) for i, n in enumerate(COLS)]
    loads += [(s["rows"][:, i, :], w[n].unsqueeze(0).to_broadcast([PT, C])) for i, n in enumerate(ROWS)]
    loads += [(s["bq_rep"][32 * i:32 * i + 32, :], w["L1_xattn_bq"].rearrange("(g r) -> r g", r=32))
              for i in range(3)]

    with nc.Block() as block:
        @block.sync
        def _(sp):
            with nc.allow_non_contiguous_dma("parameters as columns, once"):
                for dst, src in loads[::2]:
                    sp.dma_start(dst, src).then_inc(loaded, 16)

        @block.scalar
        def _(act):
            with nc.allow_non_contiguous_dma("parameters as columns, once"):
                for dst, src in loads[1::2]:
                    act.dma_start(dst, src).then_inc(loaded, 16)

        @block.gpsimd
        def _(pool):
            nc.gpsimd.memset(s["ident"][:, :], 1.0).then_inc(consts, 1)
            nc.gpsimd.memset(s["head_mask"][:, :], 1.0).then_inc(consts, 1)
            nc.gpsimd.memset(s["causal"][:, :], 0.0).then_inc(consts, 1)
            nc.gpsimd.memset(s["causal_low"][:, :], 0.0).then_inc(consts, 1)
            nc.gpsimd.memset(s["minus_half"][:, :], -0.5).then_inc(consts, 1)
            nc.gpsimd.memset(s["zero_cols"][:, :], 0.0).then_inc(consts, 1)
            pool.wait_ge(consts, 6)
            nc.gpsimd.affine_select(out=s["ident"][:, :], in_=s["ident"][:, :], compare_op=ALU.is_equal,
                                    fill=0.0, base=0, pattern=[[-1, 128]], channel_multiplier=1
                                    ).then_inc(consts, 1)
            nc.gpsimd.affine_select(out=s["head_mask"][:, :], in_=s["head_mask"][:, :],
                                    compare_op=ALU.is_ge, fill=0.0, base=0, pattern=[[-D, H]],
                                    channel_multiplier=1).then_inc(consts, 1)
            pool.wait_ge(consts, 8)
            nc.gpsimd.affine_select(out=s["head_mask"][:, :], in_=s["head_mask"][:, :],
                                    compare_op=ALU.is_ge, fill=0.0, base=D - 1, pattern=[[D, H]],
                                    channel_multiplier=-1).then_inc(consts, 1)
            nc.gpsimd.affine_select(out=s["causal"][:, :], in_=s["causal"][:, :], compare_op=ALU.is_ge,
                                    fill=MASKED, base=0, pattern=[[-1, T]], channel_multiplier=1
                                    ).then_inc(consts, 1)
            nc.gpsimd.affine_select(out=s["causal_low"][:, :], in_=s["causal_low"][:, :],
                                    compare_op=ALU.is_ge, fill=MASKED, base=-64, pattern=[[-1, T]],
                                    channel_multiplier=1).then_inc(consts, 1)

        @block.tensor
        def _(pe):
            pe.wait_ge(loaded, 16 * len(loads))
            nc.tensor.matmul(ps[:, 0, 0:1], s["ed_wkv"][:, 0:C], s["cols"][:, LN2_B:LN2_B + 1],
                             start=True, stop=True)
            nc.tensor.matmul(ps[:, 0, 1:2], s["ed_wkv"][:, C:2 * C], s["cols"][:, LN2_B:LN2_B + 1],
                             start=True, stop=True).then_inc(bias_ready, 1)

        @block.vector
        def _(dve):
            dve.wait_ge(consts, 11)
            nc.vector.tensor_reduce(s["quad_mask"][:, :],
                                    s["head_mask"][:, :].rearrange("p (g a) -> p a g", a=GH),
                                    AX.X, ALU.add).then_inc(consts_dve, 1)
            nc.vector.tensor_copy(s["causal"][64:128, :], s["causal_low"][64:128, :]).then_inc(consts_dve, 1)
            dve.wait_ge(loaded, 16 * len(loads))
            g2 = s["cols"][:, LN2_G:LN2_G + 1]
            nc.vector.tensor_scalar(s["wk0"][:, :], s["ed_wkv"][:, 0:C], g2, None, ALU.mult).then_inc(folded, 1)
            nc.vector.tensor_scalar(s["wv0"][:, :], s["ed_wkv"][:, C:2 * C], g2, None, ALU.mult).then_inc(folded, 1)
            for layer in (0, 1):
                for part in range(3):
                    nc.vector.tensor_copy(s[f"wq_rep{layer}"][:, :, part, :],
                                          s[f"wq{layer}"][:, :].rearrange("p (g r) -> p g r", r=32)
                                          ).then_inc(folded, 1)
            nc.vector.tensor_scalar(s["bq_rep_scaled"][:, :], s["bq_rep"][:, :], SCALE[1], None,
                                    ALU.mult).then_inc(folded, 1)
            nc.vector.tensor_scalar(s["bq_scaled"][:, :], s["cols"][:, BQ:BQ + 1], SCALE[1], None,
                                    ALU.mult).then_inc(folded, 1)
            dve.wait_ge(bias_ready, 1)
            nc.vector.tensor_copy(s["kv_bias"][:, :], ps[:, 0, 0:2]).then_inc(folded, 1)


def queries(layer, s):
    if layer == 0:
        return s["wq0"], s["wq_rep0"], SCALE[0], s["zero_cols"][:, 0:1], s["zero_cols"][0:96, :]
    return s["wq1"], s["wq_rep1"], SCALE[1], s["bq_scaled"][:, :], s["bq_rep_scaled"][:, :]


def q_project_pe(nc, s, layer, ps, hT, bank_q, banks_g, done):
    wq, wq_rep, _, _, _ = queries(layer, s)
    nc.tensor.matmul(ps[:, bank_q, 0:CT], wq[:, :], hT[:, :], start=True, stop=True).then_inc(done, 1)
    for g in range(G):
        nc.tensor.matmul(ps[0:96, banks_g[g], 0:CT], wq_rep[:, g, :, :].rearrange("p a r -> p (a r)"),
                         hT[:, :], start=True, stop=True).then_inc(done, 1)


def self_attention_and_ff(nc, s, own, ps, x, mask):
    def sb(name, shape, dt=F32):
        return own.enter_context(nc.sbuf_tensor(name, shape, dt))

    xc = sb("a_x", [PT, NP, C])
    pad = sb("a_pad", [128, NP, T], U8)
    bias = sb("a_bias", [128, NP, T])
    stats = sb("a_stats", [PT, NP, 6])
    mv = sb("a_mv", [PT, NP, 2])
    ve = sb("a_ve", [PT, NP])
    rstd = sb("a_rstd", [PT, NP])
    xhat = sb("a_xhat", [PT, NP, C])
    x_b = sb("a_x_b", [PT, NP, C])
    h1T = sb("a_h1T", [C, CT])
    h3T = sb("a_h3T", [C, CT])
    qTp = sb("a_qTp", [C, CB, 64])
    kT = sb("a_kT", [C, CB, T])
    vS = sb("a_v", [T, CB, C])
    kblk = sb("a_kblk", [C, CB, H, T])
    scores = sb("a_scores", [128, NP, H, T])
    negmax = sb("a_negmax", [128, NP, H])
    probs = sb("a_probs", [128, NP, H, T])
    denom = sb("a_denom", [128, NP, H])
    rden = sb("a_rden", [128, NP, H])
    probsT = sb("a_probsT", [T, 2, H, 128])
    ao = sb("a_ao", [128, NP, H, D])
    aoT = sb("a_aoT", [C, NP, PT])
    r1 = sb("a_r1", [PT, NP, C])
    r1_b = sb("a_r1_b", [PT, NP, C])
    h2T = sb("a_h2T", [C, CT])
    hidT = sb("a_hidT", [C, 4, CT])
    ff = sb("a_ff", [PT, NP, C])
    q32 = sb("a_q32", [96, G, CT])

    names = ["x_loaded", "zeroed", "bias_done", "st1", "ag1", "ve1", "rs1", "xh1", "tr1", "h1", "h3",
             "qkv", "q_ev", "k_ev", "v_ev", "kblk_done", "ff1", "hid", "ff2", "ff_ev", "xb", "sc",
             "masked", "mx", "shifted", "exp", "den", "rden_done", "ptr", "pt_ev", "pv", "ao_done",
             "ao_tr", "aoT_ev", "proj", "r1_done", "r1b", "st2", "ag2", "ve2", "rs2", "xh2", "tr2", "h2",
             "qp", "q_store", "q32_done", "q_hi", "q_lo", "res_done", "gates", "pe_gates"]
    m = own.enter_context(semaphores(nc, "a_", names))
    x_pairs = x.rearrange("b t d -> (b t) d").rearrange("(n p) d -> p n d", p=PT)
    mask_pairs = mask.rearrange("(n u) s -> u n s", u=2)

    with nc.Block() as block:
        @block.vector
        def _(dve):
            nc.vector.memset(qTp[:, :, :], 0.0).then_inc(m["zeroed"], 1)
            nc.vector.memset(pad[:, :, :], 0).then_inc(m["zeroed"], 1)

    with nc.Fori(0, NC) as c:
        with nc.Block() as block:
            def step(name, per_chunk, k):
                return m[name], c * per_chunk + k

            @block.sync
            def _(sp):
                sp.dma_start(xc[:, :, :], x_pairs[:, bass.ds(c * NP, NP), :]).then_inc(m["x_loaded"], 16)
                for u in range(2):
                    sp.dma_start(pad[64 * u:64 * u + T, :, :],
                                 mask_pairs[u:u + 1, bass.ds(c * NP, NP), :].to_broadcast([T, NP, T])
                                 ).then_inc(m["x_loaded"], 16)

            @block.gpsimd
            def _(pool):
                pool.wait_ge(*step("x_loaded", 48, 48))
                nc.gpsimd.tensor_tensor(x_b[:, :, :], xc[:, :, :],
                                        s["rows"][:, SA_B, :].unsqueeze(1).to_broadcast([PT, NP, C]),
                                        ALU.add).then_inc(m["xb"], 1)
                pool.wait_ge(*step("ve1", 1, 1))
                nc.gpsimd.tensor_tensor(rstd[:, :], ve[:, :], s["minus_half"][0:PT, 0:NP], ALU.pow
                                        ).then_inc(m["rs1"], 1)
                for j in range(CB):
                    if j == 0:
                        pool.wait_ge(*step("k_ev", 1, 1))
                    nc.gpsimd.tensor_tensor(kblk[:, j, :, :],
                                            kT[:, j, :].unsqueeze(1).to_broadcast([C, H, T]),
                                            s["head_mask"][:, :].unsqueeze(2).to_broadcast([C, H, T]),
                                            ALU.mult).then_inc(m["kblk_done"], 1)
                pool.wait_ge(*step("r1_done", 1, 1))
                nc.gpsimd.tensor_tensor(r1_b[:, :, :], r1[:, :, :],
                                        s["rows"][:, ED_B, :].unsqueeze(1).to_broadcast([PT, NP, C]),
                                        ALU.add).then_inc(m["r1b"], 1)
                pool.wait_ge(*step("ve2", 1, 1))
                nc.gpsimd.tensor_tensor(rstd[:, :], ve[:, :], s["minus_half"][0:PT, 0:NP], ALU.pow
                                        ).then_inc(m["rs2"], 1)

            def layer_norm(dve, src, n, wait):
                dve.wait_ge(*wait)
                for p in range(NP):
                    nc.vector.bn_stats(stats[:, p, :], src[:, p, :]).then_inc(m[f"st{n}"], 1)
                wait_alone(dve, m["gates"], *step(f"st{n}", NP, NP))
                for p in range(NP):
                    nc.vector.bn_aggr(mv[:, p, :], stats[:, p, :]).then_inc(m[f"ag{n}"], 1)
                dve.wait_ge(*step(f"ag{n}", NP, NP))
                nc.vector.tensor_scalar(ve[:, :], mv[:, :, 1], EPS, None, ALU.add).then_inc(m[f"ve{n}"], 1)
                dve.wait_ge(*step(f"rs{n}", 1, 1))
                for p in range(NP):
                    nc.vector.tensor_scalar(xhat[:, p, :], src[:, p, :], mv[:, p, 0:1], rstd[:, p:p + 1],
                                            ALU.subtract, ALU.mult).then_inc(m[f"xh{n}"], 1)

            @block.vector
            def _(dve):
                layer_norm(dve, xc, 1, step("x_loaded", 48, 48))
                nc.vector.scalar_tensor_tensor(out=bias[:, :, :], in0=pad[:, :, :], scalar=MASKED,
                                               in1=s["causal"][:, :].unsqueeze(1).to_broadcast([128, NP, T]),
                                               op0=ALU.mult, op1=ALU.add).then_inc(m["bias_done"], 1)
                dve.wait_ge(*step("h1", 1, 1))
                nc.vector.tensor_scalar(h3T[:, :], ps[:, 0, 0:CT], s["cols"][:, LN3_G:LN3_G + 1],
                                        s["cols"][:, LN3_B:LN3_B + 1], ALU.mult, ALU.add
                                        ).then_inc(m["h3"], 1)
                dve.wait_ge(*step("qkv", 4, 1))
                nc.vector.tensor_copy(kT[:, :, :], ps[:, 1, 0:CT].rearrange("p (b t) -> p b t", t=T)
                                      ).then_inc(m["k_ev"], 1)
                dve.wait_ge(*step("qkv", 4, 4))
                nc.vector.tensor_copy(vS[:, :, :], ps[0:T, 2:4, :].rearrange("p a (b n) -> p (a b) n", n=C)
                                      ).then_inc(m["v_ev"], 1)
                dve.wait_ge(*step("ff2", 1, 1))
                nc.vector.tensor_tensor(ff[:, :, :], ps[0:PT, 5, :].rearrange("p (a n) -> p a n", n=C),
                                        s["rows"][:, FF_B2, :].unsqueeze(1).to_broadcast([PT, NP, C]),
                                        ALU.add).then_inc(m["ff_ev"], 1)

                def normalised(p):
                    dve.wait_ge(*step("pv", NP, p + 1))
                    dve.wait_ge(*step("rden_done", NP, p + 1))
                    nc.vector.tensor_tensor(ao[:, p, :, :],
                                            ps[:, 6 + p % 2, 0:C].rearrange("p (h d) -> p h d", d=D),
                                            rden[:, p, :].unsqueeze(2).to_broadcast([128, H, D]),
                                            ALU.mult).then_inc(m["ao_done"], 1)

                def denominators(p):
                    dve.wait_ge(*step("exp", NP, p + 1))
                    nc.vector.tensor_reduce(denom[:, p, :], probs[:, p, :, :], AX.X, ALU.add
                                            ).then_inc(m["den"], 1)
                    dve.wait_ge(*step("den", NP, p + 1))
                    nc.vector.reciprocal(rden[:, p, :], denom[:, p, :]).then_inc(m["rden_done"], 1)

                for p in range(NP):
                    dve.wait_ge(*step("sc", NP, p + 1))
                    if p == 0:
                        dve.wait_ge(*step("bias_done", 1, 1))
                    for half in range(2):
                        hs = slice(8 * half, 8 * half + 8)
                        nc.vector.tensor_tensor(scores[:, p, hs, :],
                                                ps[:, 4 + half, 0:CT].rearrange("p (h t) -> p h t", t=T),
                                                bias[:, p, :].unsqueeze(1).to_broadcast([128, 8, T]),
                                                ALU.add).then_inc(m["masked"], 1)
                    dve.wait_ge(*step("masked", 2 * NP, 2 * p + 2))
                    nc.vector.tensor_reduce(negmax[:, p, :], scores[:, p, :, :], AX.X, ALU.max,
                                            negate=True).then_inc(m["mx"], 1)
                    dve.wait_ge(*step("mx", NP, p + 1))
                    nc.vector.tensor_tensor(scores[:, p, :, :], scores[:, p, :, :],
                                            negmax[:, p, :].unsqueeze(2).to_broadcast([128, H, T]),
                                            ALU.add).then_inc(m["shifted"], 1)
                    if p >= 1:
                        denominators(p - 1)
                    if p >= 2:
                        normalised(p - 2)
                denominators(NP - 1)
                normalised(NP - 2)
                normalised(NP - 1)
                dve.wait_ge(*step("proj", 1, 1))
                dve.wait_ge(*step("xb", 1, 1))
                nc.vector.tensor_tensor(r1[:, :, :], ps[0:PT, 6, :].rearrange("p (a n) -> p a n", n=C),
                                        x_b[:, :, :], ALU.add).then_inc(m["r1_done"], 1)
                layer_norm(dve, r1, 2, step("r1_done", 1, 1))
                dve.wait_ge(*step("r1b", 1, 1))
                nc.vector.tensor_tensor(s["resid"][:, bass.ds(c * NP, NP), :], r1_b[:, :, :], ff[:, :, :],
                                        ALU.add).then_inc(m["res_done"], 1)
                q_low_dve(nc, dve, s, c, q32, m, step)

            @block.scalar
            def _(act):
                act.wait_ge(*step("tr1", 1, 1))
                nc.scalar.activation(h1T[:, :], ps[:, 0, 0:CT], ACT.Identity, bias=s["cols"][:, LN1_B:LN1_B + 1],
                                     scale=s["cols"][:, LN1_G:LN1_G + 1]).then_inc(m["h1"], 1)
                act.wait_ge(*step("qkv", 4, 2))
                nc.scalar.activation(qTp[:, :, 0:T], ps[:, 0, 0:CT].rearrange("p (b t) -> p b t", t=T),
                                     ACT.Copy, scale=SCALE[0]).then_inc(m["q_ev"], 1)
                for k in range(4):
                    act.wait_ge(*step("ff1", 4, k + 1))
                    nc.scalar.activation(hidT[:, k, :], ps[:, 6 + k % 2, 0:CT], ACT.Relu,
                                         bias=s["b1_cols"][:, k:k + 1]).then_inc(m["hid"], 1)

                def transposed(p):
                    act.wait_ge(*step("ptr", NP, p + 1))
                    nc.scalar.activation(probsT[:, p % 2, :, :].rearrange("p h n -> p (h n)"),
                                         ps[0:T, 0:4, :].rearrange("p a n -> p (a n)"), ACT.Copy
                                         ).then_inc(m["pt_ev"], 1)

                for p in range(NP):
                    act.wait_ge(*step("shifted", NP, p + 1))
                    nc.scalar.activation(probs[:, p, :, :], scores[:, p, :, :], ACT.Exp).then_inc(m["exp"], 1)
                    if p >= 1:
                        transposed(p - 1)
                transposed(NP - 1)
                act.wait_ge(*step("ao_tr", 1, 1))
                for p in range(NP):
                    nc.scalar.activation(aoT[:, p, :].rearrange("p (u t) -> p u t", t=T),
                                         ps[:, 7, 128 * p:128 * p + 128].rearrange("p (u t) -> p u t", t=64)[:, :, 0:T],
                                         ACT.Copy).then_inc(m["aoT_ev"], 1)
                act.wait_ge(*step("tr2", 1, 1))
                nc.scalar.activation(h2T[:, :], ps[:, 7, 0:CT], ACT.Identity, bias=s["cols"][:, LN2_B:LN2_B + 1],
                                     scale=s["cols"][:, LN2_G:LN2_G + 1]).then_inc(m["h2"], 1)
                q_store_act(nc, act, s, 0, c, ps, q32, 4, range(G), m, step)

            @block.tensor
            def _(pe):
                pe.wait_ge(*step("xh1", NP, NP))
                for p in range(NP):
                    mm = nc.tensor.transpose(ps[:, 0, PT * p:PT * p + PT], xhat[:, p, :], s["ident"][0:PT, 0:PT])
                mm.then_inc(m["tr1"], 1)
                pe.wait_ge(*step("h1", 1, 1))
                nc.tensor.matmul(ps[:, 1, 0:CT], s["wqkv"][:, C:2 * C], h1T[:, :], start=True, stop=True
                                 ).then_inc(m["qkv"], 1)
                pe.wait_ge(*step("h3", 1, 1))
                nc.tensor.matmul(ps[:, 0, 0:CT], s["wqkv"][:, 0:C], h1T[:, :], start=True, stop=True
                                 ).then_inc(m["qkv"], 1)
                for j in range(CB):
                    mm = nc.tensor.matmul(ps[0:T, 2 + j // 4, C * (j % 4):C * (j % 4) + C],
                                          h1T[:, T * j:T * j + T], s["wqkv"][:, 2 * C:3 * C],
                                          start=True, stop=True)
                    if j % 4 == 3:
                        mm.then_inc(m["qkv"], 1)
                for k in range(4):
                    if k >= 2:
                        pe.wait_ge(*step("hid", 4, k - 1))
                    nc.tensor.matmul(ps[:, 6 + k % 2, 0:CT], s["w1"][:, C * k:C * k + C], h3T[:, :],
                                     start=True, stop=True).then_inc(m["ff1"], 1)
                pe.wait_ge(*step("hid", 4, 4))
                for p in range(NP):
                    for k in range(4):
                        mm = nc.tensor.matmul(ps[0:PT, 5, C * p:C * p + C], hidT[:, k, PT * p:PT * p + PT],
                                              s["w2"][:, k, :], start=(k == 0), stop=(k == 3))
                mm.then_inc(m["ff2"], 1)
                pe.wait_ge(*step("ff_ev", 1, 1))
                pe.wait_ge(*step("q_ev", 1, 1))
                pe.wait_ge(m["zeroed"], 2)

                def score(p):
                    pe.wait_ge(*step("kblk_done", CB, 2 * p + 2))
                    if p >= 1:
                        pe.wait_ge(*step("masked", 2 * NP, 2 * p))
                    for half in range(2):
                        for u in range(2):
                            mm = nc.tensor.matmul(ps[64 * u:64 * u + 64, 4 + half, 0:CT], qTp[:, 2 * p + u, :],
                                                  kblk[:, 2 * p + u, 8 * half:8 * half + 8, :].rearrange(
                                                      "p h t -> p (h t)"), start=True, stop=True)
                    mm.then_inc(m["sc"], 1)

                def transpose_probs(p):
                    pe.wait_ge(*step("exp", NP, p + 1))
                    if p == 0:
                        wait_alone(pe, m["pe_gates"], *step("v_ev", 1, 1))
                    else:
                        wait_alone(pe, m["pe_gates"], *step("pt_ev", NP, p))
                    for h in range(H):
                        mm = nc.tensor.transpose(ps[0:T, h // 4, 128 * (h % 4):128 * (h % 4) + 128],
                                                 probs[:, p, h, :], s["ident"][:, :])
                    mm.then_inc(m["ptr"], 1)

                def values(p):
                    if p >= 2:
                        pe.wait_ge(*step("ao_done", NP, p - 1))
                    wait_alone(pe, m["pe_gates"], *step("pt_ev", NP, p + 1))
                    for u in range(2):
                        for h in range(H):
                            mm = nc.tensor.matmul(ps[64 * u:64 * u + 64, 6 + p % 2, D * h:D * h + D],
                                                  probsT[:, p % 2, h, 64 * u:64 * u + 64],
                                                  vS[:, 2 * p + u, D * h:D * h + D], start=True, stop=True)
                    mm.then_inc(m["pv"], 1)

                score(0)
                for p in range(NP):
                    if p + 1 < NP:
                        score(p + 1)
                    transpose_probs(p)
                    values(p)
                pe.wait_ge(*step("ao_done", NP, NP))
                for p in range(NP):
                    mm = nc.tensor.transpose(ps[:, 7, 128 * p:128 * p + 128],
                                             ao[:, p, :, :].rearrange("p h d -> p (h d)"), s["ident"][:, :])
                mm.then_inc(m["ao_tr"], 1)
                pe.wait_ge(*step("aoT_ev", NP, NP))
                for p in range(NP):
                    mm = nc.tensor.matmul(ps[0:PT, 6, C * p:C * p + C], aoT[:, p, :], s["wproj"][:, :],
                                          start=True, stop=True)
                mm.then_inc(m["proj"], 1)
                pe.wait_ge(*step("xh2", NP, NP))
                for p in range(NP):
                    mm = nc.tensor.transpose(ps[:, 7, PT * p:PT * p + PT], xhat[:, p, :], s["ident"][0:PT, 0:PT])
                mm.then_inc(m["tr2"], 1)
                pe.wait_ge(*step("h2", 1, 1))
                q_project_pe(nc, s, 0, ps, h2T, 4, range(G), m["qp"])


def q_store_act(nc, act, s, layer, c, ps, q32, bank_q, banks_g, m, step):
    _, _, scale, bias, bias_rep = queries(layer, s)
    tokens = bass.ds(c * CT, CT)
    act.wait_ge(*step("qp", 1 + G, 1))
    nc.scalar.activation(s["qT_all"][:, tokens], ps[:, bank_q, 0:CT], ACT.Identity, bias=bias,
                         scale=scale).then_inc(m["q_store"], 1)
    for g in range(G):
        act.wait_ge(*step("qp", 1 + G, 2 + g))
        nc.scalar.activation(q32[:, g, :], ps[0:96, banks_g[g], 0:CT], ACT.Identity,
                             bias=bias_rep[:, g:g + 1], scale=scale).then_inc(m["q32_done"], 1)
    act.wait_ge(*step("q32_done", G, G))
    nc.scalar.activation(s["q_parts"][:, :, tokens].bitcast(F32R), q32[:, :, :], ACT.Copy
                         ).then_inc(m["q_hi"], 1)


def q_low_dve(nc, dve, s, c, q32, m, step):
    low = s["q_parts"][64:96, :, bass.ds(c * CT, CT)]
    dve.wait_ge(*step("q_hi", 1, 1))
    nc.vector.tensor_tensor(low, q32[64:96, :, :], low, ALU.subtract).then_inc(m["q_lo"], 1)


def cross_attention(nc, s, own, ps, ctx, layer):
    def sb(name, shape, dt=F32):
        return own.enter_context(nc.sbuf_tensor(f"c{layer}_{name}", shape, dt))

    raw = [sb(f"raw{u}", [JP, NT, C]) for u in range(2)]
    xhat = [sb(f"xhat{u}", [JP, NT, C]) for u in range(2)] if layer == 0 else raw
    stats = sb("stats", [JP, NT, 6])
    mv = sb("mv", [JP, NT, 2])
    ve = sb("ve", [JP, NT])
    rstd = sb("rstd", [JP, NT])
    ctxT = sb("ctxT", [C, J])
    k_hi = sb("k_hi", [C, J], F32R)
    k_lo = sb("k_lo", [C, J], F32R)
    k_op = [sb(f"k_op{u}", [KROWS, G, J], F32R) for u in range(2)]
    v_op = [sb(f"v_op{u}", [JP, NT, VW]) for u in range(2)]
    q_blk = [sb(f"q_blk{u}", [C, H, T], F32R) for u in range(2)]
    q_op = [sb(f"q_op{u}", [KROWS, G, GH, T], F32R) for u in range(2)]
    part_max = sb("part_max", [128, SM, 3])
    negmax = sb("negmax", [128, SM])
    probs = [sb(f"probs{u}", [JP, HT]) for u in range(2)]
    wk, wv = s[f"wk{layer}"], s[f"wv{layer}"]
    k_bias = s["kv_bias"][:, 0:1] if layer == 0 else s["cols"][:, BK:BK + 1]

    CREDIT = {"scored": 1, "exped": 2, "summed": 2, "sums_read": 1, "transposed": 2, "v_read": 1,
              "copied": 16, "max_scored": 1, "normed": 1, "stats_read": 0}
    names = ["loaded0", "loaded1", "stat", "aggr", "ve_done", "rstd_done", "centred", "normed", "transposed", "ctxT_done",
             "k_projected", "k_hi_done", "k_lo_done", "copied", "q_blk_done", "q_op_done", "max_scored",
             "max_done", "negmax_done", "max_turned", "max_rows", "v_projected", "v_read", "scored", "exped", "summed",
             "sums_read", "ones_done", "gates"]
    m = own.enter_context(semaphores(nc, f"c{layer}_", names))
    CPY = 3 * G * 16

    def loaded(q, u):
        return m[f"loaded{u}"], 8 * (q - u) + 16

    source_ready = (lambda q, u: (m["normed"], q + 1 + CREDIT["normed"])) if layer == 0 else \
                   loaded
    ctx_rows = ctx.rearrange("b (p n) d -> p b (n d)", p=JP)
    AHEAD = 3 if layer == 0 else 2

    def load(sp, q, u):
        sp.dma_start(raw[u][:, :, :].rearrange("p n d -> p (n d)").unsqueeze(1),
                     ctx_rows[:, bass.ds(q, 1), :]).then_inc(m[f"loaded{u}"], 16)

    def load_ahead(sp, b, u):
        if layer == 0:
            sp.wait_ge(m["normed"], b + 2 + CREDIT["normed"])
        else:
            sp.wait_ge(m["transposed"], 3 * (b + 1) + CREDIT["transposed"])
        load(sp, b + AHEAD, (u + AHEAD) % 2)

    def copy_keys(sp, q, u, first):
        sp.wait_ge(m["k_hi_done"], 3 * (q + 1))
        sp.wait_ge(m["k_lo_done"], 3 * (q + 1))
        if not first:
            sp.wait_ge(m["scored"], 12 * (q - 1) + CREDIT["scored"])
        for part, src in enumerate((k_hi, k_lo, k_hi)):
            for g in range(G):
                sp.dma_start(k_op[u][32 * part:32 * part + 32, g, :].bitcast(F32),
                             src[32 * g:32 * g + 32, :].bitcast(F32)).then_inc(m["copied"], 16)

    def build_queries(pool, q, u, first):
        if not first:
            pool.wait_ge(m["max_scored"], 3 * SM * (q - 1) + CREDIT["max_scored"])
        qT = s["qT_all"][:, bass.ds(q * T, T)]
        nc.gpsimd.tensor_tensor(q_blk[u][:, :, :], qT.unsqueeze(1).to_broadcast([C, H, T]),
                                s["head_mask"][:, :].unsqueeze(2).to_broadcast([C, H, T]), ALU.mult
                                ).then_inc(m["q_blk_done"], 1)
        if not first:
            pool.wait_ge(m["scored"], 12 * (q - 1) + CREDIT["scored"])
        for g in range(G):
            parts = s["q_parts"][:, g, bass.ds(q * T, T)]
            nc.gpsimd.tensor_tensor(q_op[u][0:96, g, :, :], parts.unsqueeze(1).to_broadcast([96, GH, T]),
                                    s["quad_mask"][0:96, :].unsqueeze(2).to_broadcast([96, GH, T]),
                                    ALU.mult).then_inc(m["q_op_done"], 1)

    def normalise(pool, q, u, first):
        pool.wait_ge(m["ve_done"], q + 1)
        nc.gpsimd.tensor_tensor(rstd[:, :], ve[:, :], s["minus_half"][0:JP, :], ALU.pow
                                ).then_inc(m["rstd_done"], 1)
        if not first:
            pool.wait_ge(m["transposed"], 3 * (q - 1) + CREDIT["transposed"])
        nc.gpsimd.tensor_tensor(xhat[u][:, :, :], raw[u][:, :, :],
                                mv[:, :, 0:1].to_broadcast([JP, NT, C]), ALU.subtract
                                ).then_inc(m["centred"], 1)
        pool.wait_ge(m["centred"], q + 1)
        pool.wait_ge(m["rstd_done"], q + 1)
        nc.gpsimd.tensor_tensor(xhat[u][:, :, :], xhat[u][:, :, :],
                                rstd[:, :].unsqueeze(2).to_broadcast([JP, NT, C]), ALU.mult
                                ).then_inc(m["normed"], 1)

    def row_statistics(dve, q, u, tiles, first):
        if tiles[0] == 0:
            dve.wait_ge(*loaded(q, u))
            if not first:
                dve.wait_ge(m["normed"], q + CREDIT["normed"])
        for n in tiles:
            nc.vector.bn_stats(stats[:, n, :], raw[u][:, n, :]).then_inc(m["stat"], 1)

    def variances(dve, q, tiles):
        if tiles[0] == 0:
            wait_alone(dve, m["gates"], m["stat"], NT * (q + 1))
        for n in tiles:
            nc.vector.bn_aggr(mv[:, n, :], stats[:, n, :]).then_inc(m["aggr"], 1)
        if tiles[-1] == NT - 1:
            dve.wait_ge(m["aggr"], NT * (q + 1))
            nc.vector.tensor_scalar(ve[:, :], mv[:, :, 1], EPS, None, ALU.add).then_inc(m["ve_done"], 1)

    def read_ctxT(dve, q, a):
        dve.wait_ge(m["transposed"], 3 * q + a + 1 + CREDIT["transposed"])
        nc.vector.tensor_copy(ctxT[:, JB * a:JB * a + JB], ps[:, 4 + a, 0:JB]).then_inc(m["ctxT_done"], 1)

    def low_keys(dve, q, a, first):
        if a == 0 and not first:
            dve.wait_ge(m["copied"], CPY * q + CREDIT["copied"])
        dve.wait_ge(m["k_hi_done"], 3 * q + a + 1)
        nc.vector.scalar_tensor_tensor(out=k_lo[:, JB * a:JB * a + JB], in0=ps[:, 4 + a, 0:JB],
                                       scalar=k_bias, in1=k_hi[:, JB * a:JB * a + JB].bitcast(F32),
                                       op0=ALU.add, op1=ALU.subtract).then_inc(m["k_lo_done"], 1)

    def maximum(dve, q, i, first):
        dve.wait_ge(m["max_scored"], 3 * SM * q + i + 1 + CREDIT["max_scored"])
        if i == 0 and not first:
            dve.wait_ge(m["negmax_done"], q)
        nc.vector.tensor_reduce(part_max[:, i // 3, i % 3:i % 3 + 1], ps[:, 4 + i % 3, 0:JB], AX.X, ALU.max
                                ).then_inc(m["max_done"], 1)

    def join_maxima(dve, q, first):
        dve.wait_ge(m["max_done"], 3 * SM * (q + 1))
        if not first:
            dve.wait_ge(m["max_turned"], q)
        nc.vector.tensor_reduce(negmax[:, :], part_max[:, :, :], AX.X, ALU.max, negate=True
                                ).then_inc(m["negmax_done"], 1)

    def maxima_rows(dve, q, u):
        dve.wait_ge(m["max_turned"], q + 1)
        nc.vector.tensor_tensor(q_op[u][96:KROWS, :, :, :].rearrange("p g h t -> p (g h t)").rearrange(
                                    "p (a n) -> p a n", n=128),
                                ps[0:SM, 7, 0:128].unsqueeze(1).to_broadcast([SM, SM, 128]),
                                s["ident"][0:SM, 0:SM].unsqueeze(2).to_broadcast([SM, SM, 128]),
                                ALU.mult).then_inc(m["max_rows"], 1)

    def read_sums(dve, b):
        dve.wait_ge(m["summed"], NT * (b + 1) + CREDIT["summed"])
        nc.vector.tensor_copy(s["oT_all"][:, :, bass.ds(b * T, T)],
                              ps[:, 7, 0:GT].rearrange("p (k t) -> p k t", t=T)).then_inc(m["sums_read"], 1)

    def exponential(act, b, u, n):
        act.wait_ge(m["scored"], NT * b + n + 1 + CREDIT["scored"])
        act.wait_ge(m["summed"], NT * b + n - 1 + CREDIT["summed"])
        k = n % 2
        nc.scalar.activation(probs[k][:, :].rearrange("p (a n) -> p a n", a=2),
                             ps[0:JP, 2 * k:2 * k + 2, 0:2 * GT], ACT.Exp).then_inc(m["exped"], 1)

    def high_keys(act, q, a, first):
        act.wait_ge(m["k_projected"], 3 * q + a + 1)
        if a == 0 and not first:
            act.wait_ge(m["copied"], CPY * q + CREDIT["copied"])
        nc.scalar.activation(k_hi[:, JB * a:JB * a + JB], ps[:, 4 + a, 0:JB], ACT.Identity, bias=k_bias
                             ).then_inc(m["k_hi_done"], 1)

    def read_values(act, q, u, a):
        act.wait_ge(m["v_projected"], 3 * q + a + 1)
        nc.scalar.activation(v_op[u][:, 4 * a:4 * a + 4, 0:H * VH].rearrange(
                                 "p n (h e) -> p n h e", e=VH)[:, :, :, 0:D],
                             ps[0:JP, 4 + a, :].rearrange("p (b h d) -> p b h d", b=4, d=D), ACT.Copy
                             ).then_inc(m["v_read"], 1)

    def transpose_ctx(pe, q, u, first):
        pe.wait_ge(*source_ready(q, u))
        for a in range(3):
            if not first:
                pe.wait_ge(m["v_read"], 3 * (q - 1) + a + 1 + CREDIT["v_read"])
            for n in range(4 * a, 4 * a + 4):
                mm = nc.tensor.transpose(ps[:, 4 + a, JP * (n % 4):JP * (n % 4) + JP], xhat[u][:, n, :],
                                         s["ident"][0:JP, 0:JP])
            mm.then_inc(m["transposed"], 1)

    def project_keys(pe, q, a):
        pe.wait_ge(m["ctxT_done"], 3 * q + a + 1)
        nc.tensor.matmul(ps[:, 4 + a, 0:JB], wk[:, :], ctxT[:, JB * a:JB * a + JB],
                         start=True, stop=True).then_inc(m["k_projected"], 1)

    def score_for_max(pe, q, u, i):
        t, a = i // 3, i % 3
        if t == 0:
            pe.wait_ge(m["k_lo_done"], 3 * q + a + 1)
            if a == 0:
                pe.wait_ge(m["q_blk_done"], q + 1)
        else:
            pe.wait_ge(m["max_done"], 3 * SM * q + i - 2)
        rows = q_blk[u][:, :, :].rearrange("p h t -> p (h t)")[:, 128 * t:128 * t + 128]
        nc.tensor.matmul(ps[:, 4 + a, 0:JB], rows, k_hi[:, JB * a:JB * a + JB], start=True, stop=True
                         ).then_inc(m["max_scored"], 1)

    def turn_maxima(pe, q, b):
        pe.wait_ge(m["negmax_done"], q + 1)
        if b is not None:
            pe.wait_ge(m["sums_read"], b + 1 + CREDIT["sums_read"])
        nc.tensor.transpose(ps[0:SM, 7, 0:128], negmax[:, :], s["ident"][:, :]).then_inc(m["max_turned"], 1)

    def project_values(pe, q, a):
        pe.wait_ge(m["max_done"], 3 * SM * (q + 1) - 2 + a)
        for n in range(4 * a, 4 * a + 4):
            mm = nc.tensor.matmul(ps[0:JP, 4 + a, C * (n % 4):C * (n % 4) + C],
                                  ctxT[:, JP * n:JP * n + JP], wv[:, :], start=True, stop=True)
        mm.then_inc(m["v_projected"], 1)

    def score(pe, b, u, n):
        if n == 0:
            pe.wait_ge(m["copied"], CPY * (b + 1) + CREDIT["copied"])
            pe.wait_ge(m["q_op_done"], G * (b + 1))
            pe.wait_ge(m["max_rows"], b + 1)
        pe.wait_ge(m["exped"], NT * b + n - 1 + CREDIT["exped"])
        for g in range(G):
            mm = nc.tensor.matmul(ps[0:JP, 2 * (n % 2) + g // 2, GT * (g % 2):GT * (g % 2) + GT],
                                  k_op[u][:, g, JP * n:JP * n + JP],
                                  q_op[u][:, g, :, :].rearrange("p h t -> p (h t)"), start=True, stop=True)
        mm.then_inc(m["scored"], 1)

    def weighted_sum(pe, b, u, n):
        if n == 0:
            pe.wait_ge(m["v_read"], 3 * (b + 1) + CREDIT["v_read"])
            pe.wait_ge(m["sums_read"], b + CREDIT["sums_read"])
            pe.wait_ge(m["max_rows"], b + 1)
        pe.wait_ge(m["exped"], NT * b + n + 1 + CREDIT["exped"])
        for c0, c1, v0 in ((0, 3 * T, 0), (3 * T, 4 * T, 3 * VH)):
            for g in range(G):
                mm = nc.tensor.matmul(ps[32 * g:32 * g + 32, 7, c0:c1],
                                      v_op[u][:, n, GH * VH * g + v0:GH * VH * g + v0 + 32],
                                      probs[n % 2][:, GT * g + c0:GT * g + c1],
                                      start=(n == 0 and c0 == 0), stop=(n == NT - 1), skip_group_check=True)
        mm.then_inc(m["summed"], 1)

    T_SLOT, S_SLOT = 0, 3
    K_SLOTS = [[], [0, 1], [2]]
    HIGH_SLOTS = [[], [0, 1], [2]]
    STATISTICS = {"ctxT": range(0, 6), "k_lo 1": range(6, 9), "maximum 2": range(9, 11),
                  "maximum 4": range(11, 12)}
    VARIANCES = {6: range(0, 4), 8: range(4, 8), 10: range(8, 12)}
    S_COUNT = [3, 2, 3, 2, 3, 2, 2, 2, 2]
    assert sum(S_COUNT) == 3 * SM and S_SLOT + len(S_COUNT) == NT

    def tensor_step(pe, b, u, prepare):
        i = 0
        for n in range(NT):
            score(pe, b, u, n)
            if prepare and n == T_SLOT:
                transpose_ctx(pe, b + 1, 1 - u, False)
            if prepare and n < len(K_SLOTS):
                for a in K_SLOTS[n]:
                    project_keys(pe, b + 1, a)
            if prepare and n >= S_SLOT:
                for _ in range(S_COUNT[n - S_SLOT]):
                    score_for_max(pe, b + 1, 1 - u, i)
                    i += 1
            if n >= 1:
                weighted_sum(pe, b, u, n - 1)
        weighted_sum(pe, b, u, NT - 1)
        if prepare:
            project_values(pe, b + 1, 0)
            turn_maxima(pe, b + 1, b)
            project_values(pe, b + 1, 1)
            project_values(pe, b + 1, 2)

    def scalar_step(act, b, u, prepare):
        for n in range(NT):
            exponential(act, b, u, n)
            if prepare and n < len(HIGH_SLOTS):
                for a in HIGH_SLOTS[n]:
                    high_keys(act, b + 1, a, False)
        if prepare:
            for a in range(3):
                read_values(act, b + 1, 1 - u, a)

    def vector_step(dve, b, u, prepare, ahead):
        ahead = ahead and layer == 0

        def row_statistics_ahead(after):
            if ahead:
                row_statistics(dve, b + 2, u, STATISTICS[after], False)

        if prepare:
            for a in range(3):
                read_ctxT(dve, b + 1, a)
        row_statistics_ahead("ctxT")
        for a in range(3):
            if prepare:
                low_keys(dve, b + 1, a, False)
            if a == 1:
                row_statistics_ahead("k_lo 1")
        if prepare:
            for i in range(3 * SM):
                maximum(dve, b + 1, i, False)
                if ahead and i in VARIANCES:
                    variances(dve, b + 2, VARIANCES[i])
                if i == 2:
                    row_statistics_ahead("maximum 2")
                if i == 4:
                    row_statistics_ahead("maximum 4")
            join_maxima(dve, b + 1, False)
        read_sums(dve, b)
        if prepare:
            maxima_rows(dve, b + 1, 1 - u)

    def gpsimd_step(pool, b, u, prepare, ahead):
        if prepare:
            build_queries(pool, b + 1, 1 - u, False)
        if layer == 0 and ahead:
            normalise(pool, b + 2, u, False)

    def sync_step(sp, b, u, prepare, load_next):
        if load_next:
            load_ahead(sp, b, u)
        if prepare:
            copy_keys(sp, b + 1, 1 - u, False)

    LOOPED = B - 4
    TAIL = range(LOOPED, B)

    with nc.Block() as block:
        @block.gpsimd
        def _(pool):
            for name, credit in CREDIT.items():
                if credit:
                    pool.sem_inc(m[name], credit)

        @block.vector
        def _(dve):
            for u in range(2):
                nc.vector.memset(k_op[u][96:KROWS, :, :].bitcast(F32), 1.0).then_inc(m["ones_done"], 1)
                nc.vector.memset(v_op[u][:, :, :], 1.0).then_inc(m["ones_done"], 1)

    with nc.Block() as block:
        @block.sync
        def _(sp):
            load(sp, 0, 0)
            load(sp, 1, 1)
            if layer == 0:
                sp.wait_ge(m["normed"], 1 + CREDIT["normed"])
                load(sp, 2, 0)
            copy_keys(sp, 0, 0, True)
            with sp.Fori(0, LOOPED, 2) as b:
                for u in range(2):
                    sync_step(sp, b + u, u, True, True)
            for b in TAIL:
                sync_step(sp, b, b % 2, b + 1 < B, b + AHEAD < B)

        @block.gpsimd
        def _(pool):
            build_queries(pool, 0, 0, True)
            if layer == 0:
                normalise(pool, 0, 0, True)
                normalise(pool, 1, 1, True)
            with pool.Fori(0, LOOPED, 2) as b:
                for u in range(2):
                    gpsimd_step(pool, b + u, u, True, True)
            for b in TAIL:
                gpsimd_step(pool, b, b % 2, b + 1 < B, b + 2 < B)

        @block.vector
        def _(dve):
            if layer == 0:
                for q in range(2):
                    row_statistics(dve, q, q, range(NT), q == 0)
                    variances(dve, q, range(NT))
            for a in range(3):
                read_ctxT(dve, 0, a)
            for a in range(3):
                low_keys(dve, 0, a, True)
            for i in range(3 * SM):
                maximum(dve, 0, i, True)
            join_maxima(dve, 0, True)
            maxima_rows(dve, 0, 0)
            with dve.Fori(0, LOOPED, 2) as b:
                for u in range(2):
                    vector_step(dve, b + u, u, True, True)
            for b in TAIL:
                vector_step(dve, b, b % 2, b + 1 < B, b + 2 < B)

        @block.scalar
        def _(act):
            for a in range(3):
                high_keys(act, 0, a, True)
            for a in range(3):
                read_values(act, 0, 0, a)
            with act.Fori(0, LOOPED, 2) as b:
                for u in range(2):
                    scalar_step(act, b + u, u, True)
            for b in TAIL:
                scalar_step(act, b, b % 2, b + 1 < B)

        @block.tensor
        def _(pe):
            transpose_ctx(pe, 0, 0, True)
            for a in range(3):
                project_keys(pe, 0, a)
            for i in range(3 * SM):
                score_for_max(pe, 0, 0, i)
            turn_maxima(pe, 0, None)
            for a in range(3):
                project_values(pe, 0, a)
            with pe.Fori(0, LOOPED, 2) as b:
                for u in range(2):
                    tensor_step(pe, b + u, u, True)
            for b in TAIL:
                tensor_step(pe, b, b % 2, b + 1 < B)


def after_cross(nc, s, own, ps, layer, out):
    def sb(name, shape, dt=F32):
        return own.enter_context(nc.sbuf_tensor(f"p{layer}_{name}", shape, dt))

    oT = sb("oT", [128, GH, CT])
    rden = sb("rden", [PT, NP, G, GH])
    ao = sb("ao", [PT, NP, G, GH, D])
    aoT = sb("aoT", [C, CT])
    y = sb("y", [PT, NP, C])
    yT = sb("yT", [C, CT])
    q32 = sb("q32", [96, G, CT])
    stats = sb("stats", [PT, NP, 6])
    mv = sb("mv", [PT, NP, 2])
    ve = sb("ve", [PT, NP])
    rstd = sb("rstd", [PT, NP])
    yhat = sb("yhat", [PT, NP, C])
    yg = sb("yg", [PT, NP, C])
    yb = sb("yb", [PT, NP, C])
    names = ["staged", "turned", "rden_done", "ao_done", "ao_tr", "aoT_done", "proj", "y_done", "y_kept",
             "y_tr", "yT_done", "qp", "q_store", "q32_done", "q_hi", "q_lo", "st", "ag", "ve_done", "rs",
             "xh", "gained", "offset", "stored", "gates", "sp_gates"]
    m = own.enter_context(semaphores(nc, f"p{layer}_", names))
    wo = s[f"wo{layer}"]
    v_bias = s["kv_bias"][:, 1:2] if layer == 0 else s["cols"][:, BV:BV + 1]
    out_pairs = out.rearrange("b t d -> (b t) d").rearrange("(n p) d -> p n d", p=PT)

    with nc.Fori(0, NC) as c:
        with nc.Block() as block:
            def step(name, per_chunk, k):
                return m[name], c * per_chunk + k

            @block.scalar
            def _(act):
                nc.scalar.activation(oT[:, :, :], s["oT_all"][:, :, bass.ds(c * CT, CT)], ACT.Copy
                                     ).then_inc(m["staged"], 1)
                act.wait_ge(*step("ao_tr", 1, 1))
                nc.scalar.activation(aoT[:, :], ps[:, 4, 0:CT], ACT.Identity, bias=v_bias
                                     ).then_inc(m["aoT_done"], 1)
                if layer == 0:
                    act.wait_ge(*step("y_tr", 1, 1))
                    nc.scalar.activation(yT[:, :], ps[:, 6, 0:CT], ACT.Copy).then_inc(m["yT_done"], 1)
                    q_store_act(nc, act, s, 1, c, ps, q32, 7, range(G), m, step)

            @block.tensor
            def _(pe):
                pe.wait_ge(*step("staged", 1, 1))
                for p in range(NP):
                    for k in range(GH):
                        mm = nc.tensor.transpose(ps[0:PT, p, 128 * k:128 * k + 128],
                                                 oT[:, k, PT * p:PT * p + PT], s["ident"][:, :])
                    mm.then_inc(m["turned"], 1)
                for p in range(NP):
                    pe.wait_ge(*step("ao_done", 2 * NP, 2 * p + 2))
                    mm = nc.tensor.transpose(ps[:, 4, PT * p:PT * p + PT],
                                             ao[:, p, :, :, :].rearrange("p g k d -> p (g k d)"),
                                             s["ident"][0:PT, 0:PT])
                mm.then_inc(m["ao_tr"], 1)
                pe.wait_ge(*step("aoT_done", 1, 1))
                for p in range(NP):
                    mm = nc.tensor.matmul(ps[0:PT, 5, C * p:C * p + C], aoT[:, PT * p:PT * p + PT], wo[:, :],
                                          start=True, stop=True)
                mm.then_inc(m["proj"], 1)
                if layer == 0:
                    pe.wait_ge(*step("y_done", 1, 1))
                    for p in range(NP):
                        mm = nc.tensor.transpose(ps[:, 6, PT * p:PT * p + PT], y[:, p, :], s["ident"][0:PT, 0:PT])
                    mm.then_inc(m["y_tr"], 1)
                    pe.wait_ge(*step("yT_done", 1, 1))
                    q_project_pe(nc, s, 1, ps, yT, 7, range(G), m["qp"])

            @block.vector
            def _(dve):
                for p in range(NP):
                    dve.wait_ge(*step("turned", NP, p + 1))
                    low = ps[0:PT, p, 0:3 * (128 + VH)].rearrange("p (k f) -> p k f", k=3)[:, :, 0:128].rearrange(
                        "p k (g r) -> p k g r", g=G)
                    top = ps[0:PT, p, 3 * 128:4 * 128].rearrange("p (g r) -> p g r", g=G)
                    nc.vector.reciprocal(rden[:, p, :, 0:3].rearrange("p g k -> p k g"), low[:, :, :, D]
                                         ).then_inc(m["rden_done"], 1)
                    nc.vector.reciprocal(rden[:, p, :, 3], top[:, :, D]).then_inc(m["rden_done"], 1)
                    dve.wait_ge(*step("rden_done", 2 * NP, 2 * p + 2))
                    nc.vector.tensor_tensor(ao[:, p, :, 0:3, :].rearrange("p g k d -> p k g d"),
                                            low[:, :, :, 0:D],
                                            rden[:, p, :, 0:3].rearrange("p g k -> p k g").unsqueeze(3).to_broadcast(
                                                [PT, 3, G, D]), ALU.mult).then_inc(m["ao_done"], 1)
                    nc.vector.tensor_tensor(ao[:, p, :, 3, :], top[:, :, 0:D],
                                            rden[:, p, :, 3].unsqueeze(2).to_broadcast([PT, G, D]), ALU.mult
                                            ).then_inc(m["ao_done"], 1)
                dve.wait_ge(*step("proj", 1, 1))
                nc.vector.tensor_tensor(y[:, :, :], ps[0:PT, 5, :].rearrange("p (a n) -> p a n", n=C),
                                        s["resid"][:, bass.ds(c * NP, NP), :], ALU.add).then_inc(m["y_done"], 1)
                if layer == 0:
                    q_low_dve(nc, dve, s, c, q32, m, step)
                    return
                dve.wait_ge(*step("y_done", 1, 1))
                for p in range(NP):
                    nc.vector.bn_stats(stats[:, p, :], y[:, p, :]).then_inc(m["st"], 1)
                wait_alone(dve, m["gates"], *step("st", NP, NP))
                for p in range(NP):
                    nc.vector.bn_aggr(mv[:, p, :], stats[:, p, :]).then_inc(m["ag"], 1)
                dve.wait_ge(*step("ag", NP, NP))
                nc.vector.tensor_scalar(ve[:, :], mv[:, :, 1], EPS, None, ALU.add).then_inc(m["ve_done"], 1)
                dve.wait_ge(*step("rs", 1, 1))
                for p in range(NP):
                    nc.vector.tensor_scalar(yhat[:, p, :], y[:, p, :], mv[:, p, 0:1], rstd[:, p:p + 1],
                                            ALU.subtract, ALU.mult).then_inc(m["xh"], 1)
                dve.wait_ge(*step("xh", NP, NP))
                nc.vector.tensor_tensor(yg[:, :, :], yhat[:, :, :],
                                        s["rows"][:, LN_G, :].unsqueeze(1).to_broadcast([PT, NP, C]), ALU.mult
                                        ).then_inc(m["gained"], 1)
                dve.wait_ge(*step("gained", 1, 1))
                nc.vector.tensor_tensor(yb[:, :, :], yg[:, :, :],
                                        s["rows"][:, LN_B, :].unsqueeze(1).to_broadcast([PT, NP, C]), ALU.add
                                        ).then_inc(m["offset"], 1)

            @block.gpsimd
            def _(pool):
                if layer == 0:
                    pool.wait_ge(*step("y_done", 1, 1))
                    nc.gpsimd.tensor_tensor(s["resid"][:, bass.ds(c * NP, NP), :], y[:, :, :],
                                            s["rows"][:, BO, :].unsqueeze(1).to_broadcast([PT, NP, C]), ALU.add
                                            ).then_inc(m["y_kept"], 1)
                else:
                    pool.wait_ge(*step("ve_done", 1, 1))
                    nc.gpsimd.tensor_tensor(rstd[:, :], ve[:, :], s["minus_half"][0:PT, 0:NP], ALU.pow
                                            ).then_inc(m["rs"], 1)

            @block.sync
            def _(sp):
                if layer == 1:
                    sp.wait_ge(*step("offset", 1, 1))
                    sp.dma_start(out_pairs[:, bass.ds(c * NP, NP), :], yb[:, :, :]).then_inc(m["stored"], 16)
                    wait_alone(sp, m["sp_gates"], *step("stored", 16, 16))


def kernel(**inputs):
    import numpy as _np
    import concourse.bacc as _bacc
    from concourse import mybir as _mybir
    from concourse.bass_utils import run_bass_kernel_spmd as _run

    nc = _bacc.Bacc("TRN2", target_bir_lowering=False, num_devices=1)
    arrays, args = {}, {}
    for name, value in inputs.items():
        a = _np.ascontiguousarray(value)
        arrays[f"in_{name}_dram"] = a
        args[name] = nc.dram_tensor(f"in_{name}_dram", a.shape, _mybir.dt.from_np(a.dtype),
                                    kind="ExternalInput").ap()
    y = nc.dram_tensor("out_0_dram", (B, T, C), F32, kind="ExternalOutput").ap()
    build(nc, args.pop("x"), args.pop("ctx_1024"), args.pop("mask_BxS_bf0"), args, y)
    r = _run(nc, [arrays], core_ids=[0])
    return r.results[0]["out_0_dram"]
```

```python
from contextlib import ExitStack, contextmanager

import concourse.bass as bass
from concourse import mybir
from concourse.alu_op_type import AluOpType as ALU

F32 = mybir.dt.float32
F32R = mybir.dt.float32r
U8 = mybir.dt.uint8
ACT = mybir.ActivationFunctionType
AX = mybir.AxisListType

B, T, J, C, H = 32, 56, 1500, 128, 16
D = C // H
FF = 4 * C
GH = 4
G = H // GH
HT = H * T
GT = GH * T
NT = 12
JP = J // NT
JB = J // 3
SM = HT // 128
KROWS = 96 + SM
VH = D + 1
VW = 168
TOK = B * T
PT = 2 * T
NP = B // 2
NU = 8
UT = TOK // NU
UP = UT // PT
UB = B // NU
EPS = 1e-5
MASKED = -1e30


def build(nc, x, ctx, mask, w, out):
    with ExitStack() as stack:
        def sb(name, shape, dt=F32):
            return stack.enter_context(nc.sbuf_tensor(name, shape, dt))

        s = {
            "ident": sb("ident", [128, 128]),
            "head_mask": sb("head_mask", [128, H]),
            "quad_mask": sb("quad_mask", [128, GH]),
            "minus_half": sb("minus_half", [128, NT]),
            "zero_cols": sb("zero_cols", [128, 1]),
            "rows": sb("rows", [PT, 6, C]),
            "cols": sb("cols", [C, 9]),
            "bq_scaled": sb("bq_scaled", [C, 1]),
            "kv_bias": sb("kv_bias", [C, 2]),
            "resid": sb("resid", [PT, B // 2, C]),
            "q_hi": sb("q_hi", [C, TOK], F32R),
            "q_parts": sb("q_parts", [96, G, TOK]),
            "oT_all": sb("oT_all", [128, GH, TOK]),
        }
        s["q_lo"] = s["oT_all"][:, GH - 1, :]
        s["wq1"] = sb("wq1", [C, C])
        for layer in (0, 1):
            s[f"wk{layer}"] = sb(f"wk{layer}", [C, C])
            s[f"wv{layer}"] = sb(f"wv{layer}", [C, C])
            s[f"wo{layer}"] = sb(f"wo{layer}", [C, C])
        ps = stack.enter_context(nc.psum_tensor("ps", [128, 8, 512], F32))

        with ExitStack() as own:
            for name, shape in (("wqkv", [C, 3 * C]), ("wproj", [C, C]), ("wproj_heads", [C, GH, C]), ("w1", [C, FF]), ("w2", [C, 4, C]),
                                ("ed_wkv", [C, 2 * C]), ("b1_cols", [C, 4]), ("causal", [128, T]),
                                ("causal_low", [128, T]), ("wq0", [C, C]), ("x_all", [PT, NP, C])):
                s[name] = own.enter_context(nc.sbuf_tensor(name, shape, F32))
            s["pad"] = own.enter_context(nc.sbuf_tensor("pad", [128, NP, T], U8))
            setup(nc, s, own, ps, x, mask, w)
            with ExitStack() as inner:
                inputs = {name: inner.enter_context(nc.sbuf_tensor(name, shape, F32)) for name, shape in (
                    ("a_qT", [C, TOK]), ("a_kT", [C, B, T]), ("a_v", [T, B, C]), ("a_x_b", [PT, NP, C]))}
                with ExitStack() as own:
                    projections_and_ff(nc, s, own, ps, inputs)
                with ExitStack() as own:
                    self_attention(nc, s, own, ps, inputs)
        for layer in (0, 1):
            with ExitStack() as own:
                cross_attention(nc, s, own, ps, ctx, layer)
            with ExitStack() as own:
                after_cross(nc, s, own, ps, layer, out)


@contextmanager
def semaphores(nc, prefix, names):
    m = {n: nc.alloc_semaphore(prefix + n) for n in names}
    yield m
    nc.clear_and_free_semaphores(list(m.values()))
    nc.all_engine_barrier()


def wait_alone(eng, gates, sem, value):
    eng.wait_ge(sem, value)
    eng.sem_inc(gates, 1)


COLS = ["L0_xattn_ln1_g", "L0_xattn_ln1_b", "L0_xattn_ln2_g", "L0_xattn_ln2_b", "L0_xattn_ln3_g",
        "L0_xattn_ln3_b", "L1_xattn_bq", "L1_xattn_bk", "L1_xattn_bv"]
LN1_G, LN1_B, LN2_G, LN2_B, LN3_G, LN3_B, BQ, BK, BV = range(9)
ROWS = ["L0_xattn_sa_bproj", "L0_xattn_ed_bproj", "L0_xattn_ff_b2", "L1_xattn_bo", "L1_xattn_ln_g",
        "L1_xattn_ln_b"]
SA_B, ED_B, FF_B2, BO, LN_G, LN_B = range(6)
SCALE = [C ** -0.5, D ** -0.5]


def setup(nc, s, own, ps, x, mask, w):
    m = own.enter_context(semaphores(nc, "su_", ["loaded", "pad_zeroed", "mask_loaded", "consts", "consts_dve", "bias_ready", "folded"]))
    loaded, consts, consts_dve = m["loaded"], m["consts"], m["consts_dve"]
    bias_ready, folded = m["bias_ready"], m["folded"]
    loads = [
        (s["x_all"][:, :, :], x.rearrange("b t d -> (b t) d").rearrange("(n p) d -> p n d", p=PT)),
        (s["wqkv"][:, :], w["L0_xattn_sa_wqkv"]),
        (s["wproj"][:, :], w["L0_xattn_sa_wproj"]),
        (s["w1"][:, :], w["L0_xattn_ff_w1"]),
        (s["w2"][:, :, :], w["L0_xattn_ff_w2"].rearrange("(k p) n -> p k n", p=C)),
        (s["ed_wkv"][:, :], w["L0_xattn_ed_wkv"]),
        (s["wq0"][:, :], w["L0_xattn_ed_wq"]),
        (s["wo0"][:, :], w["L0_xattn_ed_wproj"]),
        (s["wq1"][:, :], w["L1_xattn_Wq"]),
        (s["wk1"][:, :], w["L1_xattn_Wk"]),
        (s["wv1"][:, :], w["L1_xattn_Wv"]),
        (s["wo1"][:, :], w["L1_xattn_Wo"]),
        (s["b1_cols"][:, :], w["L0_xattn_ff_b1"].rearrange("(k p) -> p k", p=C)),
    ]
    loads += [(s["cols"][:, i:i + 1], w[n].unsqueeze(1)) for i, n in enumerate(COLS)]
    loads += [(s["rows"][:, i, :], w[n].unsqueeze(0).to_broadcast([PT, C])) for i, n in enumerate(ROWS)]

    with nc.Block() as block:
        @block.sync
        def _(sp):
            with nc.allow_non_contiguous_dma("parameters as columns, once"):
                for dst, src in loads[::2]:
                    sp.dma_start(dst, src).then_inc(loaded, 16)
                sp.wait_ge(m["pad_zeroed"], 1)
                for u in range(2):
                    sp.dma_start(s["pad"][64 * u:64 * u + T, :, :],
                                 mask.rearrange("(n u) s -> u n s", u=2)[u:u + 1, :, :].to_broadcast([T, NP, T])
                                 ).then_inc(m["mask_loaded"], 16)
                sp.wait_ge(m["mask_loaded"], 32)

        @block.scalar
        def _(act):
            with nc.allow_non_contiguous_dma("parameters as columns, once"):
                for dst, src in loads[1::2]:
                    act.dma_start(dst, src).then_inc(loaded, 16)

        @block.gpsimd
        def _(pool):
            nc.gpsimd.memset(s["ident"][:, :], 1.0).then_inc(consts, 1)
            nc.gpsimd.memset(s["head_mask"][:, :], 1.0).then_inc(consts, 1)
            nc.gpsimd.memset(s["causal"][:, :], 0.0).then_inc(consts, 1)
            nc.gpsimd.memset(s["causal_low"][:, :], 0.0).then_inc(consts, 1)
            nc.gpsimd.memset(s["minus_half"][:, :], -0.5).then_inc(consts, 1)
            nc.gpsimd.memset(s["zero_cols"][:, :], 0.0).then_inc(consts, 1)
            pool.wait_ge(consts, 6)
            nc.gpsimd.affine_select(out=s["ident"][:, :], in_=s["ident"][:, :], compare_op=ALU.is_equal,
                                    fill=0.0, base=0, pattern=[[-1, 128]], channel_multiplier=1
                                    ).then_inc(consts, 1)
            nc.gpsimd.affine_select(out=s["head_mask"][:, :], in_=s["head_mask"][:, :],
                                    compare_op=ALU.is_ge, fill=0.0, base=0, pattern=[[-D, H]],
                                    channel_multiplier=1).then_inc(consts, 1)
            pool.wait_ge(consts, 8)
            nc.gpsimd.affine_select(out=s["head_mask"][:, :], in_=s["head_mask"][:, :],
                                    compare_op=ALU.is_ge, fill=0.0, base=D - 1, pattern=[[D, H]],
                                    channel_multiplier=-1).then_inc(consts, 1)
            nc.gpsimd.affine_select(out=s["causal"][:, :], in_=s["causal"][:, :], compare_op=ALU.is_ge,
                                    fill=MASKED, base=0, pattern=[[-1, T]], channel_multiplier=1
                                    ).then_inc(consts, 1)
            nc.gpsimd.affine_select(out=s["causal_low"][:, :], in_=s["causal_low"][:, :],
                                    compare_op=ALU.is_ge, fill=MASKED, base=-64, pattern=[[-1, T]],
                                    channel_multiplier=1).then_inc(consts, 1)

        @block.tensor
        def _(pe):
            pe.wait_ge(loaded, 16 * len(loads))
            nc.tensor.matmul(ps[:, 0, 0:1], s["ed_wkv"][:, 0:C], s["cols"][:, LN2_B:LN2_B + 1],
                             start=True, stop=True)
            nc.tensor.matmul(ps[:, 0, 1:2], s["ed_wkv"][:, C:2 * C], s["cols"][:, LN2_B:LN2_B + 1],
                             start=True, stop=True).then_inc(bias_ready, 1)

        @block.vector
        def _(dve):
            nc.vector.memset(s["pad"][:, :, :], 0).then_inc(m["pad_zeroed"], 1)
            dve.wait_ge(consts, 11)
            nc.vector.tensor_reduce(s["quad_mask"][:, :],
                                    s["head_mask"][:, :].rearrange("p (g a) -> p a g", a=GH),
                                    AX.X, ALU.add).then_inc(consts_dve, 1)
            nc.vector.tensor_copy(s["causal"][64:128, :], s["causal_low"][64:128, :]).then_inc(consts_dve, 1)
            dve.wait_ge(consts_dve, 1)
            dve.wait_ge(loaded, 16 * len(loads))
            for k in range(GH):
                nc.vector.tensor_scalar(s["wproj_heads"][:, k, :], s["wproj"][:, :], s["quad_mask"][:, k:k + 1], None,
                                        ALU.mult).then_inc(folded, 1)
            nc.vector.tensor_tensor(s["rows"][:, FF_B2, :], s["rows"][:, FF_B2, :], s["rows"][:, ED_B, :],
                                    ALU.add).then_inc(folded, 1)
            g2 = s["cols"][:, LN2_G:LN2_G + 1]
            nc.vector.tensor_scalar(s["wk0"][:, :], s["ed_wkv"][:, 0:C], g2, None, ALU.mult).then_inc(folded, 1)
            nc.vector.tensor_scalar(s["wv0"][:, :], s["ed_wkv"][:, C:2 * C], g2, None, ALU.mult).then_inc(folded, 1)
            nc.vector.tensor_scalar(s["bq_scaled"][:, :], s["cols"][:, BQ:BQ + 1], SCALE[1], None,
                                    ALU.mult).then_inc(folded, 1)
            dve.wait_ge(bias_ready, 1)
            nc.vector.tensor_copy(s["kv_bias"][:, :], ps[:, 0, 0:2]).then_inc(folded, 1)


def queries(layer, s):
    if layer == 0:
        return s["wq0"], SCALE[0], s["zero_cols"][:, 0:1]
    return s["wq1"], SCALE[1], s["bq_scaled"][:, :]


class Counts:
    def __init__(self, m, per):
        self.m, self.per = m, per

    def __getitem__(self, name):
        return self.m[name]

    def done(self, name, item):
        return self.m[name], (item + 3) * self.per[name]

    def part(self, name, item, k):
        return self.m[name], (item + 2) * self.per[name] + k

    def give_credit(self, nc):
        with nc.Block() as block:
            @block.gpsimd
            def _(pool):
                for name, per in self.per.items():
                    pool.sem_inc(self.m[name], 2 * per)


def projections_and_ff(nc, s, own, ps, inputs):
    def two(name, shape):
        return [own.enter_context(nc.sbuf_tensor(f"f_{name}{u}", shape, F32)) for u in range(2)]

    stats, mv, ve, rstd = two("stats", [PT, UP, 6]), two("mv", [PT, UP, 2]), two("ve", [PT, UP]), two("rstd", [PT, UP])
    xhat, h1T, h3T = two("xhat", [PT, UP, C]), two("h1T", [C, UT]), two("h3T", [C, UT])
    hidT = two("hidT", [C, 4, UT])
    x_all, x_b = s["x_all"], inputs["a_x_b"]
    per = {"stat": UP, "aggr": UP, "ve_done": 1, "rstd_done": 1, "xhat_done": UP, "transposed": 1, "h1": 1,
           "h3": 1, "k_proj": 1, "q_proj": 1, "v_proj": 1, "kT": 1, "qT": 1, "v": 1, "hidden": 2, "relu": 4,
           "ff_proj": 1, "ff": 1, "gates": 1, "x_b": 1}
    m = Counts(own.enter_context(semaphores(nc, "f_", list(per))), per)
    m.give_credit(nc)

    def statistics(dve, n, u):
        dve.wait_ge(*m.done("xhat_done", n - 2))
        for p in range(UP):
            nc.vector.bn_stats(stats[u][:, p, :], 
                               x_all[:, bass.ds(n * UP + p, 1), :].rearrange("p a n -> p (a n)")
                               ).then_inc(m["stat"], 1)
        wait_alone(dve, m["gates"], *m.done("stat", n))
        for p in range(UP):
            nc.vector.bn_aggr(mv[u][:, p, :], stats[u][:, p, :]).then_inc(m["aggr"], 1)
        dve.wait_ge(*m.done("aggr", n))
        nc.vector.tensor_scalar(ve[u][:, :], mv[u][:, :, 1], EPS, None, ALU.add).then_inc(m["ve_done"], 1)

    def normalise(dve, n, u):
        dve.wait_ge(*m.done("rstd_done", n))
        dve.wait_ge(*m.done("transposed", n - 2))
        for p in range(UP):
            nc.vector.tensor_scalar(xhat[u][:, p, :], x_all[:, bass.ds(n * UP + p, 1), :].rearrange("p a n -> p (a n)"),
                                    mv[u][:, p, 0:1], rstd[u][:, p:p + 1], ALU.subtract, ALU.mult
                                    ).then_inc(m["xhat_done"], 1)

    def gain_for_ff(dve, n, u):
        dve.wait_ge(*m.done("h1", n))
        dve.wait_ge(*m.done("hidden", n - 2))
        nc.vector.tensor_scalar(h3T[u][:, :], ps[:, 0, 0:UT], s["cols"][:, LN3_G:LN3_G + 1],
                                s["cols"][:, LN3_B:LN3_B + 1], ALU.mult, ALU.add).then_inc(m["h3"], 1)

    def read_keys(dve, n):
        dve.wait_ge(*m.done("k_proj", n))
        nc.vector.tensor_copy(inputs["a_kT"][:, bass.ds(n * UB, UB), :],
                              ps[:, 1, 0:UT].rearrange("p (b t) -> p b t", t=T)).then_inc(m["kT"], 1)

    def read_values(dve, n):
        dve.wait_ge(*m.done("v_proj", n))
        nc.vector.tensor_copy(inputs["a_v"][:, bass.ds(n * UB, UB), :],
                              ps[0:T, 3, :].rearrange("p (b n) -> p b n", n=C)).then_inc(m["v"], 1)

    def read_ff(dve, n):
        dve.wait_ge(*m.done("ff_proj", n))
        nc.vector.tensor_tensor(s["resid"][:, bass.ds(n * UP, UP), :],
                                ps[0:PT, 6, 0:UP * C].rearrange("p (a n) -> p a n", n=C),
                                s["rows"][:, FF_B2, :].unsqueeze(1).to_broadcast([PT, UP, C]), ALU.add
                                ).then_inc(m["ff"], 1)

    def reciprocal_deviation(pool, n, u):
        pool.wait_ge(*m.done("ve_done", n))
        pool.wait_ge(*m.done("xhat_done", n - 2))
        nc.gpsimd.tensor_tensor(rstd[u][:, :], ve[u][:, :], s["minus_half"][0:PT, 0:UP], ALU.pow
                                ).then_inc(m["rstd_done"], 1)

    def add_projection_bias(pool, n):
        nc.gpsimd.tensor_tensor(x_b[:, bass.ds(n * UP, UP), :], x_all[:, bass.ds(n * UP, UP), :],
                                s["rows"][:, SA_B, :].unsqueeze(1).to_broadcast([PT, UP, C]), ALU.add
                                ).then_inc(m["x_b"], 1)

    def gain_for_attention(act, n, u):
        act.wait_ge(*m.done("transposed", n))
        act.wait_ge(*m.done("v_proj", n - 2))
        nc.scalar.activation(h1T[u][:, :], ps[:, 0, 0:UT], ACT.Identity, bias=s["cols"][:, LN1_B:LN1_B + 1],
                             scale=s["cols"][:, LN1_G:LN1_G + 1]).then_inc(m["h1"], 1)

    def read_queries(act, n):
        act.wait_ge(*m.done("q_proj", n))
        nc.scalar.activation(inputs["a_qT"][:, bass.ds(n * UT, UT)], ps[:, 2, 0:UT], ACT.Copy, scale=SCALE[0]
                             ).then_inc(m["qT"], 1)

    def relu(act, n, u):
        act.wait_ge(*m.done("ff_proj", n - 2))
        for k in range(4):
            if k % 2 == 0:
                act.wait_ge(*m.part("hidden", n, k // 2 + 1))
            nc.scalar.activation(hidT[u][:, k, :], ps[:, 4 + k // 2, UT * (k % 2):UT * (k % 2) + UT], ACT.Relu,
                                 bias=s["b1_cols"][:, k:k + 1]).then_inc(m["relu"], 1)

    def transpose_xhat(pe, n, u):
        pe.wait_ge(*m.done("xhat_done", n))
        pe.wait_ge(*m.done("h3", n - 1))
        for p in range(UP):
            mm = nc.tensor.transpose(ps[:, 0, PT * p:PT * p + PT], xhat[u][:, p, :], s["ident"][0:PT, 0:PT])
        mm.then_inc(m["transposed"], 1)

    def project_keys_queries(pe, n, u):
        pe.wait_ge(*m.done("h1", n))
        pe.wait_ge(*m.done("kT", n - 1))
        nc.tensor.matmul(ps[:, 1, 0:UT], s["wqkv"][:, C:2 * C], h1T[u][:, :], start=True, stop=True
                         ).then_inc(m["k_proj"], 1)
        pe.wait_ge(*m.done("qT", n - 1))
        nc.tensor.matmul(ps[:, 2, 0:UT], s["wqkv"][:, 0:C], h1T[u][:, :], start=True, stop=True
                         ).then_inc(m["q_proj"], 1)

    def project_values(pe, n, u):
        wait_alone(pe, m["gates"], *m.done("v", n - 1))
        for j in range(UB):
            mm = nc.tensor.matmul(ps[0:T, 3, C * j:C * j + C], h1T[u][:, T * j:T * j + T],
                                  s["wqkv"][:, 2 * C:3 * C], start=True, stop=True)
        mm.then_inc(m["v_proj"], 1)

    def project_hidden(pe, n, u):
        pe.wait_ge(*m.done("h3", n))
        for k in range(4):
            if k % 2 == 0:
                pe.wait_ge(*m.part("relu", n - 1, k + 2))
            mm = nc.tensor.matmul(ps[:, 4 + k // 2, UT * (k % 2):UT * (k % 2) + UT], s["w1"][:, C * k:C * k + C],
                                  h3T[u][:, :], start=True, stop=True)
            if k % 2 == 1:
                mm.then_inc(m["hidden"], 1)

    def project_ff(pe, n, u):
        pe.wait_ge(*m.done("relu", n))
        pe.wait_ge(*m.done("ff", n - 1))
        for p in range(UP):
            for k in range(4):
                mm = nc.tensor.matmul(ps[0:PT, 6, C * p:C * p + C], hidT[u][:, k, PT * p:PT * p + PT],
                                      s["w2"][:, k, :], start=(k == 0), stop=(k == 3))
        mm.then_inc(m["ff_proj"], 1)

    def vector_step(dve, n, u, has):
        if has(1):
            normalise(dve, n + 1, 1 - u)
        if has(2):
            statistics(dve, n + 2, u)
        if has(0):
            read_keys(dve, n)
        if has(1):
            gain_for_ff(dve, n + 1, 1 - u)
        if has(0):
            read_values(dve, n)
            read_ff(dve, n)

    def gpsimd_step(pool, n, u, has):
        if has(2):
            reciprocal_deviation(pool, n + 2, u)
        if has(0):
            add_projection_bias(pool, n)

    def scalar_step(act, n, u, has):
        if has(0):
            read_queries(act, n)
        if has(1):
            gain_for_attention(act, n + 1, 1 - u)
        if has(0):
            relu(act, n, u)

    def tensor_step(pe, n, u, has):
        if has(0):
            project_keys_queries(pe, n, u)
        if has(1):
            transpose_xhat(pe, n + 1, 1 - u)
        if has(0):
            project_hidden(pe, n, u)
            project_values(pe, n, u)
            project_ff(pe, n, u)

    with nc.Block() as block:
        @block.vector
        def _(dve):
            run_steps(dve, vector_step, -2, (0, NU - 4), NU, NU)

        @block.gpsimd
        def _(pool):
            run_steps(pool, gpsimd_step, -2, (0, NU - 4), NU, NU)

        @block.scalar
        def _(act):
            run_steps(act, scalar_step, -2, (0, NU - 4), NU, NU)

        @block.tensor
        def _(pe):
            run_steps(pe, tensor_step, -2, (0, NU - 4), NU, NU)



def run_steps(eng, step, first, looped, end, count):
    for i in range(first, looped[0]):
        step(eng, i, i % 2, lambda k, i=i: 0 <= i + k < count)
    with eng.Fori(looped[0], looped[1], 2) as i:
        for u in range(2):
            step(eng, i + u, u, lambda k: True)
    for i in range(looped[1], end):
        step(eng, i, i % 2, lambda k, i=i: 0 <= i + k < count)


def self_attention(nc, s, own, ps, inputs):
    def two(name, shape):
        return [own.enter_context(nc.sbuf_tensor(f"a_{name}{u}", shape, F32)) for u in range(2)]

    bias = own.enter_context(nc.sbuf_tensor("a_bias", [128, NP, T], F32))
    q_pair, v_pair, kblk = two("q_pair", [C, 2, 64]), two("v_pair", [T, 2, C]), two("kblk", [C, 2, H, T])
    scores, negmax, probs = two("scores", [128, H, T]), two("negmax", [128, H]), two("probs", [128, H, T])
    denom, rden = two("denom", [128, H]), two("rden", [128, H])
    probsT = two("probsT", [T, H, 128])
    wT, r1 = two("wT", [C, GH, 2, T]), two("r1", [PT, C])
    stats, mv, ve, rstd = two("stats", [PT, 6]), two("mv", [PT, 2]), two("ve", [PT, 1]), two("rstd", [PT, 1])
    xhat, h2T, q32 = two("xhat", [PT, C]), two("h2T", [C, PT]), two("q32", [C, PT])
    qT, kT, v_all, x_b = inputs["a_qT"], inputs["a_kT"], inputs["a_v"], inputs["a_x_b"]
    TJ = 4
    TH = H // TJ
    per = {"k_blocked": 2, "q_staged": 1, "v_staged": 1, "scored": 1, "masked": 2, "maximum": 1, "shifted": 1,
           "exped": 1, "denom_done": 1, "rden_done": 1, "p_turned": TJ, "p_read": TJ, "divided": 1, "weighed": 1,
           "weighed_read": 1, "projected": 1, "r1_done": 1, "stat": 1, "aggr": 1, "ve_done": 1,
           "rstd_done": 1, "xhat_done": 1, "transposed": 1, "h2_done": 1, "q_projected": 1, "q32_done": 1,
           "q_hi_done": 1, "q_lo_done": 1, "resid_done": 1, "gates": 1, "pe_gates": 1, "prepared": 1}
    m = Counts(own.enter_context(semaphores(nc, "a_", list(per))), per)
    m.give_credit(nc)

    def block_keys(pool, j, u):
        pool.wait_ge(*m.done("scored", j - 2))
        for w in range(2):
            nc.gpsimd.tensor_tensor(kblk[u][:, w, :, :],
                                    kT[:, bass.ds(2 * j + w, 1), :].to_broadcast([C, H, T]),
                                    s["head_mask"][:, :].unsqueeze(2).to_broadcast([C, H, T]),
                                    ALU.mult).then_inc(m["k_blocked"], 1)

    def divide(pool, j, u):
        pool.wait_ge(*m.done("rden_done", j))
        nc.gpsimd.tensor_tensor(probs[u][:, :, :], probs[u][:, :, :],
                                rden[u][:, :].unsqueeze(2).to_broadcast([128, H, T]), ALU.mult
                                ).then_inc(m["divided"], 1)

    def extend_residual(pool, j, u):
        pool.wait_ge(*m.done("r1_done", j))
        nc.gpsimd.tensor_tensor(s["resid"][:, bass.ds(j, 1), :], s["resid"][:, bass.ds(j, 1), :],
                                r1[u][:, :].unsqueeze(1), ALU.add).then_inc(m["resid_done"], 1)

    def reciprocal_deviation(pool, j, u):
        pool.wait_ge(*m.done("ve_done", j))
        pool.wait_ge(*m.done("xhat_done", j - 2))
        nc.gpsimd.tensor_tensor(rstd[u][:, :], ve[u][:, :], s["minus_half"][0:PT, 0:1], ALU.pow
                                ).then_inc(m["rstd_done"], 1)

    def low_queries(pool, j, u):
        pool.wait_ge(*m.done("q_hi_done", j))
        nc.gpsimd.tensor_tensor(s["q_lo"][:, bass.ds(j * PT, PT)], q32[u][:, :],
                                s["q_hi"][:, bass.ds(j * PT, PT)].bitcast(F32), ALU.subtract
                                ).then_inc(m["q_lo_done"], 1)

    def normalise(dve, j, u):
        dve.wait_ge(*m.done("rstd_done", j))
        dve.wait_ge(*m.done("transposed", j - 2))
        nc.vector.tensor_scalar(xhat[u][:, :], r1[u][:, :], mv[u][:, 0:1], rstd[u][:, 0:1],
                                ALU.subtract, ALU.mult).then_inc(m["xhat_done"], 1)

    def denominators(dve, j, u):
        dve.wait_ge(*m.done("exped", j))
        nc.vector.tensor_reduce(denom[u][:, :], probs[u][:, :, :], AX.X, ALU.add).then_inc(m["denom_done"], 1)
        dve.wait_ge(*m.done("denom_done", j))
        dve.wait_ge(*m.done("divided", j - 2))
        nc.vector.reciprocal(rden[u][:, :], denom[u][:, :]).then_inc(m["rden_done"], 1)

    def mask_and_shift(dve, j, u):
        dve.wait_ge(*m.done("scored", j))
        dve.wait_ge(*m.done("exped", j - 2))
        for half in range(2):
            hs = slice(8 * half, 8 * half + 8)
            nc.vector.tensor_tensor(scores[u][:, hs, :], ps[:, 4 + half, 0:8 * T].rearrange("p (h t) -> p h t", t=T),
                                    bias[:, bass.ds(j, 1), :].to_broadcast([128, 8, T]), ALU.add
                                    ).then_inc(m["masked"], 1)
        dve.wait_ge(*m.done("masked", j))
        nc.vector.tensor_reduce(negmax[u][:, :], scores[u][:, :, :], AX.X, ALU.max, negate=True
                                ).then_inc(m["maximum"], 1)
        dve.wait_ge(*m.done("maximum", j))
        nc.vector.tensor_tensor(scores[u][:, :, :], scores[u][:, :, :],
                                negmax[u][:, :].unsqueeze(2).to_broadcast([128, H, T]), ALU.add
                                ).then_inc(m["shifted"], 1)

    def residual_and_statistics(dve, j, u):
        dve.wait_ge(*m.done("projected", j))
        dve.wait_ge(*m.done("resid_done", j - 2))
        dve.wait_ge(*m.done("xhat_done", j - 2))
        nc.vector.tensor_tensor(r1[u][:, :].unsqueeze(1), ps[0:PT, 7, 0:C].unsqueeze(1),
                                x_b[:, bass.ds(j, 1), :], ALU.add).then_inc(m["r1_done"], 1)
        dve.wait_ge(*m.done("r1_done", j))
        nc.vector.bn_stats(stats[u][:, :], r1[u][:, :]).then_inc(m["stat"], 1)
        wait_alone(dve, m["gates"], *m.done("stat", j))
        nc.vector.bn_aggr(mv[u][:, :], stats[u][:, :]).then_inc(m["aggr"], 1)
        dve.wait_ge(*m.done("aggr", j))
        nc.vector.tensor_scalar(ve[u][:, :], mv[u][:, 1:2], EPS, None, ALU.add).then_inc(m["ve_done"], 1)

    def stage_queries(act, j, u):
        act.wait_ge(*m.done("scored", j - 2))
        nc.scalar.activation(q_pair[u][:, :, 0:T], qT[:, bass.ds(j * PT, PT)].rearrange("p (w t) -> p w t", t=T),
                             ACT.Copy).then_inc(m["q_staged"], 1)

    def stage_values(act, j, u):
        act.wait_ge(*m.done("weighed", j - 2))
        nc.scalar.activation(v_pair[u][:, :, :], v_all[:, bass.ds(2 * j, 2), :], ACT.Copy
                             ).then_inc(m["v_staged"], 1)

    def exponential(act, j, u):
        act.wait_ge(*m.done("shifted", j))
        nc.scalar.activation(probs[u][:, :, :], scores[u][:, :, :], ACT.Exp).then_inc(m["exped"], 1)

    def read_probabilities(act, j, u):
        act.wait_ge(*m.done("weighed", j - 2))
        for k in range(TJ):
            act.wait_ge(*m.part("p_turned", j, k + 1))
            nc.scalar.activation(probsT[u][:, TH * k:TH * k + TH, :].rearrange("p h n -> p (h n)"),
                                 ps[0:T, k % 2, :], ACT.Copy).then_inc(m["p_read"], 1)

    def read_weighed(act, j, u):
        act.wait_ge(*m.done("weighed", j))
        act.wait_ge(*m.done("projected", j - 2))
        nc.scalar.activation(wT[u][:, :, :, :].rearrange("p k w t -> p w k t"),
                             ps[:, 6, :].rearrange("p (w k t) -> p w k t", w=2, k=GH)[:, :, :, 0:T],
                             ACT.Copy).then_inc(m["weighed_read"], 1)

    def gain(act, j, u):
        act.wait_ge(*m.done("transposed", j))
        act.wait_ge(*m.done("q_projected", j - 2))
        nc.scalar.activation(h2T[u][:, :], ps[:, 3, 0:PT], ACT.Identity, bias=s["cols"][:, LN2_B:LN2_B + 1],
                             scale=s["cols"][:, LN2_G:LN2_G + 1]).then_inc(m["h2_done"], 1)

    def high_queries(act, j, u):
        act.wait_ge(*m.done("q_projected", j))
        act.wait_ge(*m.done("q_lo_done", j - 2))
        nc.scalar.activation(q32[u][:, :], ps[:, 2, 0:PT], ACT.Copy, scale=SCALE[0]).then_inc(m["q32_done"], 1)
        act.wait_ge(*m.done("q32_done", j))
        nc.scalar.activation(s["q_hi"][:, bass.ds(j * PT, PT)], q32[u][:, :], ACT.Copy).then_inc(m["q_hi_done"], 1)

    def score(pe, j, u):
        pe.wait_ge(*m.done("k_blocked", j))
        pe.wait_ge(*m.done("q_staged", j))
        wait_alone(pe, m["pe_gates"], *m.done("masked", j - 1))
        for half in range(2):
            for w in range(2):
                mm = nc.tensor.matmul(ps[64 * w:64 * w + 64, 4 + half, 0:8 * T], q_pair[u][:, w, :],
                                      kblk[u][:, w, 8 * half:8 * half + 8, :].rearrange("p h t -> p (h t)"),
                                      start=True, stop=True)
        mm.then_inc(m["scored"], 1)

    def turn_probabilities(pe, j, u):
        pe.wait_ge(*m.done("divided", j))
        for k in range(TJ):
            wait_alone(pe, m["pe_gates"], *(m.part("p_read", j, k - 1) if k >= 2 else
                                            m.part("p_read", j - 1, k + TJ - 1)))
            for h in range(TH * k, TH * k + TH):
                mm = nc.tensor.transpose(ps[0:T, k % 2, 128 * (h % TH):128 * (h % TH) + 128], probs[u][:, h, :],
                                         s["ident"][:, :])
            mm.then_inc(m["p_turned"], 1)

    def project_out(pe, j, u):
        pe.wait_ge(*m.done("weighed_read", j))
        pe.wait_ge(*m.done("r1_done", j - 1))
        for k in range(GH):
            mm = nc.tensor.matmul(ps[0:PT, 7, 0:C], wT[u][:, k, :, :].rearrange("p w t -> p (w t)"),
                                  s["wproj_heads"][:, k, :], start=(k == 0), stop=(k == GH - 1))
        mm.then_inc(m["projected"], 1)

    def transpose_xhat(pe, j, u):
        pe.wait_ge(*m.done("xhat_done", j))
        pe.wait_ge(*m.done("h2_done", j - 1))
        nc.tensor.transpose(ps[:, 3, 0:PT], xhat[u][:, :], s["ident"][0:PT, 0:PT]).then_inc(m["transposed"], 1)

    def weigh_values(pe, j, u):
        pe.wait_ge(*m.done("v_staged", j))
        pe.wait_ge(*m.done("weighed_read", j - 1))
        wait_alone(pe, m["pe_gates"], *m.done("p_read", j))
        for w in range(2):
            for g in range(G):
                mm = nc.tensor.matmul(ps[32 * g:32 * g + 32, 6, 256 * w:256 * w + 256],
                                      v_pair[u][:, w, 32 * g:32 * g + 32],
                                      probsT[u][:, GH * g:GH * g + GH, 64 * w:64 * w + 64], start=True, stop=True)
        mm.then_inc(m["weighed"], 1)

    def project_queries(pe, j, u):
        pe.wait_ge(*m.done("h2_done", j))
        pe.wait_ge(*m.done("q32_done", j - 1))
        nc.tensor.matmul(ps[:, 2, 0:PT], s["wq0"][:, :], h2T[u][:, :], start=True, stop=True
                         ).then_inc(m["q_projected"], 1)

    def gpsimd_step(pool, p, u, has):
        if has(1):
            divide(pool, p + 1, 1 - u)
        if has(3):
            block_keys(pool, p + 3, 1 - u)
        if has(-1):
            extend_residual(pool, p - 1, 1 - u)
            reciprocal_deviation(pool, p - 1, 1 - u)
        if has(-2):
            low_queries(pool, p - 2, u)

    def vector_step(dve, p, u, has):
        if has(-2):
            normalise(dve, p - 2, u)
        if has(1):
            denominators(dve, p + 1, 1 - u)
        if has(-1):
            residual_and_statistics(dve, p - 1, 1 - u)
        if has(2):
            mask_and_shift(dve, p + 2, u)

    def scalar_step(act, p, u, has):
        if has(-1):
            read_weighed(act, p - 1, 1 - u)
        if has(3):
            stage_queries(act, p + 3, 1 - u)
        if has(0):
            read_probabilities(act, p, u)
        if has(1):
            exponential(act, p + 1, 1 - u)
        if has(-2):
            gain(act, p - 2, u)
            high_queries(act, p - 2, u)
        if has(2):
            stage_values(act, p + 2, u)

    def tensor_step(pe, p, u, has):
        if has(0):
            turn_probabilities(pe, p, u)
        if has(-1):
            project_out(pe, p - 1, 1 - u)
        if has(-2):
            transpose_xhat(pe, p - 2, u)
        if has(2):
            score(pe, p + 2, u)
        if has(-2):
            project_queries(pe, p - 2, u)
        if has(0):
            weigh_values(pe, p, u)

    with nc.Block() as block:
        @block.vector
        def _(dve):
            for u in range(2):
                nc.vector.memset(q_pair[u][:, :, :], 0.0).then_inc(m["prepared"], 1)
            nc.vector.scalar_tensor_tensor(out=bias[:, :, :], in0=s["pad"][:, :, :], scalar=MASKED,
                                           in1=s["causal"][:, :].unsqueeze(1).to_broadcast([128, NP, T]),
                                           op0=ALU.mult, op1=ALU.add).then_inc(m["prepared"], 1)

    with nc.Block() as block:
        @block.vector
        def _(dve):
            run_steps(dve, vector_step, -3, (2, NP - 4), NP + 2, NP)

        @block.gpsimd
        def _(pool):
            run_steps(pool, gpsimd_step, -3, (2, NP - 4), NP + 2, NP)

        @block.scalar
        def _(act):
            run_steps(act, scalar_step, -3, (2, NP - 4), NP + 2, NP)

        @block.tensor
        def _(pe):
            run_steps(pe, tensor_step, -3, (2, NP - 4), NP + 2, NP)



def cross_attention(nc, s, own, ps, ctx, layer):
    def sb(name, shape, dt=F32):
        return own.enter_context(nc.sbuf_tensor(f"c{layer}_{name}", shape, dt))

    raw = [sb(f"raw{u}", [JP, NT, C]) for u in range(2)]
    xhat = [sb(f"xhat{u}", [JP, NT, C]) for u in range(2)] if layer == 0 else raw
    stats = sb("stats", [JP, NT, 6])
    mv = sb("mv", [JP, NT, 2])
    ve = sb("ve", [JP, NT])
    rstd = sb("rstd", [JP, NT])
    ctxT = sb("ctxT", [C, J])
    k_hi = sb("k_hi", [C, J], F32R)
    k_lo = sb("k_lo", [C, J], F32R)
    k_op = [sb(f"k_op{u}", [KROWS, G, J], F32R) for u in range(2)]
    v_op = [sb(f"v_op{u}", [JP, NT, VW]) for u in range(2)]
    q_blk = [sb(f"q_blk{u}", [C, H, T], F32R) for u in range(2)]
    q_op = [sb(f"q_op{u}", [KROWS, G, GH, T], F32R) for u in range(2)]
    part_max = sb("part_max", [128, SM, 3])
    negmax = sb("negmax", [128, SM])
    probs = [sb(f"probs{u}", [JP, HT]) for u in range(2)]
    wk, wv = s[f"wk{layer}"], s[f"wv{layer}"]
    k_bias = s["kv_bias"][:, 0:1] if layer == 0 else s["cols"][:, BK:BK + 1]

    CREDIT = {"scored": 1, "exped": 2, "summed": 2, "sums_read": 1, "transposed": 2, "v_read": 1,
              "copied": 16, "max_scored": 1, "normed": 1, "stats_read": 0}
    names = ["loaded0", "loaded1", "stat", "aggr", "ve_done", "rstd_done", "centred", "normed", "transposed", "ctxT_done",
             "k_projected", "k_hi_done", "k_lo_done", "copied", "q_blk_done", "q_op_done", "max_scored",
             "max_done", "negmax_done", "max_turned", "max_rows", "v_projected", "v_read", "scored", "exped", "summed",
             "sums_read", "key_ones", "value_ones", "gates", "q_copied"]
    Q_COPIED = 3 * G * 16
    m = own.enter_context(semaphores(nc, f"c{layer}_", names))
    CPY = 3 * G * 16

    def loaded(q, u):
        return m[f"loaded{u}"], 8 * (q - u) + 16

    source_ready = (lambda q, u: (m["normed"], q + 1 + CREDIT["normed"])) if layer == 0 else \
                   loaded
    ctx_rows = ctx.rearrange("b (p n) d -> p b (n d)", p=JP)
    AHEAD = 3 if layer == 0 else 2

    def load(sp, q, u):
        sp.dma_start(raw[u][:, :, :].rearrange("p n d -> p (n d)").unsqueeze(1),
                     ctx_rows[:, bass.ds(q, 1), :]).then_inc(m[f"loaded{u}"], 16)

    def load_ahead(sp, b, u):
        if layer == 0:
            sp.wait_ge(m["normed"], b + 2 + CREDIT["normed"])
        else:
            sp.wait_ge(m["transposed"], 3 * (b + 1) + CREDIT["transposed"])
        load(sp, b + AHEAD, (u + AHEAD) % 2)

    def copy_keys(sp, q, u, first):
        sp.wait_ge(m["k_hi_done"], 3 * (q + 1))
        sp.wait_ge(m["k_lo_done"], 3 * (q + 1))
        if not first:
            sp.wait_ge(m["scored"], 12 * (q - 1) + CREDIT["scored"])
        for part, src in enumerate((k_hi, k_lo, k_hi)):
            for g in range(G):
                sp.dma_start(k_op[u][32 * part:32 * part + 32, g, :].bitcast(F32),
                             src[32 * g:32 * g + 32, :].bitcast(F32)).then_inc(m["copied"], 16)

    def copy_queries(sp):
        for part, src in enumerate((s["q_hi"], s["q_hi"], s["q_lo"])):
            for g in range(G):
                rows = src[32 * g:32 * g + 32, :]
                sp.dma_start(s["q_parts"][32 * part:32 * part + 32, g, :],
                             rows if part == 2 else rows.bitcast(F32)).then_inc(m["q_copied"], 16)

    def block_queries(pool, q, u, first):
        if not first:
            pool.wait_ge(m["max_scored"], 3 * SM * (q - 1) + CREDIT["max_scored"])
        qT = s["q_hi"][:, bass.ds(q * T, T)].bitcast(F32)
        nc.gpsimd.tensor_tensor(q_blk[u][:, :, :], qT.unsqueeze(1).to_broadcast([C, H, T]),
                                s["head_mask"][:, :].unsqueeze(2).to_broadcast([C, H, T]), ALU.mult
                                ).then_inc(m["q_blk_done"], 1)

    def expand_queries(pool, q, u, first):
        if not first:
            pool.wait_ge(m["scored"], 12 * (q - 1) + CREDIT["scored"])
        else:
            pool.wait_ge(m["q_copied"], Q_COPIED)
        for g in range(G):
            parts = s["q_parts"][:, g, bass.ds(q * T, T)]
            nc.gpsimd.tensor_tensor(q_op[u][0:96, g, :, :], parts.unsqueeze(1).to_broadcast([96, GH, T]),
                                    s["quad_mask"][0:96, :].unsqueeze(2).to_broadcast([96, GH, T]),
                                    ALU.mult).then_inc(m["q_op_done"], 1)

    def ones_of_values(pool, u):
        nc.gpsimd.memset(v_op[u][:, :, :], 1.0).then_inc(m["value_ones"], 1)

    def reciprocal_deviation(pool, q):
        pool.wait_ge(m["ve_done"], q + 1)
        nc.gpsimd.tensor_tensor(rstd[:, :], ve[:, :], s["minus_half"][0:JP, :], ALU.pow
                                ).then_inc(m["rstd_done"], 1)

    def normalise_first(dve):
        dve.wait_ge(m["rstd_done"], 1)
        for n in range(NT):
            xh = nc.vector.tensor_scalar(xhat[0][:, n, :], raw[0][:, n, :], mv[:, n, 0:1], rstd[:, n:n + 1],
                                         ALU.subtract, ALU.mult)
        xh.then_inc(m["normed"], 1)

    def normalise(pool, q, u, first):
        reciprocal_deviation(pool, q)
        if not first:
            pool.wait_ge(m["transposed"], 3 * (q - 1) + CREDIT["transposed"])
        nc.gpsimd.tensor_tensor(xhat[u][:, :, :], raw[u][:, :, :],
                                mv[:, :, 0:1].to_broadcast([JP, NT, C]), ALU.subtract
                                ).then_inc(m["centred"], 1)
        pool.wait_ge(m["centred"], q)
        pool.wait_ge(m["rstd_done"], q + 1)
        nc.gpsimd.tensor_tensor(xhat[u][:, :, :], xhat[u][:, :, :],
                                rstd[:, :].unsqueeze(2).to_broadcast([JP, NT, C]), ALU.mult
                                ).then_inc(m["normed"], 1)

    def row_statistics(dve, q, u, tiles):
        if tiles[0] == 0:
            dve.wait_ge(*loaded(q, u))
        for n in tiles:
            nc.vector.bn_stats(stats[:, n, :], raw[u][:, n, :]).then_inc(m["stat"], 1)

    def variances(dve, q, first):
        if not first:
            dve.wait_ge(m["normed"], q + CREDIT["normed"])
        wait_alone(dve, m["gates"], m["stat"], NT * (q + 1))
        for n in range(NT):
            nc.vector.bn_aggr(mv[:, n, :], stats[:, n, :]).then_inc(m["aggr"], 1)
        dve.wait_ge(m["aggr"], NT * (q + 1))
        nc.vector.tensor_scalar(ve[:, :], mv[:, :, 1], EPS, None, ALU.add).then_inc(m["ve_done"], 1)

    def read_ctxT(dve, q, a):
        dve.wait_ge(m["transposed"], 3 * q + a + 1 + CREDIT["transposed"])
        nc.vector.tensor_copy(ctxT[:, JB * a:JB * a + JB], ps[:, 4 + a, 0:JB]).then_inc(m["ctxT_done"], 1)

    def low_keys(dve, q, a, first):
        if a == 0 and not first:
            dve.wait_ge(m["copied"], CPY * q + CREDIT["copied"])
        dve.wait_ge(m["k_hi_done"], 3 * q + a + 1)
        nc.vector.scalar_tensor_tensor(out=k_lo[:, JB * a:JB * a + JB], in0=ps[:, 4 + a, 0:JB],
                                       scalar=k_bias, in1=k_hi[:, JB * a:JB * a + JB].bitcast(F32),
                                       op0=ALU.add, op1=ALU.subtract).then_inc(m["k_lo_done"], 1)

    def maximum(dve, q, i, first):
        dve.wait_ge(m["max_scored"], 3 * SM * q + i + 1 + CREDIT["max_scored"])
        if i == 0 and not first:
            dve.wait_ge(m["negmax_done"], q)
        nc.vector.tensor_reduce(part_max[:, i // 3, i % 3:i % 3 + 1], ps[:, 4 + i % 3, 0:JB], AX.X, ALU.max
                                ).then_inc(m["max_done"], 1)

    def join_maxima(dve, q, first):
        dve.wait_ge(m["max_done"], 3 * SM * (q + 1))
        if not first:
            dve.wait_ge(m["max_turned"], q)
        nc.vector.tensor_reduce(negmax[:, :], part_max[:, :, :], AX.X, ALU.max, negate=True
                                ).then_inc(m["negmax_done"], 1)

    def maxima_rows(dve, q, u):
        dve.wait_ge(m["max_turned"], q + 1)
        nc.vector.tensor_tensor(q_op[u][96:KROWS, :, :, :].rearrange("p g h t -> p (g h t)").rearrange(
                                    "p (a n) -> p a n", n=128),
                                ps[0:SM, 7, 0:128].unsqueeze(1).to_broadcast([SM, SM, 128]),
                                s["ident"][0:SM, 0:SM].unsqueeze(2).to_broadcast([SM, SM, 128]),
                                ALU.mult).then_inc(m["max_rows"], 1)

    def read_sums(dve, b):
        dve.wait_ge(m["summed"], NT * (b + 1) + CREDIT["summed"])
        nc.vector.tensor_copy(s["oT_all"][:, :, bass.ds(b * T, T)],
                              ps[:, 7, 0:GT].rearrange("p (k t) -> p k t", t=T)).then_inc(m["sums_read"], 1)

    def exponential(act, b, u, n):
        act.wait_ge(m["scored"], NT * b + n + 1 + CREDIT["scored"])
        act.wait_ge(m["summed"], NT * b + n - 1 + CREDIT["summed"])
        k = n % 2
        nc.scalar.activation(probs[k][:, :].rearrange("p (a n) -> p a n", a=2),
                             ps[0:JP, 2 * k:2 * k + 2, 0:2 * GT], ACT.Exp).then_inc(m["exped"], 1)

    def high_keys(act, q, a, first):
        act.wait_ge(m["k_projected"], 3 * q + a + 1)
        if a == 0 and not first:
            act.wait_ge(m["copied"], CPY * q + CREDIT["copied"])
        nc.scalar.activation(k_hi[:, JB * a:JB * a + JB], ps[:, 4 + a, 0:JB], ACT.Identity, bias=k_bias
                             ).then_inc(m["k_hi_done"], 1)

    def ones_of_keys(act, u):
        nc.scalar.activation(k_op[u][96:KROWS, :, :], s["minus_half"][96:KROWS, 0:1].unsqueeze(2).to_broadcast(
                                 [SM, G, J]), ACT.Copy, scale=-2.0).then_inc(m["key_ones"], 1)

    def read_values(act, q, u, a, bank):
        act.wait_ge(m["v_projected"], 3 * q + a + 1)
        nc.scalar.activation(v_op[u][:, 4 * a:4 * a + 4, 0:H * VH].rearrange(
                                 "p n (h e) -> p n h e", e=VH)[:, :, :, 0:D],
                             ps[0:JP, bank, :].rearrange("p (b h d) -> p b h d", b=4, d=D), ACT.Copy
                             ).then_inc(m["v_read"], 1)

    def transpose_ctx(pe, q, u, first):
        pe.wait_ge(*source_ready(q, u))
        for a in range(3):
            if not first:
                pe.wait_ge(m["v_read"], 3 * (q - 1) + a + 1 + CREDIT["v_read"])
            for n in range(4 * a, 4 * a + 4):
                mm = nc.tensor.transpose(ps[:, 4 + a, JP * (n % 4):JP * (n % 4) + JP], xhat[u][:, n, :],
                                         s["ident"][0:JP, 0:JP])
            mm.then_inc(m["transposed"], 1)

    def project_keys(pe, q, a):
        pe.wait_ge(m["ctxT_done"], 3 * q + a + 1)
        nc.tensor.matmul(ps[:, 4 + a, 0:JB], wk[:, :], ctxT[:, JB * a:JB * a + JB],
                         start=True, stop=True).then_inc(m["k_projected"], 1)

    def score_for_max(pe, q, u, i):
        t, a = i // 3, i % 3
        if t == 0:
            pe.wait_ge(m["k_lo_done"], 3 * q + a + 1)
            if a == 0:
                pe.wait_ge(m["q_blk_done"], q + 1)
        else:
            pe.wait_ge(m["max_done"], 3 * SM * q + i - 2)
        rows = q_blk[u][:, :, :].rearrange("p h t -> p (h t)")[:, 128 * t:128 * t + 128]
        nc.tensor.matmul(ps[:, 4 + a, 0:JB], rows, k_hi[:, JB * a:JB * a + JB], start=True, stop=True
                         ).then_inc(m["max_scored"], 1)

    def turn_maxima(pe, q, b):
        pe.wait_ge(m["negmax_done"], q + 1)
        if b is not None:
            pe.wait_ge(m["sums_read"], b + 1 + CREDIT["sums_read"])
        nc.tensor.transpose(ps[0:SM, 7, 0:128], negmax[:, :], s["ident"][:, :]).then_inc(m["max_turned"], 1)

    def project_values(pe, q, a, bank):
        for n in range(4 * a, 4 * a + 4):
            mm = nc.tensor.matmul(ps[0:JP, bank, C * (n % 4):C * (n % 4) + C],
                                  ctxT[:, JP * n:JP * n + JP], wv[:, :], start=True, stop=True)
        mm.then_inc(m["v_projected"], 1)

    def score(pe, b, u, n):
        if n == 0:
            pe.wait_ge(m["copied"], CPY * (b + 1) + CREDIT["copied"])
            pe.wait_ge(m["q_op_done"], G * (b + 1))
            pe.wait_ge(m["max_rows"], b + 1)
        pe.wait_ge(m["exped"], NT * b + n - 1 + CREDIT["exped"])
        for g in range(G):
            mm = nc.tensor.matmul(ps[0:JP, 2 * (n % 2) + g // 2, GT * (g % 2):GT * (g % 2) + GT],
                                  k_op[u][:, g, JP * n:JP * n + JP],
                                  q_op[u][:, g, :, :].rearrange("p h t -> p (h t)"), start=True, stop=True)
        mm.then_inc(m["scored"], 1)

    def weighted_sum(pe, b, u, n):
        if n == 0:
            pe.wait_ge(m["v_read"], 3 * (b + 1) + CREDIT["v_read"])
            pe.wait_ge(m["sums_read"], b + CREDIT["sums_read"])
            pe.wait_ge(m["max_rows"], b + 1)
        pe.wait_ge(m["exped"], NT * b + n + 1 + CREDIT["exped"])
        for c0, c1, v0 in ((0, 3 * T, 0), (3 * T, 4 * T, 3 * VH)):
            for g in range(G):
                mm = nc.tensor.matmul(ps[32 * g:32 * g + 32, 7, c0:c1],
                                      v_op[u][:, n, GH * VH * g + v0:GH * VH * g + v0 + 32],
                                      probs[n % 2][:, GT * g + c0:GT * g + c1],
                                      start=(n == 0 and c0 == 0), stop=(n == NT - 1), skip_group_check=True)
        mm.then_inc(m["summed"], 1)

    T_SLOT, S_SLOT = 0, 3
    K_SLOTS = [[], [0, 1], [2]]
    HIGH_SLOTS = [[], [0, 1], [2]]
    EARLY_TILES, LATE_TILES = range(0, 6), range(6, NT)
    S_COUNT = [3, 2, 3, 2, 3, 2, 2, 2, 2]
    assert sum(S_COUNT) == 3 * SM and S_SLOT + len(S_COUNT) == NT

    def tensor_step(pe, b, u, prepare):
        i = 0
        for n in range(NT):
            score(pe, b, u, n)
            if prepare and n == T_SLOT:
                transpose_ctx(pe, b + 1, 1 - u, False)
            if prepare and n < len(K_SLOTS):
                for a in K_SLOTS[n]:
                    project_keys(pe, b + 1, a)
            if prepare and n >= S_SLOT:
                for _ in range(S_COUNT[n - S_SLOT]):
                    score_for_max(pe, b + 1, 1 - u, i)
                    i += 1
            if n >= 1:
                weighted_sum(pe, b, u, n - 1)
        weighted_sum(pe, b, u, NT - 1)
        if prepare:
            for a in range(3):
                pe.wait_ge(m["max_done"], 3 * SM * (b + 2) - 2 + a)
                project_values(pe, b + 1, a, 4 + a)
                if a == 0:
                    turn_maxima(pe, b + 1, b)

    def scalar_step(act, b, u, prepare):
        for n in range(NT):
            exponential(act, b, u, n)
            if prepare and n < len(HIGH_SLOTS):
                for a in HIGH_SLOTS[n]:
                    high_keys(act, b + 1, a, False)
        if prepare:
            for a in range(3):
                read_values(act, b + 1, 1 - u, a, 4 + a)

    def vector_step(dve, b, u, prepare, ahead, more):
        ahead = ahead and layer == 0
        if prepare:
            for a in range(3):
                read_ctxT(dve, b + 1, a)
        if ahead:
            row_statistics(dve, b + 2, u, LATE_TILES)
        if prepare:
            for a in range(2):
                low_keys(dve, b + 1, a, False)
        if ahead:
            variances(dve, b + 2, False)
        if prepare:
            low_keys(dve, b + 1, 2, False)
            for i in range(3 * SM):
                maximum(dve, b + 1, i, False)
            join_maxima(dve, b + 1, False)
        read_sums(dve, b)
        if prepare:
            maxima_rows(dve, b + 1, 1 - u)
        if layer == 0 and more:
            row_statistics(dve, b + 3, 1 - u, EARLY_TILES)

    def gpsimd_step(pool, b, u, prepare, ahead):
        if prepare:
            block_queries(pool, b + 1, 1 - u, False)
            expand_queries(pool, b + 1, 1 - u, False)
        if layer == 0 and ahead:
            normalise(pool, b + 2, u, False)

    def sync_step(sp, b, u, prepare, load_next):
        if load_next:
            load_ahead(sp, b, u)
        if prepare:
            copy_keys(sp, b + 1, 1 - u, False)

    LOOPED = B - 4
    TAIL = range(LOOPED, B)

    with nc.Block() as block:
        @block.gpsimd
        def _(pool):
            for name, credit in CREDIT.items():
                if credit:
                    pool.sem_inc(m[name], credit)

    with nc.Block() as block:
        @block.sync
        def _(sp):
            load(sp, 0, 0)
            load(sp, 1, 1)
            copy_queries(sp)
            if layer == 0:
                sp.wait_ge(m["normed"], 1 + CREDIT["normed"])
                load(sp, 2, 0)
            copy_keys(sp, 0, 0, True)
            with sp.Fori(0, LOOPED, 2) as b:
                for u in range(2):
                    sync_step(sp, b + u, u, True, True)
            for b in TAIL:
                sync_step(sp, b, b % 2, b + 1 < B, b + AHEAD < B)

        @block.gpsimd
        def _(pool):
            ones_of_values(pool, 0)
            block_queries(pool, 0, 0, True)
            if layer == 0:
                reciprocal_deviation(pool, 0)
            expand_queries(pool, 0, 0, True)
            ones_of_values(pool, 1)
            if layer == 0:
                normalise(pool, 1, 1, True)
            with pool.Fori(0, LOOPED, 2) as b:
                for u in range(2):
                    gpsimd_step(pool, b + u, u, True, True)
            for b in TAIL:
                gpsimd_step(pool, b, b % 2, b + 1 < B, b + 2 < B)

        @block.vector
        def _(dve):
            if layer == 0:
                row_statistics(dve, 0, 0, range(NT))
                variances(dve, 0, True)
                row_statistics(dve, 1, 1, range(NT))
                normalise_first(dve)
                variances(dve, 1, False)
            for a in range(3):
                read_ctxT(dve, 0, a)
            for a in range(3):
                low_keys(dve, 0, a, True)
            for i in range(3 * SM):
                maximum(dve, 0, i, True)
            join_maxima(dve, 0, True)
            maxima_rows(dve, 0, 0)
            if layer == 0:
                row_statistics(dve, 2, 0, EARLY_TILES)
            dve.wait_ge(m["q_copied"], Q_COPIED)
            with dve.Fori(0, LOOPED, 2) as b:
                for u in range(2):
                    vector_step(dve, b + u, u, True, True, True)
            for b in TAIL:
                vector_step(dve, b, b % 2, b + 1 < B, b + 2 < B, b + 3 < B)

        @block.scalar
        def _(act):
            ones_of_keys(act, 0)
            for a in range(3):
                high_keys(act, 0, a, True)
            ones_of_keys(act, 1)
            act.wait_ge(m["value_ones"], 1)
            for a in range(3):
                read_values(act, 0, 0, a, a)
            act.wait_ge(m["value_ones"], 2)
            with act.Fori(0, LOOPED, 2) as b:
                for u in range(2):
                    scalar_step(act, b + u, u, True)
            for b in TAIL:
                scalar_step(act, b, b % 2, b + 1 < B)

        @block.tensor
        def _(pe):
            transpose_ctx(pe, 0, 0, True)
            for a in range(3):
                project_keys(pe, 0, a)
            for i in range(3 * SM):
                score_for_max(pe, 0, 0, i)
                if i % 3 == 2 and i // 3 < 3:
                    project_values(pe, 0, i // 3, i // 3)
            turn_maxima(pe, 0, None)
            pe.wait_ge(m["v_read"], 3 + CREDIT["v_read"])
            pe.wait_ge(m["key_ones"], 2)
            with pe.Fori(0, LOOPED, 2) as b:
                for u in range(2):
                    tensor_step(pe, b + u, u, True)
            for b in TAIL:
                tensor_step(pe, b, b % 2, b + 1 < B)


def after_cross(nc, s, own, ps, layer, out):
    def sb(name, shape, dt=F32):
        return own.enter_context(nc.sbuf_tensor(f"p{layer}_{name}", shape, dt))

    def two(name, shape):
        return [sb(f"{name}{u}", shape) for u in range(2)]

    oT = two("oT", [128, GH, UT])
    rden = two("rden", [PT, UP, G, GH])
    ao = two("ao", [PT, UP, G, GH, D])
    aoT = two("aoT", [C, UT])
    y = two("y", [PT, UP, C])
    yT = two("yT", [C, UT])
    q32 = two("q32", [C, UT])
    stats = two("stats", [PT, UP, 6])
    mv = two("mv", [PT, UP, 2])
    ve = two("ve", [PT, UP])
    rstd = two("rstd", [PT, UP])
    yhat = two("yhat", [PT, UP, C])
    yg = two("yg", [PT, UP, C])
    yb = two("yb", [PT, UP, C])
    names = ["staged", "turned", "rden_done", "ao_done", "ao_tr", "aoT_done", "proj", "y_done", "y_kept",
             "y_tr", "yT_done", "qp", "q_store", "q_hi", "q_low", "st", "ag", "ve_done", "rs",
             "xh", "gained", "offset", "stored0", "stored1", "gates"]
    CREDIT = {"ao_done": 2 * UP, "ao_tr": 1, "proj": 1, "y_tr": 2, "y_kept": 2, "y_done": 1, "q_store": 1,
              "qp": 2, "q_low": 2, "xh": 2 * UP, "gained": 2, "offset": 2, "stored0": 16, "stored1": 16}
    m = own.enter_context(semaphores(nc, f"p{layer}_", names))
    wo = s[f"wo{layer}"]
    v_bias = s["kv_bias"][:, 1:2] if layer == 0 else s["cols"][:, BV:BV + 1]
    wq, q_scale, q_bias = queries(1, s)
    out_pairs = out.rearrange("b t d -> (b t) d").rearrange("(n p) d -> p n d", p=PT)

    def value(name, k):
        return m[name], k + CREDIT.get(name, 0)

    def stage(act, i, u):
        act.wait_ge(*value("turned", UP * (i - 1)))
        nc.scalar.activation(oT[u][:, :, :], s["oT_all"][:, :, bass.ds(i * UT, UT)], ACT.Copy
                             ).then_inc(m["staged"], 1)

    def read_aoT(act, i, u, first):
        act.wait_ge(*value("ao_tr", i + 1))
        if not first:
            act.wait_ge(*value("proj", i - 1))
        nc.scalar.activation(aoT[u][:, :], ps[:, 4 + u, 0:UT], ACT.Identity, bias=v_bias
                             ).then_inc(m["aoT_done"], 1)

    def read_yT(act, i, u):
        act.wait_ge(*value("y_tr", i + 1))
        act.wait_ge(*value("qp", i - 1))
        nc.scalar.activation(yT[u][:, :], ps[:, 7, 0:UT], ACT.Copy).then_inc(m["yT_done"], 1)

    def high_queries(act, i, u):
        act.wait_ge(*value("qp", i + 1))
        act.wait_ge(*value("q_low", i - 1))
        nc.scalar.activation(q32[u][:, :], ps[:, 7, 0:UT], ACT.Identity, bias=q_bias, scale=q_scale
                             ).then_inc(m["q_store"], 1)
        act.wait_ge(*value("q_store", i + 1))
        nc.scalar.activation(s["q_hi"][:, bass.ds(i * UT, UT)], q32[u][:, :], ACT.Copy
                             ).then_inc(m["q_hi"], 1)

    def turn_sums(pe, i, u, first):
        pe.wait_ge(*value("staged", i + 1))
        for p in range(UP):
            if not first:
                pe.wait_ge(*value("ao_done", 2 * UP * (i - 2) + 2 * p + 2))
            for k in range(GH):
                mm = nc.tensor.transpose(ps[0:PT, 2 * u + p, 128 * k:128 * k + 128],
                                         oT[u][:, k, PT * p:PT * p + PT], s["ident"][:, :])
            mm.then_inc(m["turned"], 1)

    def transpose_ao(pe, i, u):
        pe.wait_ge(*value("ao_done", 2 * UP * (i + 1)))
        for p in range(UP):
            mm = nc.tensor.transpose(ps[:, 4 + u, PT * p:PT * p + PT],
                                     ao[u][:, p, :, :, :].rearrange("p g k d -> p (g k d)"),
                                     s["ident"][0:PT, 0:PT])
        mm.then_inc(m["ao_tr"], 1)

    def project_out(pe, i, u):
        pe.wait_ge(*value("aoT_done", i + 1))
        pe.wait_ge(*value("y_done", i))
        for p in range(UP):
            mm = nc.tensor.matmul(ps[0:PT, 6, C * p:C * p + C], aoT[u][:, PT * p:PT * p + PT], wo[:, :],
                                  start=True, stop=True)
        mm.then_inc(m["proj"], 1)

    def transpose_y(pe, i, u):
        pe.wait_ge(*value("y_done", i + 1))
        pe.wait_ge(*value("q_store", i))
        for p in range(UP):
            mm = nc.tensor.transpose(ps[:, 7, PT * p:PT * p + PT], y[u][:, p, :], s["ident"][0:PT, 0:PT])
        mm.then_inc(m["y_tr"], 1)

    def project_queries(pe, i, u):
        pe.wait_ge(*value("yT_done", i + 1))
        nc.tensor.matmul(ps[:, 7, 0:UT], wq[:, :], yT[u][:, :], start=True, stop=True).then_inc(m["qp"], 1)

    def normalise_sums(dve, i, u, first):
        if not first:
            dve.wait_ge(*value("ao_tr", i - 1))
        for p in range(UP):
            dve.wait_ge(*value("turned", UP * i + p + 1))
            low = ps[0:PT, 2 * u + p, 0:3 * (128 + VH)].rearrange("p (k f) -> p k f", k=3)[:, :, 0:128].rearrange(
                "p k (g r) -> p k g r", g=G)
            top = ps[0:PT, 2 * u + p, 3 * 128:4 * 128].rearrange("p (g r) -> p g r", g=G)
            nc.vector.reciprocal(rden[u][:, p, :, 0:3].rearrange("p g k -> p k g"), low[:, :, :, D]
                                 ).then_inc(m["rden_done"], 1)
            nc.vector.reciprocal(rden[u][:, p, :, 3], top[:, :, D]).then_inc(m["rden_done"], 1)
            dve.wait_ge(*value("rden_done", 2 * UP * i + 2 * p + 2))
            nc.vector.tensor_tensor(ao[u][:, p, :, 0:3, :].rearrange("p g k d -> p k g d"),
                                    low[:, :, :, 0:D],
                                    rden[u][:, p, :, 0:3].rearrange("p g k -> p k g").unsqueeze(3).to_broadcast(
                                        [PT, 3, G, D]), ALU.mult).then_inc(m["ao_done"], 1)
            nc.vector.tensor_tensor(ao[u][:, p, :, 3, :], top[:, :, 0:D],
                                    rden[u][:, p, :, 3].unsqueeze(2).to_broadcast([PT, G, D]), ALU.mult
                                    ).then_inc(m["ao_done"], 1)

    def add_residual(dve, i, u):
        dve.wait_ge(*value("proj", i + 1))
        if layer == 0:
            dve.wait_ge(*value("y_tr", i - 1))
            dve.wait_ge(*value("y_kept", i - 1))
        else:
            dve.wait_ge(*value("xh", UP * (i - 1)))
        nc.vector.tensor_tensor(y[u][:, :, :], ps[0:PT, 6, 0:UP * C].rearrange("p (a n) -> p a n", n=C),
                                s["resid"][:, bass.ds(i * UP, UP), :], ALU.add).then_inc(m["y_done"], 1)

    def low_queries(dve, i, u):
        dve.wait_ge(*value("q_hi", i + 1))
        nc.vector.tensor_tensor(s["q_lo"][:, bass.ds(i * UT, UT)], q32[u][:, :],
                                s["q_hi"][:, bass.ds(i * UT, UT)].bitcast(F32), ALU.subtract
                                ).then_inc(m["q_low"], 1)

    def variances(dve, i, u):
        dve.wait_ge(*value("y_done", i + 1))
        for p in range(UP):
            nc.vector.bn_stats(stats[u][:, p, :], y[u][:, p, :]).then_inc(m["st"], 1)
        wait_alone(dve, m["gates"], *value("st", UP * (i + 1)))
        for p in range(UP):
            nc.vector.bn_aggr(mv[u][:, p, :], stats[u][:, p, :]).then_inc(m["ag"], 1)
        dve.wait_ge(*value("ag", UP * (i + 1)))
        nc.vector.tensor_scalar(ve[u][:, :], mv[u][:, :, 1], EPS, None, ALU.add).then_inc(m["ve_done"], 1)

    def normalise(dve, i, u):
        dve.wait_ge(*value("rs", i + 1))
        dve.wait_ge(*value("gained", i - 1))
        for p in range(UP):
            nc.vector.tensor_scalar(yhat[u][:, p, :], y[u][:, p, :], mv[u][:, p, 0:1], rstd[u][:, p:p + 1],
                                    ALU.subtract, ALU.mult).then_inc(m["xh"], 1)

    def keep_residual(pool, i, u):
        pool.wait_ge(*value("y_done", i + 1))
        nc.gpsimd.tensor_tensor(s["resid"][:, bass.ds(i * UP, UP), :], y[u][:, :, :],
                                s["rows"][:, BO, :].unsqueeze(1).to_broadcast([PT, UP, C]), ALU.add
                                ).then_inc(m["y_kept"], 1)

    def reciprocal_deviation(pool, i, u):
        pool.wait_ge(*value("ve_done", i + 1))
        nc.gpsimd.tensor_tensor(rstd[u][:, :], ve[u][:, :], s["minus_half"][0:PT, 0:UP], ALU.pow
                                ).then_inc(m["rs"], 1)

    def gain_and_offset(pool, i, u):
        pool.wait_ge(*value("xh", UP * (i + 1)))
        pool.wait_ge(*value("offset", i - 1))
        nc.gpsimd.tensor_tensor(yg[u][:, :, :], yhat[u][:, :, :],
                                s["rows"][:, LN_G, :].unsqueeze(1).to_broadcast([PT, UP, C]), ALU.mult
                                ).then_inc(m["gained"], 1)
        pool.wait_ge(*value("gained", i + 1))
        pool.wait_ge(*value(f"stored{u}", 8 * (i - u)))
        nc.gpsimd.tensor_tensor(yb[u][:, :, :], yg[u][:, :, :],
                                s["rows"][:, LN_B, :].unsqueeze(1).to_broadcast([PT, UP, C]), ALU.add
                                ).then_inc(m["offset"], 1)

    def tensor_step(pe, i, u, left):
        project_out(pe, i, u)
        if left >= 1:
            transpose_ao(pe, i + 1, 1 - u)
        if layer == 0:
            transpose_y(pe, i, u)
        if left >= 2:
            turn_sums(pe, i + 2, u, False)
        if layer == 0:
            project_queries(pe, i, u)

    def scalar_step(act, i, u, left):
        if left >= 1:
            read_aoT(act, i + 1, 1 - u, False)
        if left >= 3:
            stage(act, i + 3, 1 - u)
        if layer == 0:
            read_yT(act, i, u)
            high_queries(act, i, u)

    def vector_step(dve, i, u, left):
        add_residual(dve, i, u)
        if layer == 1:
            variances(dve, i, u)
        if left >= 2:
            normalise_sums(dve, i + 2, u, False)
        if layer == 0:
            low_queries(dve, i, u)
        else:
            normalise(dve, i, u)

    def gpsimd_step(pool, i, u):
        if layer == 0:
            keep_residual(pool, i, u)
        else:
            reciprocal_deviation(pool, i, u)
            gain_and_offset(pool, i, u)

    def store(sp, i, u):
        wait_alone(sp, m["gates"], *value("offset", i + 1))
        sp.dma_start(out_pairs[:, bass.ds(i * UP, UP), :], yb[u][:, :, :]).then_inc(m[f"stored{u}"], 16)

    LOOPED = NU - 4
    TAIL = range(LOOPED, NU)

    with nc.Block() as block:
        @block.gpsimd
        def _(pool):
            for name, credit in CREDIT.items():
                pool.sem_inc(m[name], credit)

    with nc.Block() as block:
        @block.scalar
        def _(act):
            for i in range(2):
                nc.scalar.activation(oT[i][:, :, :], s["oT_all"][:, :, i * UT:i * UT + UT], ACT.Copy
                                     ).then_inc(m["staged"], 1)
            stage(act, 2, 0)
            read_aoT(act, 0, 0, True)
            with act.Fori(0, LOOPED, 2) as i:
                for u in range(2):
                    scalar_step(act, i + u, u, 3)
            for i in TAIL:
                scalar_step(act, i, i % 2, NU - 1 - i)

        @block.tensor
        def _(pe):
            turn_sums(pe, 0, 0, True)
            turn_sums(pe, 1, 1, True)
            transpose_ao(pe, 0, 0)
            with pe.Fori(0, LOOPED, 2) as i:
                for u in range(2):
                    tensor_step(pe, i + u, u, 3)
            for i in TAIL:
                tensor_step(pe, i, i % 2, NU - 1 - i)

        @block.vector
        def _(dve):
            normalise_sums(dve, 0, 0, True)
            normalise_sums(dve, 1, 1, True)
            with dve.Fori(0, LOOPED, 2) as i:
                for u in range(2):
                    vector_step(dve, i + u, u, 3)
            for i in TAIL:
                vector_step(dve, i, i % 2, NU - 1 - i)

        @block.gpsimd
        def _(pool):
            with pool.Fori(0, LOOPED, 2) as i:
                for u in range(2):
                    gpsimd_step(pool, i + u, u)
            for i in TAIL:
                gpsimd_step(pool, i, i % 2)

        if layer == 1:
            @block.sync
            def _(sp):
                with sp.Fori(0, LOOPED, 2) as i:
                    for u in range(2):
                        store(sp, i + u, u)
                for i in TAIL:
                    store(sp, i, i % 2)
                for u in range(2):
                    sp.wait_ge(*value(f"stored{u}", 8 * NU))


def kernel(**inputs):
    import numpy as _np
    import concourse.bacc as _bacc
    from concourse import mybir as _mybir
    from concourse.bass_utils import run_bass_kernel_spmd as _run

    nc = _bacc.Bacc("TRN2", target_bir_lowering=False, num_devices=1)
    arrays, args = {}, {}
    for name, value in inputs.items():
        a = _np.ascontiguousarray(value)
        arrays[f"in_{name}_dram"] = a
        args[name] = nc.dram_tensor(f"in_{name}_dram", a.shape, _mybir.dt.from_np(a.dtype),
                                    kind="ExternalInput").ap()
    y = nc.dram_tensor("out_0_dram", (B, T, C), F32, kind="ExternalOutput").ap()
    build(nc, args.pop("x"), args.pop("ctx_1024"), args.pop("mask_BxS_bf0"), args, y)
    r = _run(nc, [arrays], core_ids=[0])
    return r.results[0]["out_0_dram"]
```
